# Optimizing a Trainium2 kernel written in Bass

```python
import numpy as np
import jax
import jax.numpy as jnp

def _softmax(x, axis=-1):
    return jax.nn.softmax(x, axis=axis)
def _gelu(x):
    return jax.nn.gelu(x, approximate=True)
def _silu(x):
    return jax.nn.silu(x)
def _sigmoid(x):
    return jax.nn.sigmoid(x)
def _layernorm(x, axis=-1, eps=1e-5):
    m = jnp.mean(x, axis=axis, keepdims=True)
    v = jnp.var(x, axis=axis, keepdims=True)
    return (x - m) / jnp.sqrt(v + eps)
def _scatter_add(tgt, idx, src, axis=0):
    return tgt.at[idx].add(src)
def _segment_sum(src, seg, n):
    return jax.ops.segment_sum(src, seg, n)

kernel_name = 'mk_conv_preact_d4_conv_nchw384_d9e6d1'

def setup_inputs(seed: int = 0):
    np.random.seed(seed)
    _w = jnp.asarray
    def _rec_inputs():
        import jax
        import jax.numpy as jnp
        _gk = jax.random.key(seed)
        x = -0.0005963 + 1.001 * jax.random.normal(jax.random.fold_in(_gk, 1), (8, 384, 32, 32), jnp.float32)
        return x
    x = _rec_inputs()
    def _L0_conv_setup():
        import jax, jax.numpy as jnp
        import numpy as np
        DIM = 384
        HEADS = 8
        key = jax.random.key(seed)
        k_x, k_qkv, k_pw, k_pb = jax.random.split(key, 4)
        x = jax.random.normal(k_x, (8, DIM, 32, 32), dtype=jnp.float32)
        w_qkv = jax.random.normal(k_qkv, (3 * DIM, DIM), dtype=jnp.float32) * DIM ** (-0.5)
        w_proj = jax.random.normal(k_pw, (DIM, DIM), dtype=jnp.float32) * DIM ** (-0.5)
        b_proj = jax.random.normal(k_pb, (DIM,), dtype=jnp.float32) * 0.02
        return {'x': x, 'w_qkv': w_qkv, 'w_proj': w_proj, 'b_proj': b_proj}
    _L0_conv_all = _L0_conv_setup()
    _L0_conv_in = {k: v for k, v in _L0_conv_all.items() if k in ('w_qkv', 'w_proj', 'b_proj', )}
    del _L0_conv_all

    def _L1_conv_setup():
        import jax, jax.numpy as jnp
        import numpy as np
        BANDLIMIT = 0.5
        STEP_SCALE = 1.0
        LN_EPS = 1e-05

        def _layernorm(x, g, b):
            mu = jnp.mean(x, axis=-1, keepdims=True)
            xc = x - mu
            inv = jax.lax.rsqrt(jnp.mean(xc * xc, axis=-1, keepdims=True) + LN_EPS)
            return xc * inv * g + b
        key = jax.random.key(seed)
        ks = jax.random.split(key, 12)
        B, C, H, W = (16, 384, 64, 64)
        P = 192
        x = jax.random.normal(ks[0], (B, C, H, W), dtype=jnp.float32)
        ln1_g = 1.0 + 0.1 * jax.random.normal(ks[1], (C,), dtype=jnp.float32)
        ln1_b = 0.1 * jax.random.normal(ks[2], (C,), dtype=jnp.float32)
        lam_re = -(0.3 + jax.random.uniform(ks[3], (P,), dtype=jnp.float32))
        lam_im = jnp.pi * jnp.arange(P, dtype=jnp.float32)
        Lambda = jnp.stack([lam_re, lam_im], axis=-1)
        Bmat = jax.random.normal(ks[4], (P, C, 2), dtype=jnp.float32) / np.sqrt(C)
        Cmat = jax.random.normal(ks[5], (C, P, 2), dtype=jnp.float32) / np.sqrt(P)
        D = jax.random.normal(ks[6], (C,), dtype=jnp.float32)
        log_step = jax.random.uniform(ks[7], (P,), dtype=jnp.float32, minval=float(np.log(0.001)), maxval=float(np.log(0.1)))
        ln2_g = 1.0 + 0.1 * jax.random.normal(ks[8], (C,), dtype=jnp.float32)
        ln2_b = 0.1 * jax.random.normal(ks[9], (C,), dtype=jnp.float32)
        W_enc = jax.random.normal(ks[10], (2 * C, C), dtype=jnp.float32) / np.sqrt(C)
        W_dec = jax.random.normal(ks[11], (C, C), dtype=jnp.float32) / np.sqrt(C)
        return {'x': x, 'ln1_g': ln1_g, 'ln1_b': ln1_b, 'Lambda': Lambda, 'Bmat': Bmat, 'Cmat': Cmat, 'D': D, 'log_step': log_step, 'ln2_g': ln2_g, 'ln2_b': ln2_b, 'W_enc': W_enc, 'W_dec': W_dec}
    _L1_conv_all = _L1_conv_setup()
    _L1_conv_in = {k: v for k, v in _L1_conv_all.items() if k in ('ln1_g', 'ln1_b', 'Lambda', 'Bmat', 'Cmat', 'D', 'log_step', 'ln2_g', 'ln2_b', 'W_enc', 'W_dec', )}
    del _L1_conv_all

    def _L2_conv_setup():
        import jax, jax.numpy as jnp
        import numpy as np
        C = 384

        def dwconv(x, w, pad_h, pad_w, stride=(1, 1)):
            return jax.lax.conv_general_dilated(x, w, window_strides=stride, padding=((pad_h, pad_h), (pad_w, pad_w)), dimension_numbers=('NCHW', 'OIHW', 'NCHW'), feature_group_count=C)
        key = jax.random.key(seed)
        ks = jax.random.split(key, 12)
        f = lambda k, shape: jax.random.normal(k, shape, dtype=jnp.float32) * 0.05
        return {'x': jax.random.normal(ks[0], (32, C, 56, 56), dtype=jnp.float32), 'w77': f(ks[1], (C, 1, 7, 7)), 'b77': f(ks[2], (C,)), 'w53': f(ks[3], (C, 1, 5, 3)), 'b53': f(ks[4], (C,)), 'w35': f(ks[5], (C, 1, 3, 5)), 'b35': f(ks[6], (C,)), 'w7w': f(ks[7], (C, 1, 1, 7)), 'w7h': f(ks[8], (C, 1, 7, 1)), 'w5w': f(ks[9], (C, 1, 1, 5)), 'w5h': f(ks[10], (C, 1, 5, 1))}
    _L2_conv_all = _L2_conv_setup()
    _L2_conv_in = {k: v for k, v in _L2_conv_all.items() if k in ('w77', 'b77', 'w53', 'b53', 'w35', 'b35', 'w7w', 'w7h', 'w5w', 'w5h', )}
    del _L2_conv_all

    def _L3_conv_setup():
        import jax, jax.numpy as jnp
        import numpy as np
        NEG = -1e+38

        def wkv_scan(w, u, k, v):
            B, T, C = k.shape
            kT = jnp.swapaxes(k, 0, 1)
            vT = jnp.swapaxes(v, 0, 1)
            aa = jnp.zeros((B, C), k.dtype)
            bb = jnp.zeros((B, C), k.dtype)
            pp = jnp.full((B, C), NEG, k.dtype)

            def step(carry, kv):
                aa, bb, pp = carry
                kt, vt = kv
                ww = u + kt
                p = jnp.maximum(pp, ww)
                e1 = jnp.exp(pp - p)
                e2 = jnp.exp(ww - p)
                y = (e1 * aa + e2 * vt) / (e1 * bb + e2)
                ww2 = pp + w
                p2 = jnp.maximum(ww2, kt)
                f1 = jnp.exp(ww2 - p2)
                f2 = jnp.exp(kt - p2)
                return ((f1 * aa + f2 * vt, f1 * bb + f2, p2), y)
            _, y = jax.lax.scan(step, (aa, bb, pp), (kT, vT))
            return jnp.swapaxes(y, 0, 1)
        key = jax.random.key(seed)
        ks = jax.random.split(key, 12)
        B, C, H, W = (16, 384, 48, 48)
        s = 1.0 / np.sqrt(C)
        return {'x': jax.random.normal(ks[0], (B, C, H, W), jnp.float32), 'Wk': jax.random.normal(ks[1], (C, C), jnp.float32) * s, 'Wv': jax.random.normal(ks[2], (C, C), jnp.float32) * s, 'Wr': jax.random.normal(ks[3], (C, C), jnp.float32) * s, 'Wo': jax.random.normal(ks[4], (C, C), jnp.float32) * s, 'ln_g': jnp.ones((C,), jnp.float32), 'ln_b': jnp.zeros((C,), jnp.float32), 'w_param': -6.0 + 0.5 * jax.random.normal(ks[5], (C,), jnp.float32), 'u': 0.1 * jax.random.normal(ks[6], (C,), jnp.float32), 'conv_w': jax.random.normal(ks[7], (C, C, 3, 3), jnp.float32) * (1.0 / np.sqrt(C * 9)), 'bn_g': jnp.ones((C,), jnp.float32), 'bn_b': jnp.zeros((C,), jnp.float32), 'gamma_g': 0.5 * jnp.ones((1, C, 1, 1), jnp.float32), 'gamma_s': 0.5 * jnp.ones((1, C, 1, 1), jnp.float32)}
    _L3_conv_all = _L3_conv_setup()
    _L3_conv_in = {k: v for k, v in _L3_conv_all.items() if k in ('Wk', 'Wv', 'Wr', 'Wo', 'ln_g', 'ln_b', 'w_param', 'u', 'conv_w', 'bn_g', 'bn_b', 'gamma_g', 'gamma_s', )}
    del _L3_conv_all

    return {
        "x": x,
        "L0_conv_w_qkv": _L0_conv_in["w_qkv"],
        "L0_conv_w_proj": _L0_conv_in["w_proj"],
        "L0_conv_b_proj": _L0_conv_in["b_proj"],
        "L1_conv_ln1_g": _L1_conv_in["ln1_g"],
        "L1_conv_ln1_b": _L1_conv_in["ln1_b"],
        "L1_conv_Lambda": _L1_conv_in["Lambda"],
        "L1_conv_Bmat": _L1_conv_in["Bmat"],
        "L1_conv_Cmat": _L1_conv_in["Cmat"],
        "L1_conv_D": _L1_conv_in["D"],
        "L1_conv_log_step": _L1_conv_in["log_step"],
        "L1_conv_ln2_g": _L1_conv_in["ln2_g"],
        "L1_conv_ln2_b": _L1_conv_in["ln2_b"],
        "L1_conv_W_enc": _L1_conv_in["W_enc"],
        "L1_conv_W_dec": _L1_conv_in["W_dec"],
        "L2_conv_w77": _L2_conv_in["w77"],
        "L2_conv_b77": _L2_conv_in["b77"],
        "L2_conv_w53": _L2_conv_in["w53"],
        "L2_conv_b53": _L2_conv_in["b53"],
        "L2_conv_w35": _L2_conv_in["w35"],
        "L2_conv_b35": _L2_conv_in["b35"],
        "L2_conv_w7w": _L2_conv_in["w7w"],
        "L2_conv_w7h": _L2_conv_in["w7h"],
        "L2_conv_w5w": _L2_conv_in["w5w"],
        "L2_conv_w5h": _L2_conv_in["w5h"],
        "L3_conv_Wk": _L3_conv_in["Wk"],
        "L3_conv_Wv": _L3_conv_in["Wv"],
        "L3_conv_Wr": _L3_conv_in["Wr"],
        "L3_conv_Wo": _L3_conv_in["Wo"],
        "L3_conv_ln_g": _L3_conv_in["ln_g"],
        "L3_conv_ln_b": _L3_conv_in["ln_b"],
        "L3_conv_w_param": _L3_conv_in["w_param"],
        "L3_conv_u": _L3_conv_in["u"],
        "L3_conv_conv_w": _L3_conv_in["conv_w"],
        "L3_conv_bn_g": _L3_conv_in["bn_g"],
        "L3_conv_bn_b": _L3_conv_in["bn_b"],
        "L3_conv_gamma_g": _L3_conv_in["gamma_g"],
        "L3_conv_gamma_s": _L3_conv_in["gamma_s"],
    }

def reference(x, L0_conv_w_qkv, L0_conv_w_proj, L0_conv_b_proj, L1_conv_ln1_g, L1_conv_ln1_b, L1_conv_Lambda, L1_conv_Bmat, L1_conv_Cmat, L1_conv_D, L1_conv_log_step, L1_conv_ln2_g, L1_conv_ln2_b, L1_conv_W_enc, L1_conv_W_dec, L2_conv_w77, L2_conv_b77, L2_conv_w53, L2_conv_b53, L2_conv_w35, L2_conv_b35, L2_conv_w7w, L2_conv_w7h, L2_conv_w5w, L2_conv_w5h, L3_conv_Wk, L3_conv_Wv, L3_conv_Wr, L3_conv_Wo, L3_conv_ln_g, L3_conv_ln_b, L3_conv_w_param, L3_conv_u, L3_conv_conv_w, L3_conv_bn_g, L3_conv_bn_b, L3_conv_gamma_g, L3_conv_gamma_s):
    import jax
    import jax.numpy as jnp
    def _L0_conv_ref(x, w_qkv, w_proj, b_proj):
        import jax, jax.numpy as jnp
        import numpy as np
        DIM = 384
        HEADS = 8
        B, C, H, W = x.shape
        h = HEADS
        d = C // h
        scale = d ** (-0.5)
        qkv = jnp.einsum('oc,bchw->bohw', w_qkv, x)
        q, k, v = jnp.split(qkv, 3, axis=1)

        def to_heads(y):
            return y.reshape(B, h, d, H * W).transpose(0, 1, 3, 2)
        q, k, v = (to_heads(q), to_heads(k), to_heads(v))
        att = jnp.einsum('bhxd,bhyd->bhxy', q * scale, k)
        att = jax.nn.softmax(att, axis=-1)
        out = jnp.einsum('bhxy,bhyd->bhxd', att, v)
        out = out.transpose(0, 1, 3, 2).reshape(B, C, H, W)
        out = jnp.einsum('oc,bchw->bohw', w_proj, out) + b_proj[None, :, None, None]
        return out

    def _L1_conv_ref(x, ln1_g, ln1_b, Lambda, Bmat, Cmat, D, log_step, ln2_g, ln2_b, W_enc, W_dec):
        import jax, jax.numpy as jnp
        import numpy as np
        BANDLIMIT = 0.5
        STEP_SCALE = 1.0
        LN_EPS = 1e-05

        def _layernorm(x, g, b):
            mu = jnp.mean(x, axis=-1, keepdims=True)
            xc = x - mu
            inv = jax.lax.rsqrt(jnp.mean(xc * xc, axis=-1, keepdims=True) + LN_EPS)
            return xc * inv * g + b
        Bsz, C, H, W = x.shape
        u = x.reshape(Bsz, C, H * W).transpose(0, 2, 1)
        fx = _layernorm(u, ln1_g, ln1_b)
        res = fx
        lam = Lambda[..., 0] + 1j * Lambda[..., 1]
        Bc = Bmat[..., 0] + 1j * Bmat[..., 1]
        Cc = Cmat[..., 0] + 1j * Cmat[..., 1]
        step = STEP_SCALE * jnp.exp(log_step)
        freqs = step / STEP_SCALE * jnp.abs(Lambda[..., 1]) / (2.0 * jnp.pi)
        mask = (freqs < BANDLIMIT * 0.5).astype(Cc.dtype)
        Cc = Cc * mask
        lam_bar = jnp.exp(lam * step)
        B_bar = ((lam_bar - 1.0) / lam)[:, None] * Bc
        Bu = jnp.einsum('ph,blh->blp', B_bar, fx.astype(B_bar.dtype))
        lam_el = jnp.broadcast_to(lam_bar, Bu.shape)

        def binop(a, b):
            return (a[0] * b[0], b[0] * a[1] + b[1])
        _, xs = jax.lax.associative_scan(binop, (lam_el, Bu), axis=1)
        y = 2.0 * jnp.real(jnp.einsum('hp,blp->blh', Cc, xs)) + D * fx
        y = jax.nn.gelu(y, approximate=False) + res
        fy = _layernorm(y, ln2_g, ln2_b)
        z = fy @ W_enc.T
        z1, z2 = jnp.split(z, 2, axis=-1)
        z = z1 * jax.nn.gelu(z2, approximate=False)
        y = z @ W_dec.T + fy
        return y.transpose(0, 2, 1).reshape(Bsz, C, H, W)

    def _L2_conv_ref(x, w77, b77, w53, b53, w35, b35, w7w, w7h, w5w, w5h):
        import jax, jax.numpy as jnp
        import numpy as np
        C = 384

        def dwconv(x, w, pad_h, pad_w, stride=(1, 1)):
            return jax.lax.conv_general_dilated(x, w, window_strides=stride, padding=((pad_h, pad_h), (pad_w, pad_w)), dimension_numbers=('NCHW', 'OIHW', 'NCHW'), feature_group_count=C)
        bias = (b77 + b53 + b35)[None, :, None, None]
        out = dwconv(x, w77, 3, 3) + dwconv(x, w53, 2, 1) + dwconv(x, w35, 1, 2) + dwconv(dwconv(x, w7w, 0, 3), w7h, 3, 0) + dwconv(dwconv(x, w5w, 0, 2), w5h, 2, 0) + bias
        return out

    def _L3_conv_ref(x, Wk, Wv, Wr, Wo, ln_g, ln_b, w_param, u, conv_w, bn_g, bn_b, gamma_g, gamma_s):
        import jax, jax.numpy as jnp
        import numpy as np
        NEG = -1e+38

        def wkv_scan(w, u, k, v):
            B, T, C = k.shape
            kT = jnp.swapaxes(k, 0, 1)
            vT = jnp.swapaxes(v, 0, 1)
            aa = jnp.zeros((B, C), k.dtype)
            bb = jnp.zeros((B, C), k.dtype)
            pp = jnp.full((B, C), NEG, k.dtype)

            def step(carry, kv):
                aa, bb, pp = carry
                kt, vt = kv
                ww = u + kt
                p = jnp.maximum(pp, ww)
                e1 = jnp.exp(pp - p)
                e2 = jnp.exp(ww - p)
                y = (e1 * aa + e2 * vt) / (e1 * bb + e2)
                ww2 = pp + w
                p2 = jnp.maximum(ww2, kt)
                f1 = jnp.exp(ww2 - p2)
                f2 = jnp.exp(kt - p2)
                return ((f1 * aa + f2 * vt, f1 * bb + f2, p2), y)
            _, y = jax.lax.scan(step, (aa, bb, pp), (kT, vT))
            return jnp.swapaxes(y, 0, 1)
        B, C, H, W = x.shape
        T = H * W
        x_seq = jnp.swapaxes(x.reshape(B, C, T), 1, 2)
        k = jnp.einsum('btc,dc->btd', x_seq, Wk)
        v = jnp.einsum('btc,dc->btd', x_seq, Wv)
        r = jax.nn.sigmoid(jnp.einsum('btc,dc->btd', x_seq, Wr))
        real_w = -jnp.exp(w_param)
        x_fwd = wkv_scan(real_w, u, k, v)
        x_bwd = jnp.flip(wkv_scan(real_w, u, jnp.flip(k, 1), jnp.flip(v, 1)), 1)
        h = r * (x_fwd + x_bwd) * 0.5
        mu = jnp.mean(h, -1, keepdims=True)
        var = jnp.mean((h - mu) ** 2, -1, keepdims=True)
        hn = (h - mu) * jax.lax.rsqrt(var + 1e-05) * ln_g + ln_b
        out_g = jnp.einsum('btc,dc->btd', hn, Wo)
        out_g = jnp.swapaxes(out_g, 1, 2).reshape(B, C, H, W)
        y = jax.lax.conv_general_dilated(x, conv_w, (1, 1), 'SAME', dimension_numbers=('NCHW', 'OIHW', 'NCHW'))
        y = y * (bn_g / jnp.sqrt(1.0 + 1e-05)).reshape(1, C, 1, 1) + bn_b.reshape(1, C, 1, 1)
        y = jnp.where(y > 0, y, 0.01 * y)
        return out_g * gamma_g + y * gamma_s

    def _gn(v, G=32, eps=1e-5):
        B_, C_, H_, W_ = v.shape
        g = v.reshape(B_, G, C_ // G, H_, W_)
        m = jnp.mean(g, axis=(2, 3, 4), keepdims=True)
        s = jnp.var(g, axis=(2, 3, 4), keepdims=True)
        return ((g - m) / jnp.sqrt(s + eps)).reshape(v.shape)

    def _ln_c(v, eps=1e-6):
        m = jnp.mean(v, axis=1, keepdims=True)
        s = jnp.var(v, axis=1, keepdims=True)
        return (v - m) / jnp.sqrt(s + eps)

    def _ln_t(v, eps=1e-5):
        m = jnp.mean(v, axis=-1, keepdims=True)
        s = jnp.var(v, axis=-1, keepdims=True)
        return (v - m) / jnp.sqrt(s + eps)

    def _to_tokens(v):
        B_, C_, H_, W_ = v.shape
        return v.reshape(B_, C_, H_ * W_).transpose(0, 2, 1)
    def _from_tokens(t, like):
        B_, C_, H_, W_ = like.shape
        return t.transpose(0, 2, 1).reshape(B_, C_, H_, W_)

    x = x + _L0_conv_ref(_gn(x), L0_conv_w_qkv, L0_conv_w_proj, L0_conv_b_proj)
    x = x + _L1_conv_ref(_gn(x), L1_conv_ln1_g, L1_conv_ln1_b, L1_conv_Lambda, L1_conv_Bmat, L1_conv_Cmat, L1_conv_D, L1_conv_log_step, L1_conv_ln2_g, L1_conv_ln2_b, L1_conv_W_enc, L1_conv_W_dec)
    x = x + _L2_conv_ref(_gn(x), L2_conv_w77, L2_conv_b77, L2_conv_w53, L2_conv_b53, L2_conv_w35, L2_conv_b35, L2_conv_w7w, L2_conv_w7h, L2_conv_w5w, L2_conv_w5h)
    x = x + _L3_conv_ref(_gn(x), L3_conv_Wk, L3_conv_Wv, L3_conv_Wr, L3_conv_Wo, L3_conv_ln_g, L3_conv_ln_b, L3_conv_w_param, L3_conv_u, L3_conv_conv_w, L3_conv_bn_g, L3_conv_bn_b, L3_conv_gamma_g, L3_conv_gamma_s)
    return x


_drawn_inputs = setup_inputs


def setup_inputs(seed=0):
    import zlib

    import numpy as np

    out = dict(_drawn_inputs(seed))
    spreads = {'L3_conv_ln_g': (1.0, 0.2),
     'L3_conv_ln_b': (0.0, 0.315),
     'L3_conv_bn_g': (1.0, 0.548),
     'L3_conv_bn_b': (0.0, 0.481),
     'L3_conv_gamma_g': (0.5, 0.2),
     'L3_conv_gamma_s': (0.5, 0.2)}
    factors = {'L2_conv_w7w': 7.218,
     'L2_conv_w7h': 7.292,
     'L2_conv_w5w': 8.0,
     'L2_conv_w5h': 8.0,
     'L3_conv_w_param': 27.704,
     'L3_conv_u': 36.997}
    for name, (base, spread) in spreads.items():
        noise = np.random.default_rng([zlib.crc32(name.encode()), seed]).standard_normal(out[name].shape)
        drawn = base * np.exp(spread * noise) if base else spread * noise
        out[name] = jnp.asarray(drawn.astype(out[name].dtype))
    for name, factor in factors.items():
        out[name] = (out[name] * factor).astype(out[name].dtype)
    return out
```

```python
from contextlib import ExitStack

import numpy as np

import concourse.bass as bass
from concourse import mybir

F32 = mybir.dt.float32
F32R = mybir.dt.float32r
ALU = mybir.AluOpType
ACT = mybir.ActivationFunctionType
AX = mybir.AxisListType

P = 128
HALF = 512
BANKS = 8
GROUPS = 32
GN_EPS = 1e-5


class Signal:

    def __init__(self, sem, per=None, head=0):
        self.sem, self.per, self.head, self.count = sem, per, head, 0

    def next(self):
        self.count += 1
        return self.sem

    def at(self, nth, i=None):
        assert nth + self.head >= 1 and (self.per is None or nth <= self.per)
        return nth + self.head if i is None else i * self.per + nth + self.head

    def end_of_pass(self):
        assert self.per is None or self.count == self.per, (self.count, self.per)


def as_f32(ap):
    return ap.bitcast(F32)


def turn_weights(nc, name, ident, pieces, loads):
    with ExitStack() as ctx:
        turned_psum = ctx.enter_context(nc.psum_tensor(name + "_turning", [P, 4, HALF], F32))
        loaded = ctx.enter_context(nc.semaphore(name + "_loaded"))
        turned = Signal(ctx.enter_context(nc.semaphore(name + "_turned")))
        kept = [Signal(ctx.enter_context(nc.semaphore(f"{name}_kept{n}"))) for n in range(2)]
        block = ctx.enter_context(nc.Block())

        @block.sync
        def _(sp):
            for tile, source in loads:
                sp.dma_start(tile, source).then_inc(loaded, 16)

        @block.tensor
        def _(pe):
            pe.wait_ge(loaded, 16 * len(loads))
            for n, (blocks, _) in enumerate(pieces):
                if n >= 4:
                    pe.wait_ge(kept[n % 2].sem, kept[n % 2].at((n - 4) // 2 + 1))
                for j, source in enumerate(blocks):
                    rows, cols = source.shape
                    ins = nc.tensor.transpose(turned_psum[0:cols, n % 4, j * rows:(j + 1) * rows], source,
                                              ident[0:rows, 0:rows])
                ins.then_inc(turned.next(), 1)

        def keep(eng, copy, parity):
            for n, (blocks, target) in enumerate(pieces):
                if n % 2 == parity:
                    eng.wait_ge(turned.sem, turned.at(n + 1))
                    rows, cols = blocks[0].shape
                    source = turned_psum[0:cols, n % 4, 0:len(blocks) * rows]
                    if len(target.shape) == 3:
                        source = source.rearrange("p (a b) -> p a b", b=target.shape[2])
                    copy(target, source).then_inc(kept[parity].next(), 1)

        @block.scalar
        def _(act):
            act.wait_ge(loaded, 16 * len(loads))
            keep(act, nc.scalar.copy, 0)

        @block.vector
        def _(dve):
            keep(dve, nc.vector.tensor_copy, 1)


def make_constants(nc, ident, group_mean, head_mask, col_mean):
    with ExitStack() as ctx:
        filled = Signal(ctx.enter_context(nc.semaphore("filled")))
        block = ctx.enter_context(nc.Block())

        @block.gpsimd
        def _(pool):
            pool.memset(ident, 0.0).then_inc(filled.next(), 1)
            pool.memset(group_mean, GROUPS / P).then_inc(filled.next(), 1)
            pool.memset(head_mask, -1.0).then_inc(filled.next(), 1)
            pool.memset(col_mean, 1.0 / (3 * P)).then_inc(filled.next(), 1)
            pool.wait_ge(filled.sem, filled.at(filled.count))
            pool.affine_select(out=ident, in_=ident, compare_op=ALU.not_equal, fill=1.0, base=0,
                                                pattern=[[-1, P]], channel_multiplier=1).then_inc(filled.next(), 1)
            pool.affine_select(out=head_mask, in_=head_mask, compare_op=ALU.is_ge, fill=0.0,
                                                base=-HEAD, pattern=[[0, 1]], channel_multiplier=1).then_inc(filled.next(), 1)
            view = group_mean.rearrange("p (g e) -> p g e", e=4)
            pool.affine_select(out=view, in_=view, compare_op=ALU.is_ge, fill=0.0, base=0,
                                                 pattern=[[-4, GROUPS], [0, 4]], channel_multiplier=1).then_inc(filled.next(), 1)
            pool.wait_ge(filled.sem, filled.at(filled.count))
            pool.affine_select(out=view, in_=view, compare_op=ALU.is_ge, fill=0.0, base=3,
                                                 pattern=[[4, GROUPS], [0, 4]], channel_multiplier=-1).then_inc(filled.next(), 1)
            pool.wait_ge(filled.sem, filled.at(filled.count))


class GroupNorm:

    STEPS = 15

    def __init__(self, nc, sb, turn, name):
        self.nc, self.turn = nc, turn
        self.stats = sb(name + "_stats", [P, 6, 6], F32)
        self.both = sb(name + "_both", [P, 2], F32)
        self.moments = sb(name + "_moments", [P, 2], F32)
        self.var = sb(name + "_var", [P, 1], F32)
        self.log = sb(name + "_log", [P, 1], F32)
        self.rstd = sb(name + "_rstd", [P, 1], F32)
        self.shift = sb(name + "_shift", [P, 1], F32)

    def vector_moments(self, dve, x, step, i, ready):
        nc, both = self.nc, self.both
        chunks = x.shape[1] // HALF
        for n in range(chunks):
            nc.vector.bn_stats(self.stats[:, n, :], x[:, n * HALF:(n + 1) * HALF]).then_inc(step.next(), 1)
        dve.wait_ge(step.sem, step.at(step.count, i))
        dve.sem_inc(self.turn, 1)
        nc.vector.bn_aggr(both[:, :], self.stats[:, 0:chunks, :].rearrange("p a b -> p (a b)")).then_inc(step.next(), 1)
        dve.wait_ge(step.sem, step.at(step.count, i))
        nc.vector.scalar_tensor_tensor(both[:, 1:2], both[:, 0:1], both[:, 0:1], both[:, 1:2],
                                                       ALU.mult, ALU.add).then_inc(ready.next(), 1)

    def tensor_groups(self, pe, psum, group_mean):
        return self.nc.tensor.matmul(psum, group_mean, self.both[:, :], start=True, stop=True)

    def vector_variance(self, dve, psum, step, i, ready):
        nc, m = self.nc, self.moments
        nc.vector.tensor_copy(m[:, :], psum).then_inc(step.next(), 1)
        dve.wait_ge(step.sem, step.at(step.count, i))
        nc.vector.tensor_tensor(self.var[:, :], m[:, 0:1], m[:, 0:1], ALU.mult).then_inc(step.next(), 1)
        dve.wait_ge(step.sem, step.at(step.count, i))
        nc.vector.scalar_tensor_tensor(self.var[:, :], m[:, 1:2], GN_EPS, self.var[:, :],
                                                       ALU.add, ALU.subtract).then_inc(ready.next(), 1)

    def scalar_rstd(self, act, step, i, ready):
        self.nc.scalar.activation(self.log[:, :], self.var[:, :], ACT.Ln).then_inc(step.next(), 1)
        act.wait_ge(step.sem, step.at(step.count, i))
        self.nc.scalar.activation(self.rstd[:, :], self.log[:, :], ACT.Exp, scale=-0.5).then_inc(ready.next(), 1)

    def vector_shift(self, dve, step, i):
        self.nc.vector.scalar_tensor_tensor(self.shift[:, :], self.moments[:, 0:1], -1.0,
                                                           self.rstd[:, :], ALU.mult, ALU.mult).then_inc(step.next(), 1)
        dve.wait_ge(step.sem, step.at(step.count, i))


HEAD = 48
HEADS = 8
B, C, T = 8, 384, 1024
CT = C // P


def attention_layer(nc, const, x_in, x_out, w_qkv, w_proj, b_proj):
    SCALE = HEAD ** -0.5
    UNITS = 2 * T // P
    RING = 3
    DUP = 2 * HEAD
    with ExitStack() as ctx:
        def sb(name, shape, dt=F32):
            return ctx.enter_context(nc.sbuf_tensor(name, shape, dt))

        def signal(name, per=None):
            return Signal(ctx.enter_context(nc.semaphore(name)), per)

        q_w = sb("q_w", [P, CT, HEADS, 2, HEAD])
        k_w = sb("k_w", [P, CT, HEADS, 2, HEAD])
        v_w = sb("v_w", [P, CT, C])
        proj_w = sb("proj_w", [P, HEADS // 2, C])
        proj_b = sb("proj_b", [P, CT])
        with nc.sbuf_tensor("qkv_rows", [P, 9, C], F32) as qkv_rows, \
                nc.sbuf_tensor("proj_rows", [P, CT, HEADS, 64], F32) as proj_rows:
            with nc.semaphore("pad_zero") as pad_zero, nc.Block() as block:
                @block.vector
                def _(dve):
                    nc.vector.memset(proj_rows[:, :, :, :], 0.0).then_inc(pad_zero, 1)
                    dve.wait_ge(pad_zero, 1)
            pieces = []
            for t in range(CT):
                rows = [qkv_rows[:, r, t::CT] for r in range(9)]
                for w, first in ((q_w, 0), (k_w, 3)):
                    for twice in range(2):
                        pieces.append((rows[first:first + 3], w[:, t, :, twice, :]))
                pieces.append((rows[6:9], v_w[:, t, :]))
            for pair in range(HEADS // 2):
                pieces.append(([proj_rows[:, m, 2 * pair:2 * pair + 2, :].rearrange("p a b -> p (a b)")
                                for m in range(CT)], proj_w[:, pair, :]))
            turn_weights(nc, "w0", const["ident"], pieces, [
                (qkv_rows[:, :, :], w_qkv.rearrange("(r p) c -> p r c", p=P)),
                *[(proj_rows[:, m, :, 0:HEAD], w_proj.rearrange("(p m) (h d) -> m p h d", m=CT, d=HEAD)[m])
                  for m in range(CT)],
                (proj_b[:, :], b_proj.rearrange("(p t) -> p t", t=CT)),
            ])

        gn = GroupNorm(nc, sb, ctx.enter_context(nc.semaphore("gn0_turn")), "gn0")
        xin = sb("xin", [P, CT * T])
        xres = sb("xres", [P, CT * T])
        xn = sb("xn", [P, CT, T])
        q_hi = sb("q_hi", [P, 2, HALF], F32R)
        q_all = sb("q_all", [P, 2, T], F32R)
        k_hi = sb("k_hi", [P, 2, T], F32R)
        k_lo = sb("k_lo", [P, 2, T], F32R)
        v_hi = sb("v_hi", [P, T // P, HEADS // 2, 3, 64], F32R)
        v_lo = sb("v_lo", [P, T // P, HEADS // 2, 3, 64], F32R)
        maxima = sb("maxima", [P, DUP + T // P], F32R)
        probs = sb("probs", [P, RING, HALF])
        p_hi = sb("p_hi", [P, RING, HALF], F32R)
        p_lo = sb("p_lo", [P, RING, HALF], F32R)
        o_raw = sb("o_raw", [P, T])
        o_inv = sb("o_inv", [P, T])
        heads_out = sb("heads_out", [P, HEADS // 2, T])
        ident_r = sb("ident_r", [P, P], F32R)

        s_psum = ctx.enter_context(nc.psum_tensor("s_psum", [P, 2, HALF], F32))
        o_psum = ctx.enter_context(nc.psum_tensor("o_psum", [P, 2, HALF], F32))
        m_psum = ctx.enter_context(nc.psum_tensor("m_psum", [P, 4, HALF], F32))

        x_loaded, res_loaded, stored = (ctx.enter_context(nc.semaphore(n)) for n in ("x_loaded", "res_loaded", "stored"))
        N = HEADS * UNITS
        xin_free = signal("xin_free")
        step = signal("step", 7 + 2 + 1)
        act_step = signal("act_step", 1)
        gn_moments = signal("gn_moments", 1)
        gn_groups = signal("gn_groups", 1)
        gn_var = signal("gn_var", 1)
        gn_rstd = signal("gn_rstd", 1)
        xn_ready = signal("xn_ready", 1)
        v_made = signal("v_made", T // P)
        v_high = signal("v_high", T // P)
        v_low = signal("v_low", T // P)
        qk_made = signal("qk_made", 4 * HEADS)
        qk_high = signal("qk_high", 4 * HEADS)
        qk_low = signal("qk_low", 4 * HEADS)
        rows_made = signal("rows_made", 8 * HEADS)
        rows_max = signal("rows_max", 8 * HEADS)
        max_turned = signal("max_turned", HEADS)
        max_placed = signal("max_placed", HEADS)
        scored = signal("scored", N)
        exped = signal("exped", N)
        p_high = signal("p_high", N)
        p_low = signal("p_low", N)
        weighed = signal("weighed", N)
        o_copied = signal("o_copied", HEADS)
        inverted = signal("inverted", 8 * HEADS)
        head_done = signal("head_done", HEADS)
        projected = signal("projected", 2 * CT)
        y_made = signal("y_made", 2 * CT)
        ready = signal("ready")
        turned_ident = signal("turned_ident")

        def with_sums(v, tile, h):
            return v[:, tile, h // 2, h % 2:h % 2 + 2, :].rearrange("p a b -> p (a b)")

        def by_head(ap):
            return ap.rearrange("p (a b d) -> p a b d", b=2, d=HEAD)

        def heads_of(v, tile):
            return v[:, tile, :, 0::2, 0:HEAD]

        block = ctx.enter_context(nc.Block())

        @block.sync
        def _(sp):
            sp.sem_inc(stored, 16)
            with sp.Fori(0, B) as i:
                sp.wait_ge(stored, i * 16 + 16)
                sp.dma_start(xres[:, :], x_in[bass.ds(i, 1)].rearrange("a (p t) n -> p (a t n)", t=CT)).then_inc(res_loaded, 16)
                sp.wait_ge(y_made.sem, y_made.at(2 * CT, i))
                sp.dma_start(x_out[bass.ds(i, 1)].rearrange("a (p t) n -> p (a t n)", t=CT), xres[:, :]).then_inc(stored, 16)
            sp.wait_ge(stored, 16 * B + 16)

        @block.gpsimd
        def _(pool):
            pool.memset(heads_out[:, :, :], 0.0).then_inc(ready.next(), 1)
            pool.memset(as_f32(v_hi[:, :, :, :, :]), 1.0).then_inc(ready.next(), 1)
            pool.memset(as_f32(v_lo[:, :, :, :, :]), 0.0).then_inc(ready.next(), 1)
            pool.memset(as_f32(maxima[:, :]), 0.0).then_inc(ready.next(), 1)
            pool.wait_ge(ready.sem, ready.at(4))
            pool.memset(as_f32(k_hi[DUP:DUP + 1, :, :]), 1.0).then_inc(ready.next(), 1)
            with pool.Fori(0, B) as i:
                pool.wait_ge(xin_free.sem, i + 1)
                pool.dma_start(xin[:, :], x_in[bass.ds(i, 1)].rearrange("a (p t) n -> p (a t n)", t=CT)).then_inc(x_loaded, 16)

        @block.scalar
        def _(act):
            nc.scalar.copy(ident_r[:, :], const["ident"]).then_inc(turned_ident.next(), 1)
            with act.Fori(0, B) as i:
                act.wait_ge(gn_var.sem, gn_var.at(1, i))
                gn.scalar_rstd(act, act_step, i, gn_rstd)
                for tile in range(T // P):
                    act.wait_ge(v_made.sem, v_made.at(tile + 1, i))
                    nc.scalar.copy(heads_of(v_hi, tile), by_head(m_psum[:, 2 * (tile % 2), 0:C])).then_inc(v_high.next(), 1)

                def qk_part(h, n):
                    act.wait_ge(qk_made.sem, qk_made.at(4 * h + n + 1, i))
                    source = m_psum[0:DUP, n, :]
                    if n < 2:
                        if h > 0:
                            act.wait_ge(qk_low.sem, qk_low.at(4 * (h - 1) + n + 1, i))
                        target = q_hi[0:DUP, n, :]
                    else:
                        target = k_hi[0:DUP, h % 2, (n - 2) * HALF:(n - 1) * HALF]
                    nc.scalar.copy(target, source).then_inc(qk_high.next(), 1)

                def place_max(h):
                    act.wait_ge(max_turned.sem, max_turned.at(h + 1, i))
                    nc.scalar.copy(q_all[DUP:DUP + 1, h % 2, :],
                                                        m_psum[DUP:DUP + 1, 0:2, :].rearrange("p a b -> p (a b)")).then_inc(max_placed.next(), 1)

                for n in range(4):
                    qk_part(0, n)
                place_max(0)
                for h in range(HEADS):
                    for n in range(UNITS):
                        u = h * UNITS + n
                        act.wait_ge(scored.sem, scored.at(u + 1, i))
                        if u >= RING:
                            act.wait_ge(p_low.sem, p_low.at(u - RING + 1, i))
                        nc.scalar.activation(probs[:, u % RING, :], s_psum[:, u % 2, :], ACT.Exp, scale=SCALE).then_inc(exped.next(), 1)
                        if u >= RING:
                            act.wait_ge(weighed.sem, weighed.at(u - RING + 1, i))
                        act.wait_ge(exped.sem, exped.at(u + 1, i))
                        nc.scalar.copy(p_hi[:, u % RING, :], probs[:, u % RING, :]).then_inc(p_high.next(), 1)
                        if h + 1 < HEADS and n < 4:
                            qk_part(h + 1, n)
                        if h + 1 < HEADS and n == 14:
                            place_max(h + 1)
                    act.wait_ge(weighed.sem, weighed.at((h + 1) * UNITS, i))
                    if h > 0:
                        act.wait_ge(head_done.sem, head_done.at(h, i))
                    nc.scalar.copy(o_raw[:, :], o_psum[:, :, :].rearrange("p a b -> p (a b)")).then_inc(o_copied.next(), 1)
            for s in (act_step, gn_rstd, v_high, qk_high, max_placed, exped, p_high, o_copied):
                s.end_of_pass()

        @block.vector
        def _(dve):
            dve.wait_ge(ready.sem, ready.at(5))
            dve.sem_inc(xin_free.sem, 1)
            with dve.Fori(0, B) as i:
                dve.wait_ge(x_loaded, i * 16 + 16)
                gn.vector_moments(dve, xin[:, :], step, i, gn_moments)
                dve.wait_ge(gn_groups.sem, gn_groups.at(1, i))
                gn.vector_variance(dve, m_psum[:, 0, 0:2], step, i, gn_var)
                dve.wait_ge(gn_rstd.sem, gn_rstd.at(1, i))
                gn.vector_shift(dve, step, i)
                nc.vector.tensor_scalar(xn[:, :, :].rearrange("p t n -> p (t n)"), xin[:, :],
                                                           gn.rstd[:, :], gn.shift[:, :], ALU.mult, ALU.add).then_inc(xn_ready.next(), 1)
                dve.wait_ge(xn_ready.sem, xn_ready.at(1, i))
                dve.sem_inc(xin_free.sem, 1)
                for tile in range(T // P):
                    dve.wait_ge(v_high.sem, v_high.at(tile + 1, i))
                    nc.vector.tensor_tensor(heads_of(v_lo, tile), by_head(m_psum[:, 2 * (tile % 2), 0:C]),
                                                            as_f32(heads_of(v_hi, tile)), ALU.subtract).then_inc(v_low.next(), 1)

                def qk_part(h, n):
                    dve.wait_ge(qk_high.sem, qk_high.at(4 * h + n + 1, i))
                    source = m_psum[0:DUP, n, :]
                    if n < 2:
                        ins = nc.vector.scalar_tensor_tensor(
                            q_all[0:DUP, h % 2, n * HALF:(n + 1) * HALF], as_f32(q_hi[0:DUP, n, :]),
                            const["head_mask"][0:DUP, :], source, ALU.mult, ALU.add)
                    else:
                        cols = slice((n - 2) * HALF, (n - 1) * HALF)
                        ins = nc.vector.tensor_tensor(k_lo[0:DUP, h % 2, cols], source,
                                                      as_f32(k_hi[0:DUP, h % 2, cols]), ALU.subtract)
                    ins.then_inc(qk_low.next(), 1)

                def row_max(h, tile):
                    dve.wait_ge(rows_made.sem, rows_made.at(8 * h + tile + 1, i))
                    slot = 2 * (tile % 2)
                    nc.vector.tensor_reduce(
                        maxima[:, DUP + tile:DUP + tile + 1], m_psum[:, slot:slot + 2, :].rearrange("p a b -> p (a b)"),
                        AX.X, ALU.max, negate=True).then_inc(rows_max.next(), 1)

                def invert(h, part):
                    cols = slice(part * P, (part + 1) * P)
                    dve.wait_ge(o_copied.sem, o_copied.at(h + 1, i))
                    values, sums = 64 * (h % 2), 64 * (1 - h % 2)
                    nc.vector.reciprocal(o_inv[values:values + HEAD, cols], o_raw[sums:sums + HEAD, cols]).then_inc(inverted.next(), 1)

                def divide(h):
                    row = 64 * (h % 2)
                    dve.wait_ge(inverted.sem, inverted.at(8 * h + 8, i))
                    nc.vector.tensor_tensor(heads_out[row:row + HEAD, h // 2, :],
                                                                o_raw[row:row + HEAD, :], o_inv[row:row + HEAD, :], ALU.mult).then_inc(head_done.next(), 1)

                for n in range(4):
                    qk_part(0, n)
                for tile in range(8):
                    row_max(0, tile)
                for h in range(HEADS):
                    for n in range(UNITS):
                        u = h * UNITS + n
                        if h + 1 < HEADS and n < 4:
                            qk_part(h + 1, n)
                        if h + 1 < HEADS and 4 <= n < 12:
                            row_max(h + 1, n - 4)
                        dve.wait_ge(p_high.sem, p_high.at(u + 1, i))
                        if u >= RING:
                            dve.wait_ge(weighed.sem, weighed.at(u - RING + 1, i))
                        nc.vector.tensor_tensor(p_lo[:, u % RING, :], probs[:, u % RING, :],
                                                                as_f32(p_hi[:, u % RING, :]), ALU.subtract).then_inc(p_low.next(), 1)
                        if h > 0 and (n < 4 or n >= 12):
                            invert(h - 1, n if n < 4 else n - 8)
                    if h > 0:
                        divide(h - 1)
                for part in range(8):
                    invert(HEADS - 1, part)
                divide(HEADS - 1)
                dve.wait_ge(res_loaded, i * 16 + 16)
                for n in range(2 * CT):
                    m, half = n // 2, n % 2
                    dve.wait_ge(projected.sem, projected.at(n + 1, i))
                    cols = slice(m * T + half * HALF, m * T + (half + 1) * HALF)
                    nc.vector.scalar_tensor_tensor(
                        xres[:, cols], m_psum[:, n % 4, :], proj_b[:, m:m + 1], xres[:, cols], ALU.add, ALU.add).then_inc(y_made.next(), 1)
            for s in (step, gn_moments, gn_var, xn_ready, v_low, qk_low, rows_max, p_low, inverted, head_done, y_made):
                s.end_of_pass()

        @block.tensor
        def _(pe):
            pe.wait_ge(ready.sem, ready.at(5))
            pe.wait_ge(turned_ident.sem, turned_ident.at(1))
            with pe.Fori(0, B) as i:
                pe.wait_ge(gn_moments.sem, gn_moments.at(1, i))
                gn.tensor_groups(pe, m_psum[:, 0, 0:2], const["group_mean"]).then_inc(gn_groups.next(), 1)
                pe.wait_ge(xn_ready.sem, xn_ready.at(1, i))
                for tile in range(T // P):
                    if tile >= 2:
                        pe.wait_ge(v_low.sem, v_low.at(tile - 1, i))
                    for t in range(CT):
                        ins = nc.tensor.matmul(m_psum[:, 2 * (tile % 2), 0:C], xn[:, t, tile * P:(tile + 1) * P],
                                               v_w[:, t, :], start=(t == 0), stop=(t == CT - 1))
                    ins.then_inc(v_made.next(), 1)
                pe.wait_ge(v_low.sem, v_low.at(T // P, i))

                def qk_part(h, n):
                    half = n % 2
                    if h > 0 and n == 0:
                        pe.wait_ge(max_placed.sem, max_placed.at(h, i))
                    for t in range(CT):
                        w = (q_w if n < 2 else k_w)[:, t, h, :, :].rearrange("p a b -> p (a b)")
                        ins = nc.tensor.matmul(m_psum[0:DUP, n, :], w, xn[:, t, half * HALF:(half + 1) * HALF],
                                               start=(t == 0), stop=(t == CT - 1))
                    ins.then_inc(qk_made.next(), 1)

                def row_scores(h, tile):
                    if tile == 0:
                        pe.wait_ge(qk_low.sem, qk_low.at(4 * h + 4, i))
                    if tile >= 2:
                        pe.wait_ge(rows_max.sem, rows_max.at(8 * h + tile - 1, i))
                    for half in range(2):
                        ins = nc.tensor.matmul(m_psum[:, 2 * (tile % 2) + half, :],
                                               q_all[0:DUP, h % 2, tile * P:(tile + 1) * P],
                                               k_hi[0:DUP, h % 2, half * HALF:(half + 1) * HALF], start=True, stop=True)
                    ins.then_inc(rows_made.next(), 1)

                def turn_max(h):
                    pe.wait_ge(rows_max.sem, rows_max.at(8 * h + 8, i))
                    for tile in range(T // P):
                        ins = nc.tensor.matmul(m_psum[0:DUP + 1, tile // 4, (tile % 4) * P:(tile % 4 + 1) * P],
                                               maxima[:, tile:tile + DUP + 1], ident_r[:, :], start=True, stop=True)
                    ins.then_inc(max_turned.next(), 1)

                def scores(u):
                    h, n = u // UNITS, u % UNITS
                    tile, half = n // 2, n % 2
                    if n == 0:
                        pe.wait_ge(max_placed.sem, max_placed.at(h + 1, i))
                    if u >= 2:
                        pe.wait_ge(exped.sem, exped.at(u - 1, i))
                    q = q_all[:, h % 2, half * HALF:(half + 1) * HALF]
                    keys = slice(tile * P, (tile + 1) * P)
                    nc.tensor.matmul(s_psum[:, u % 2, :], k_hi[0:DUP + 1, h % 2, keys], q[0:DUP + 1, :], start=True, stop=False)
                    nc.tensor.matmul(s_psum[:, u % 2, :], k_lo[0:DUP, h % 2, keys], q[0:DUP, :],
                                                      start=False, stop=True).then_inc(scored.next(), 1)

                def weigh(u):
                    h, n = u // UNITS, u % UNITS
                    tile, half = n // 2, n % 2
                    if n == 0 and h > 0:
                        pe.wait_ge(o_copied.sem, o_copied.at(h, i))
                    o = o_psum[:, half, :]
                    pe.wait_ge(p_high.sem, p_high.at(u + 1, i))
                    pe.wait_ge(p_low.sem, p_low.at(u + 1, i))
                    first, last = tile == 0, tile == T // P - 1
                    a_hi, a_lo = with_sums(v_hi, tile, h), with_sums(v_lo, tile, h)
                    nc.tensor.matmul(o, a_hi, p_hi[:, u % RING, :], start=first, stop=False)
                    nc.tensor.matmul(o, a_hi, p_lo[:, u % RING, :], start=False, stop=False)
                    nc.tensor.matmul(o, a_lo, p_hi[:, u % RING, :], start=False, stop=last).then_inc(weighed.next(), 1)

                for n in range(4):
                    qk_part(0, n)
                for tile in range(8):
                    row_scores(0, tile)
                turn_max(0)
                scores(0)
                for u in range(N):
                    h, n = u // UNITS, u % UNITS
                    if h + 1 < HEADS:
                        if n < 4:
                            qk_part(h + 1, n)
                        elif n < 12:
                            row_scores(h + 1, n - 4)
                        elif n == 13:
                            turn_max(h + 1)
                    if u + 1 < N:
                        scores(u + 1)
                    weigh(u)
                pe.wait_ge(head_done.sem, head_done.at(HEADS, i))
                for n in range(2 * CT):
                    m, half = n // 2, n % 2
                    if n >= 4:
                        pe.wait_ge(y_made.sem, y_made.at(n - 3, i))
                    for pair in range(HEADS // 2):
                        ins = nc.tensor.matmul(m_psum[:, n % 4, :], proj_w[:, pair, m * P:(m + 1) * P],
                                               heads_out[:, pair, half * HALF:(half + 1) * HALF],
                                               start=(pair == 0), stop=(pair == HEADS // 2 - 1))
                    ins.then_inc(projected.next(), 1)
                pe.wait_ge(y_made.sem, y_made.at(2 * CT, i))
            for s in (gn_groups, v_made, qk_made, rows_made, max_turned, scored, weighed, projected):
                s.end_of_pass()


class ChannelNorm:

    def __init__(self, nc, sb, name, mean_psum, var_psum, col_mean, eps):
        self.nc, self.mean_psum, self.var_psum, self.col_mean = nc, mean_psum, var_psum, col_mean
        self.log = sb(name + "_log", [P, 2, HALF])
        self.inv = sb(name + "_inv", [P, 2, HALF])
        self.eps = eps

    def tensor_sum(self, psum, x, half):
        for t in range(CT):
            ins = self.nc.tensor.matmul(psum[:, half, :], self.col_mean, x[:, t, half * HALF:(half + 1) * HALF],
                                        start=(t == 0), stop=(t == CT - 1))
        return ins

    def over_tiles(self, ap):
        return ap.unsqueeze(1).broadcast_to([P, CT, HALF])

    def vector_centre(self, x, half):
        cols = x[:, :, half * HALF:(half + 1) * HALF]
        return self.nc.vector.tensor_tensor(cols, cols, self.over_tiles(self.mean_psum[:, half, :]), ALU.subtract)

    def scalar_square(self, squares, x, half):
        cols = slice(half * HALF, (half + 1) * HALF)
        return self.nc.scalar.activation(squares[:, :, cols], x[:, :, cols], ACT.Square)

    def scalar_inverse(self, act, half, step, i, ready):
        self.nc.scalar.activation(self.log[:, half, :], self.var_psum[:, half, :], ACT.Ln, bias=self.eps).then_inc(step.next(), 1)
        act.wait_ge(step.sem, step.at(step.count, i))
        self.nc.scalar.activation(self.inv[:, half, :], self.log[:, half, :], ACT.Exp, scale=-0.5).then_inc(ready.next(), 1)

    def vector_scale(self, x, half):
        cols = x[:, :, half * HALF:(half + 1) * HALF]
        return self.nc.vector.tensor_tensor(cols, cols, self.over_tiles(self.inv[:, half, :]), ALU.mult)


def s5_constants(nc, lam, log_step, tables, decay, gain, keep):
    Q, J = lam.shape[0], 2
    TURN = 6.283185
    TO_ONE = 12582912.0
    TO_HIGH = 1536.0
    with ExitStack() as ctx:
        def sb(name, shape, dt=F32):
            return ctx.enter_context(nc.sbuf_tensor(name, shape, dt))[tuple(slice(None) for _ in shape)]
        count = sb("count", [Q, T], mybir.dt.int32)
        t = sb("times", [Q, T])
        high, low, whole = (sb(n, [Q, T]) for n in ("turn_high", "turn_low", "turn_whole"))
        step, a, f, f_high, f_low, r, s1, s2 = (sb("s5_" + n, [Q, J]) for n in ("step", "a", "f", "fh", "fl", "r", "s1", "s2"))
        trig = sb("s5_trig", [Q, 2, J])
        eps = sb("s5_c", [Q, 4, J])
        counted = Signal(ctx.enter_context(nc.semaphore("counted")))
        v = Signal(ctx.enter_context(nc.semaphore("s5_v")))
        s = Signal(ctx.enter_context(nc.semaphore("s5_s")))
        block = ctx.enter_context(nc.Block())
        V, re, im = nc.vector, lam[:, :, 0], lam[:, :, 1]

        @block.gpsimd
        def _(pool):
            pool.iota(count, pattern=[[1, T]], base=0, channel_multiplier=0).then_inc(counted.next(), 1)

        TRIG = 10
        table_ready = [TRIG + 1 + 10 * (n // 2) + 4 + 3 * (n % 2 + 1) for n in range(2 * J)]

        @block.scalar
        def _(act):
            nc.scalar.activation(step, log_step, ACT.Exp).then_inc(s.next(), 1)
            act.wait_ge(s.sem, s.at(s.count))
            act.wait_ge(v.sem, v.at(1))
            nc.scalar.activation(r, a, ACT.Exp).then_inc(s.next(), 1)
            act.wait_ge(s.sem, s.at(s.count))
            act.wait_ge(v.sem, v.at(TRIG))
            nc.scalar.activation(trig, trig, ACT.Sin, scale=TURN).then_inc(s.next(), 1)
            act.wait_ge(s.sem, s.at(s.count))
            for n in range(2 * J):
                act.wait_ge(v.sem, v.at(table_ready[n]))
                nc.scalar.activation(tables[:, n % 2, n // 2, :], tables[:, n % 2, n // 2, :], ACT.Sin, scale=TURN).then_inc(s.next(), 1)

        @block.vector
        def _(dve):
            def do(ins):
                ins.then_inc(v.next(), 1)
                dve.wait_ge(v.sem, v.at(v.count))
            dve.wait_ge(s.sem, s.at(1))
            do(V.tensor_tensor(a, re, step, ALU.mult))
            do(V.tensor_tensor(f, im, step, ALU.mult))
            do(V.tensor_scalar(f, f, 1.0 / (2.0 * np.pi), None, ALU.mult))
            do(V.tensor_scalar(trig[:, 0, :], f, 0.25, None, ALU.add))
            do(V.tensor_scalar(s1, trig[:, 0, :], TO_ONE, TO_ONE, ALU.add, ALU.subtract))
            do(V.tensor_tensor(trig[:, 0, :], trig[:, 0, :], s1, ALU.subtract))
            do(V.tensor_scalar(s1, f, TO_ONE, TO_ONE, ALU.add, ALU.subtract))
            do(V.tensor_tensor(trig[:, 1, :], f, s1, ALU.subtract))
            do(V.tensor_scalar(f_high, f, TO_HIGH, TO_HIGH, ALU.add, ALU.subtract))
            do(V.tensor_tensor(f_low, f, f_high, ALU.subtract))
            assert v.count == TRIG
            dve.wait_ge(counted.sem, counted.at(1))
            do(V.tensor_copy(t, count))
            for j in range(J):
                do(V.tensor_scalar(high, t, f_high[:, j:j + 1], None, ALU.mult))
                do(V.tensor_scalar(whole, high, TO_ONE, TO_ONE, ALU.add, ALU.subtract))
                do(V.tensor_tensor(high, high, whole, ALU.subtract))
                do(V.scalar_tensor_tensor(high, t, f_low[:, j:j + 1], high, ALU.mult, ALU.add))
                for n, quarter in enumerate((0.25, 0.0)):
                    do(V.tensor_scalar(low, high, quarter, None, ALU.add))
                    do(V.tensor_scalar(whole, low, TO_ONE, TO_ONE, ALU.add, ALU.subtract))
                    do(V.tensor_tensor(tables[:, n, j, :], low, whole, ALU.subtract))
                    assert v.count == table_ready[2 * j + n]
            dve.wait_ge(s.sem, s.at(3))
            do(V.tensor_copy(decay, r))
            nr, ni, den = eps[:, 0, :], eps[:, 1, :], eps[:, 2, :]
            do(V.tensor_tensor(nr, r, trig[:, 0, :], ALU.mult))
            do(V.tensor_scalar(nr, nr, -1.0, None, ALU.add))
            do(V.tensor_tensor(ni, r, trig[:, 1, :], ALU.mult))
            do(V.tensor_tensor(s1, re, re, ALU.mult))
            do(V.tensor_tensor(s2, im, im, ALU.mult))
            do(V.tensor_tensor(den, s1, s2, ALU.add))
            do(V.reciprocal(den, den))
            do(V.tensor_tensor(s1, nr, re, ALU.mult))
            do(V.tensor_tensor(s2, ni, im, ALU.mult))
            do(V.tensor_tensor(s1, s1, s2, ALU.add))
            do(V.tensor_tensor(gain[:, 0, :], s1, den, ALU.mult))
            do(V.tensor_tensor(s1, ni, re, ALU.mult))
            do(V.tensor_tensor(s2, nr, im, ALU.mult))
            do(V.tensor_tensor(s1, s1, s2, ALU.subtract))
            do(V.tensor_tensor(gain[:, 1, :], s1, den, ALU.mult))
            do(V.tensor_tensor(s1, f, f, ALU.mult))
            do(V.tensor_scalar(keep[:, 0, :], s1, 0.0625, 2.0, ALU.is_lt, ALU.mult))
            do(V.tensor_scalar(keep[:, 1, :], s1, 0.0625, -2.0, ALU.is_lt, ALU.mult))


def s5_layer(nc, const, x_in, x_out, w):
    J = 2
    Q = w["log_step"].shape[0] // J
    LN_EPS = 1e-5
    with ExitStack() as ctx:
        def sb(name, shape, dt=F32):
            return ctx.enter_context(nc.sbuf_tensor(name, shape, dt))

        def signal(name, per=None):
            return Signal(ctx.enter_context(nc.semaphore(name)), per)

        b_w = sb("b_w", [P, CT, 2, J, Q])
        c_w = sb("c_w", [Q, 2, J, C])
        enc_w = sb("enc_w", [P, CT, 2 * C])
        dec_w = sb("dec_w", [P, CT, C])
        rows = {n: sb(n + "_c", [P, CT]) for n in ("ln1_g", "ln1_b", "ln2_g", "ln2_b", "D")}
        tables = sb("tables", [Q, 2, J, T])
        decay = sb("decay", [Q, J])
        gain = sb("gain", [Q, 2, J])
        keep = sb("keep", [Q, 2, J])
        lam = sb("lam", [Q, J, 2])
        log_step = sb("log_step", [Q, J])
        eps = sb("eps", [P, 1])
        with nc.semaphore("params") as params, nc.Block() as block:
            small = [(lam[:, :, :], w["Lambda"].rearrange("(j q) e -> q j e", j=J)),
                     (log_step[:, :], w["log_step"].rearrange("(j q) -> q j", j=J)),
                     *[(rows[n][:, :], w[n].rearrange("(p t) -> p t", t=CT)) for n in rows]]

            @block.sync
            def _(sp):
                for tile, source in small:
                    sp.dma_start(tile, source, allow_slow_non_contiguous=True).then_inc(params, 16)
                sp.wait_ge(params, 16 * len(small))

            @block.vector
            def _(dve):
                nc.vector.memset(eps[:, :], LN_EPS)
        s5_constants(nc, lam[:, :, :], log_step[:, :], tables[:, :, :, :], decay[:, :], gain[:, :, :], keep[:, :, :])

        with nc.sbuf_tensor("b_rows", [Q, J, C, 2], F32) as b_rows, nc.sbuf_tensor("b_bar", [Q, 2, J, C], F32) as b_bar, \
                nc.sbuf_tensor("b_part", [Q, J, C], F32) as b_part, \
                nc.sbuf_tensor("c_rows", [P, CT, 2 * J * Q], F32) as c_rows, \
                nc.sbuf_tensor("enc_rows", [P, 2, CT, C], F32) as enc_rows, nc.sbuf_tensor("dec_rows", [P, CT, C], F32) as dec_rows:
            with nc.semaphore("b_loaded") as b_loaded, nc.semaphore("b_step") as b_step, nc.Block() as block:
                @block.sync
                def _(sp):
                    sp.dma_start(b_rows[:, :, :, :], w["Bmat"].rearrange("(j q) c e -> q j c e", j=J)).then_inc(b_loaded, 16)

                @block.vector
                def _(dve):
                    dve.wait_ge(b_loaded, 16)
                    n = 0
                    for j in range(J):
                        re, im = b_rows[:, j, :, 0], b_rows[:, j, :, 1]
                        g_re, g_im = gain[:, 0, j:j + 1], gain[:, 1, j:j + 1]
                        for part, a, b, sign in ((0, re, im, ALU.subtract), (1, im, re, ALU.add)):
                            nc.vector.tensor_scalar(b_part[:, j, :], b, g_im, None, ALU.mult).then_inc(b_step, 1)
                            n += 1
                            dve.wait_ge(b_step, n)
                            nc.vector.scalar_tensor_tensor(b_bar[:, part, j, :], a, g_re, b_part[:, j, :],
                                                           ALU.mult, sign).then_inc(b_step, 1)
                            n += 1
                            dve.wait_ge(b_step, n)
            pieces = []
            for t in range(CT):
                pieces.append(([b_bar[:, part, j, t::CT] for part in range(2) for j in range(J)],
                               b_w[:, t, :, :, :].rearrange("p a b c -> p (a b c)")))
                for half in range(2):
                    pieces.append(([enc_rows[:, half, m, t::CT] for m in range(CT)], enc_w[:, t, half * C:(half + 1) * C]))
                pieces.append(([dec_rows[:, m, t::CT] for m in range(CT)], dec_w[:, t, :]))
            for part in range(2):
                for j in range(J):
                    first = 2 * j * Q + part
                    pieces.append(([c_rows[:, m, first:first + 2 * Q - 1:2] for m in range(CT)], c_w[:, part, j, :]))
            loads = [(c_rows[:, :, :], w["Cmat"].rearrange("(p m) s e -> p m (s e)", m=CT)),
                     (dec_rows[:, :, :], w["W_dec"].rearrange("(p m) c -> p m c", m=CT)),
                     *[(enc_rows[:, half, :, :], w["W_enc"].rearrange("(h p m) c -> h p m c", h=2, m=CT)[half]) for half in range(2)]]
            turn_weights(nc, "w1", const["ident"], pieces, loads)
        with nc.semaphore("c_kept") as c_kept, nc.Block() as block:
            @block.vector
            def _(dve):
                for part in range(2):
                    for j in range(J):
                        nc.vector.tensor_scalar(c_w[:, part, j, :], c_w[:, part, j, :], keep[:, part, j:j + 1], None, ALU.mult)

        gn = GroupNorm(nc, sb, ctx.enter_context(nc.semaphore("gn1_turn")), "gn1")
        xin = sb("xin1", [P, CT * T])
        xres = sb("xres1", [P, CT, T])
        a = sb("a1", [P, CT, T])
        sq = sb("sq1", [P, CT, T])
        f = sb("f1", [P, CT, T])
        u = sb("u1", [Q, 2, J, T])
        z = sb("z1", [Q, 2, J, T])
        prod = sb("prod1", [Q, 2, 2, HALF])
        gate = sb("gate1", [P, 2, HALF])
        psum = ctx.enter_context(nc.psum_tensor("psum1", [P, 4, HALF], F32))
        mean_psum = ctx.enter_context(nc.psum_tensor("mean1", [P, 2, HALF], F32))
        var_psum = ctx.enter_context(nc.psum_tensor("var1", [P, 2, HALF], F32))
        norm = ChannelNorm(nc, sb, "ln", mean_psum, var_psum, const["col_mean"], eps[:, :])

        x_loaded, res_loaded, stored = (ctx.enter_context(nc.semaphore(n)) for n in ("x_loaded1", "res_loaded1", "stored1"))
        xin_free = signal("xin_free1")
        step = signal("step1", 10 + 4)
        act_step = signal("act_step1", 1 + 4)
        gn_moments, gn_groups, gn_var, gn_rstd = (signal(n + "1", 1) for n in ("gn_moments", "gn_groups", "gn_var", "gn_rstd"))
        a_made = signal("a_made", 1 + 2 * CT)
        averaged = signal("averaged", 4)
        centred = signal("centred", 4)
        squared = signal("squared", 4)
        varied = signal("varied", 4)
        inv_made = signal("inv_made", 4)
        f_made = signal("f_made", 4 * CT)
        u_product = signal("u_product", 2 * J)
        products = signal("products", 4 * 2 * J)
        sums = signal("sums", 4 * 2 * J)
        scanned = signal("scanned", 2 * J)
        y_product = signal("y_product", 2 * CT)
        y_plain = signal("y_plain", 2 * CT)
        y_gelu = signal("y_gelu", 2 * CT)
        hidden = signal("hidden", 4 * CT)
        gated = signal("gated", 2 * CT)
        hid_made = signal("hid_made", 2 * CT)
        res_added = signal("res_added", 2)
        decoded = signal("decoded", 2 * CT)
        out_made = signal("out_made", 2 * CT)

        def cols(half):
            return slice(half * HALF, (half + 1) * HALF)

        block = ctx.enter_context(nc.Block())

        @block.sync
        def _(sp):
            sp.sem_inc(stored, 16)
            sp.dma_start(xin[:, :], x_in[0:1].rearrange("a (p t) n -> p (a t n)", t=CT)).then_inc(x_loaded, 16)
            with sp.Fori(0, B) as i:
                sp.wait_ge(stored, i * 16 + 16)
                sp.dma_start(xres[:, :, :].rearrange("p t n -> p (t n)"), x_in[bass.ds(i, 1)].rearrange("a (p t) n -> p (a t n)", t=CT)).then_inc(res_loaded, 16)
                sp.wait_ge(xin_free.sem, i + 1)
                sp.dma_start(xin[:, :], x_in[bass.ds((i + 1) % B, 1)].rearrange("a (p t) n -> p (a t n)", t=CT)).then_inc(x_loaded, 16)
                sp.wait_ge(out_made.sem, out_made.at(2 * CT, i))
                sp.dma_start(x_out[bass.ds(i, 1)].rearrange("a (p t) n -> p (a t n)", t=CT), xres[:, :, :].rearrange("p t n -> p (t n)")).then_inc(stored, 16)
            sp.wait_ge(stored, 16 * B + 16)
            sp.wait_ge(x_loaded, 16 * B + 16)

        @block.gpsimd
        def _(pool):
            with pool.Fori(0, B) as i:
                for way in range(2):
                    for j in range(J):
                        for half in range(2):
                            for part in range(2):
                                n = ((way * J + j) * 2 + half) * 2 + part
                                pool.wait_ge(products.sem, products.at(n + 1, i))
                                pool.tensor_tensor(u[:, part, j, cols(half)], prod[:, part, 0, :],
                                                                  prod[:, part, 1, :], ALU.add if part == way else ALU.subtract).then_inc(sums.next(), 1)
                pool.wait_ge(res_loaded, i * 16 + 16)
                for half in range(2):
                    pool.wait_ge(f_made.sem, f_made.at(2 * CT + CT * (half + 1), i))
                    pool.tensor_tensor(xres[:, :, cols(half)], xres[:, :, cols(half)], f[:, :, cols(half)], ALU.add).then_inc(res_added.next(), 1)
            for s in (sums, res_added):
                s.end_of_pass()

        @block.scalar
        def _(act):
            with act.Fori(0, B) as i:
                act.wait_ge(gn_var.sem, gn_var.at(1, i))
                gn.scalar_rstd(act, act_step, i, gn_rstd)

                def normalise(first):
                    for half in range(2):
                        act.wait_ge(centred.sem, centred.at(first + half + 1, i))
                        norm.scalar_square(sq, a, half).then_inc(squared.next(), 1)
                    for half in range(2):
                        act.wait_ge(varied.sem, varied.at(first + half + 1, i))
                        norm.scalar_inverse(act, half, act_step, i, inv_made)

                normalise(0)
                for n in range(2 * CT):
                    act.wait_ge(y_plain.sem, y_plain.at(n + 1, i))
                    at = a[:, n // 2, cols(n % 2)]
                    nc.scalar.activation(at, at, ACT.Gelu).then_inc(y_gelu.next(), 1)
                normalise(2)
                for n in range(2 * CT):
                    act.wait_ge(hidden.sem, hidden.at(2 * n + 1, i))
                    if n >= 2:
                        act.wait_ge(hid_made.sem, hid_made.at(n - 1, i))
                    nc.scalar.activation(gate[:, n % 2, :], psum[:, 2 * (n % 2), :], ACT.Gelu).then_inc(gated.next(), 1)
            for s in (act_step, gn_rstd, squared, inv_made, y_gelu, gated):
                s.end_of_pass()

        @block.vector
        def _(dve):
            with dve.Fori(0, B) as i:
                dve.wait_ge(x_loaded, i * 16 + 16)
                gn.vector_moments(dve, xin[:, :], step, i, gn_moments)
                dve.wait_ge(gn_groups.sem, gn_groups.at(1, i))
                gn.vector_variance(dve, psum[:, 0, 0:2], step, i, gn_var)
                dve.wait_ge(gn_rstd.sem, gn_rstd.at(1, i))
                gn.vector_shift(dve, step, i)
                nc.vector.tensor_scalar(a[:, :, :].rearrange("p t n -> p (t n)"), xin[:, :],
                                                         gn.rstd[:, :], gn.shift[:, :], ALU.mult, ALU.add).then_inc(a_made.next(), 1)
                dve.wait_ge(a_made.sem, a_made.at(1, i))
                dve.sem_inc(xin_free.sem, 1)

                def normalise(first, g, b):
                    for half in range(2):
                        dve.wait_ge(averaged.sem, averaged.at(first + half + 1, i))
                        norm.vector_centre(a, half).then_inc(centred.next(), 1)
                    for half in range(2):
                        dve.wait_ge(inv_made.sem, inv_made.at(first + half + 1, i))
                        norm.vector_scale(a, half).then_inc(step.next(), 1)
                        dve.wait_ge(step.sem, step.at(step.count, i))
                        for t in range(CT):
                            nc.vector.tensor_scalar(f[:, t, cols(half)], a[:, t, cols(half)],
                                                                     g[:, t:t + 1], b[:, t:t + 1], ALU.mult, ALU.add).then_inc(f_made.next(), 1)

                def turn(n, re, im, sin_first):
                    j, half = (n // 2) % J, n % 2
                    cos, sin = tables[:, 0, j, cols(half)], tables[:, 1, j, cols(half)]
                    for part, (x0, x1) in enumerate(((re, im), (im, re))):
                        if n > 0:
                            dve.wait_ge(sums.sem, sums.at(2 * (n - 1) + part + 1, i))
                        nc.vector.tensor_tensor(prod[:, part, 0, :], x0, cos, ALU.mult)
                        nc.vector.tensor_tensor(prod[:, part, 1, :], x1, sin, ALU.mult).then_inc(products.next(), 1)

                normalise(0, rows["ln1_g"], rows["ln1_b"])
                for n in range(2 * J):
                    dve.wait_ge(u_product.sem, u_product.at(n + 1, i))
                    turn(n, psum[0:Q, 2 * (n % 2), :], psum[0:Q, 2 * (n % 2) + 1, :], False)
                for j in range(J):
                    for part in range(2):
                        dve.wait_ge(sums.sem, sums.at(4 * (j + 1), i))
                        nc.vector.tensor_tensor_scan(
                            z[:, part, j, :], decay[:, j:j + 1].broadcast_to([Q, T]), u[:, part, j, :], 0.0, ALU.mult, ALU.add).then_inc(scanned.next(), 1)
                for n in range(2 * J):
                    j, half = n // 2, n % 2
                    dve.wait_ge(scanned.sem, scanned.at(2 * (j + 1), i))
                    turn(2 * J + n, z[:, 0, j, cols(half)], z[:, 1, j, cols(half)], True)
                for n in range(2 * CT):
                    m, half = n // 2, n % 2
                    dve.wait_ge(y_product.sem, y_product.at(n + 1, i))
                    nc.vector.scalar_tensor_tensor(a[:, m, cols(half)], f[:, m, cols(half)],
                                                                     rows["D"][:, m:m + 1], psum[:, n % 4, :], ALU.mult, ALU.add).then_inc(y_plain.next(), 1)
                for n in range(2 * CT):
                    m, half = n // 2, n % 2
                    dve.wait_ge(y_gelu.sem, y_gelu.at(n + 1, i))
                    nc.vector.tensor_tensor(a[:, m, cols(half)], a[:, m, cols(half)], f[:, m, cols(half)], ALU.add).then_inc(a_made.next(), 1)
                dve.wait_ge(a_made.sem, a_made.at(1 + 2 * CT, i))
                normalise(2, rows["ln2_g"], rows["ln2_b"])
                for n in range(2 * CT):
                    m, half = n // 2, n % 2
                    dve.wait_ge(gated.sem, gated.at(n + 1, i))
                    dve.wait_ge(hidden.sem, hidden.at(2 * n + 2, i))
                    nc.vector.tensor_tensor(sq[:, m, cols(half)], gate[:, n % 2, :],
                                                               psum[:, 2 * (n % 2) + 1, :], ALU.mult).then_inc(hid_made.next(), 1)
                dve.wait_ge(res_added.sem, res_added.at(2, i))
                for n in range(2 * CT):
                    m, half = n // 2, n % 2
                    dve.wait_ge(decoded.sem, decoded.at(n + 1, i))
                    nc.vector.tensor_tensor(xres[:, m, cols(half)], xres[:, m, cols(half)],
                                                               psum[:, n % 4, :], ALU.add).then_inc(out_made.next(), 1)
            for s in (step, gn_moments, gn_var, a_made, centred, f_made, products, scanned, y_plain, hid_made, out_made):
                s.end_of_pass()

        @block.tensor
        def _(pe):
            with pe.Fori(0, B) as i:
                pe.wait_ge(gn_moments.sem, gn_moments.at(1, i))
                gn.tensor_groups(pe, psum[:, 0, 0:2], const["group_mean"]).then_inc(gn_groups.next(), 1)

                def normalise(first):
                    for half in range(2):
                        norm.tensor_sum(mean_psum, a, half).then_inc(averaged.next(), 1)
                    for half in range(2):
                        pe.wait_ge(squared.sem, squared.at(first + half + 1, i))
                        norm.tensor_sum(var_psum, sq, half).then_inc(varied.next(), 1)

                pe.wait_ge(a_made.sem, a_made.at(1, i))
                normalise(0)
                for n in range(2 * J):
                    j, half = n // 2, n % 2
                    if half == 0 and j == 0:
                        pe.wait_ge(f_made.sem, f_made.at(CT, i))
                    if half == 1 and j == 0:
                        pe.wait_ge(f_made.sem, f_made.at(2 * CT, i))
                    if n >= 2:
                        pe.wait_ge(products.sem, products.at(2 * (n - 1), i))
                    for part in range(2):
                        for t in range(CT):
                            ins = nc.tensor.matmul(psum[0:Q, 2 * (n % 2) + part, :], b_w[:, t, part, j, :],
                                                   f[:, t, cols(half)], start=(t == 0), stop=(t == CT - 1))
                    ins.then_inc(u_product.next(), 1)
                for n in range(2 * CT):
                    m, half = n // 2, n % 2
                    if n < 2:
                        pe.wait_ge(sums.sem, sums.at(4 * J + 4 * (J - 1) + 2 * (half + 1), i))
                    if n >= 4:
                        pe.wait_ge(y_plain.sem, y_plain.at(n - 3, i))
                    k = 0
                    for part in range(2):
                        for j in range(J):
                            ins = nc.tensor.matmul(psum[:, n % 4, :], c_w[:, part, j, m * P:(m + 1) * P],
                                                   u[:, part, j, cols(half)], start=(k == 0), stop=(k == 2 * J - 1))
                            k += 1
                    ins.then_inc(y_product.next(), 1)
                pe.wait_ge(a_made.sem, a_made.at(1 + 2 * CT, i))
                normalise(2)
                for n in range(2 * CT):
                    m, half = n // 2, n % 2
                    if n == 0:
                        pe.wait_ge(f_made.sem, f_made.at(4 * CT, i))
                    if n >= 2:
                        pe.wait_ge(hid_made.sem, hid_made.at(n - 1, i))
                    for k, first in enumerate((C, 0)):
                        for t in range(CT):
                            ins = nc.tensor.matmul(psum[:, 2 * (n % 2) + k, :], enc_w[:, t, first + m * P:first + (m + 1) * P],
                                                   f[:, t, cols(half)], start=(t == 0), stop=(t == CT - 1))
                        ins.then_inc(hidden.next(), 1)
                pe.wait_ge(hid_made.sem, hid_made.at(2 * CT, i))
                for n in range(2 * CT):
                    m, half = n // 2, n % 2
                    if n >= 4:
                        pe.wait_ge(out_made.sem, out_made.at(n - 3, i))
                    for t in range(CT):
                        ins = nc.tensor.matmul(psum[:, n % 4, :], dec_w[:, t, m * P:(m + 1) * P], sq[:, t, cols(half)],
                                               start=(t == 0), stop=(t == CT - 1))
                    ins.then_inc(decoded.next(), 1)
                pe.wait_ge(out_made.sem, out_made.at(2 * CT, i))
            for s in (gn_groups, averaged, varied, u_product, y_product, hidden, decoded):
                s.end_of_pass()


def depthwise_layer(nc, const, x_in, x_out, w):
    S = 32
    TAPS = 7
    PAD = 2 * S - 1
    mid = S - 1 - TAPS // 2
    GROUP = 8
    N = B * S
    with ExitStack() as ctx:
        def sb(name, shape, dt=F32):
            return ctx.enter_context(nc.sbuf_tensor(name, shape, dt))

        def signal(name, per=None, head=0):
            return Signal(ctx.enter_context(nc.semaphore(name)), per, head)

        both = sb("both2", [P, B, 2])
        moments = sb("moments2", [P, B, 2])
        var, rstd, shift = (sb(n + "2", [P, B]) for n in ("var", "rstd", "shift"))
        stats = sb("stats2", [P, 6, 6])
        taps = {n: sb(n + "_c", [P, CT, w[n].shape[2], w[n].shape[3]]) for n in ("w77", "w53", "w35", "w7w", "w7h", "w5w", "w5h")}
        biases = {n: sb(n + "_c", [P, CT]) for n in ("b77", "b53", "b35")}
        padded = sb("padded", [P, CT, TAPS, PAD])
        padded_dram = nc.dram_tensor("padded_dram", [CT, P, TAPS, PAD], F32).ap()
        bias = sb("bias2", [P, CT])
        bands = sb("bands", [P, 2, GROUP, TAPS, P])
        psum = ctx.enter_context(nc.psum_tensor("psum2", [P, 4, 2, N], F32))

        with nc.sbuf_tensor("x_pair", [P, 2, CT * T], F32) as x_pair, ExitStack() as inner:
            sem = lambda n: inner.enter_context(nc.semaphore(n))
            loaded = [sem("stat_loaded0"), sem("stat_loaded1")]
            small_loaded, tap_written = sem("small_loaded"), sem("tap_written")
            read, v = Signal(sem("stat_read")), Signal(sem("stat_v"))
            grouped, var_made, rstd_made, tap_made = (Signal(sem(n)) for n in ("grouped2", "var_made2", "rstd_made2", "tap_made"))
            act_step = Signal(sem("act_step2"))
            zeroed = Signal(sem("zeroed2"))
            block = inner.enter_context(nc.Block())

            @block.sync
            def _(sp):
                for n in range(B):
                    if n >= 2:
                        sp.wait_ge(read.sem, read.at(n - 1))
                    sp.dma_start(x_pair[:, n % 2, :], x_in[n].rearrange("(p t) n -> p (t n)", t=CT)).then_inc(loaded[n % 2], 16)
                sp.wait_ge(tap_made.sem, tap_made.at(1))
                sp.dma_start(padded_dram.rearrange("t p a b -> p t (a b)"),
                             padded[:, :, :, :].rearrange("p t a b -> p t (a b)")).then_inc(tap_written, 16)
                sp.wait_ge(tap_written, 16)

            @block.scalar
            def _(act):
                for n, tile in taps.items():
                    act.dma_start(tile[:, :, :, :].rearrange("p t a b -> p (t a b)"),
                                  w[n].rearrange("(p t) e a b -> p (t e a b)", t=CT)).then_inc(small_loaded, 16)
                for n, tile in biases.items():
                    act.dma_start(tile[:, :], w[n].rearrange("(p t) -> p t", t=CT)).then_inc(small_loaded, 16)
                act.wait_ge(small_loaded, 16 * 10)
                act.wait_ge(var_made.sem, var_made.at(1))
                nc.scalar.activation(rstd[:, :], var[:, :], ACT.Ln).then_inc(act_step.next(), 1)
                act.wait_ge(act_step.sem, act_step.at(act_step.count))
                nc.scalar.activation(rstd[:, :], rstd[:, :], ACT.Exp, scale=-0.5).then_inc(rstd_made.next(), 1)

            @block.gpsimd
            def _(pool):
                pool.memset(bands[:, :, :, :, :], 0.0).then_inc(zeroed.next(), 1)

            @block.tensor
            def _(pe):
                pe.wait_ge(read.sem, read.at(B))
                nc.tensor.matmul(psum[:, 0, 0, 0:2 * B], const["group_mean"],
                                                   both[:, :, :].rearrange("p b e -> p (b e)"), start=True, stop=True).then_inc(grouped.next(), 1)

            @block.vector
            def _(dve):
                V = nc.vector
                V.memset(padded[:, :, :, :], 0.0).then_inc(v.next(), 1)
                dve.wait_ge(v.sem, v.at(v.count))
                dve.wait_ge(small_loaded, 16 * 10)
                V.tensor_tensor(bias[:, :], biases["b77"][:, :], biases["b53"][:, :], ALU.add).then_inc(v.next(), 1)
                dve.wait_ge(v.sem, v.at(v.count))
                V.tensor_tensor(bias[:, :], bias[:, :], biases["b35"][:, :], ALU.add).then_inc(v.next(), 1)
                dve.wait_ge(v.sem, v.at(v.count))
                V.tensor_copy(padded[:, :, :, mid:mid + 7], taps["w77"][:, :, :, :]).then_inc(v.next(), 1)
                dve.wait_ge(v.sem, v.at(v.count))
                for n, rows, columns in (("w53", 5, 3), ("w35", 3, 5)):
                    at = padded[:, :, 3 - rows // 2:4 + rows // 2, mid + 3 - columns // 2:mid + 4 + columns // 2]
                    V.tensor_tensor(at, at, taps[n][:, :, :, :], ALU.add).then_inc(v.next(), 1)
                    dve.wait_ge(v.sem, v.at(v.count))
                for down, across, size in (("w7h", "w7w", 7), ("w5h", "w5w", 5)):
                    for t in range(CT):
                        for r in range(size):
                            at = padded[:, t, 3 - size // 2 + r, mid + 3 - size // 2:mid + 4 + size // 2]
                            V.scalar_tensor_tensor(at, taps[across][:, t, 0, :], taps[down][:, t, r, :], at,
                                                               ALU.mult, ALU.add).then_inc(v.next(), 1)
                    dve.wait_ge(v.sem, v.at(v.count))
                V.tensor_copy(padded[:, :, :, 0:1], padded[:, :, :, 0:1]).then_inc(tap_made.next(), 1)
                for n in range(B):
                    dve.wait_ge(loaded[n % 2], 16 * (n // 2 + 1))
                    for c in range(6):
                        V.bn_stats(stats[:, c, :], x_pair[:, n % 2, c * HALF:(c + 1) * HALF]).then_inc(v.next(), 1)
                    dve.wait_ge(v.sem, v.at(v.count))
                    V.bn_aggr(both[:, n, :], stats[:, :, :].rearrange("p a b -> p (a b)")).then_inc(v.next(), 1)
                    dve.wait_ge(v.sem, v.at(v.count))
                    V.scalar_tensor_tensor(both[:, n, 1:2], both[:, n, 0:1], both[:, n, 0:1],
                                                          both[:, n, 1:2], ALU.mult, ALU.add).then_inc(read.next(), 1)
                dve.wait_ge(grouped.sem, grouped.at(1))
                V.tensor_copy(moments[:, :, :].rearrange("p b e -> p (b e)"), psum[:, 0, 0, 0:2 * B]).then_inc(v.next(), 1)
                dve.wait_ge(v.sem, v.at(v.count))
                V.tensor_tensor(var[:, :], moments[:, :, 0], moments[:, :, 0], ALU.mult).then_inc(v.next(), 1)
                dve.wait_ge(v.sem, v.at(v.count))
                V.scalar_tensor_tensor(var[:, :], moments[:, :, 1], GN_EPS, var[:, :], ALU.add, ALU.subtract).then_inc(var_made.next(), 1)
                dve.wait_ge(rstd_made.sem, rstd_made.at(1))
                V.scalar_tensor_tensor(shift[:, :], moments[:, :, 0], -1.0, rstd[:, :], ALU.mult, ALU.mult).then_inc(v.next(), 1)
                dve.wait_ge(v.sem, v.at(v.count))

        xb = sb("xb", [P, B, T])
        xt = sb("xt", [P, S, B, S])
        yt = sb("yt", [P, S, B, S])
        xn = sb("xn2", [P, 2, T])
        yb = sb("yb", [P, 2, T])
        bias_t = sb("bias_t", [P, 1])
        GROUPS_T = S // GROUP
        x_loaded, stored = (ctx.enter_context(nc.semaphore(n)) for n in ("x_loaded2", "stored2"))
        band_loaded = [ctx.enter_context(nc.semaphore(f"band_loaded{n}")) for n in range(2)]
        normed = signal("normed", B)
        turned = signal("turned", B)
        PAIRS = GROUP // 2
        convolved = signal("convolved", S // 2, head=2 * PAIRS)
        kept = signal("kept2", S // 2)
        back = signal("back2", B)
        out_made = signal("out_made2", B)
        block = ctx.enter_context(nc.Block())

        @block.sync
        def _(sp):
            sp.sem_inc(stored, 16)
            with sp.Fori(0, CT) as t:
                sp.wait_ge(stored, t * 16 + 16)
                sp.dma_start(xb[:, :, :], x_in.rearrange("b (p t) n -> t p b n", t=CT)[bass.ds(t, 1)].rearrange("a p b n -> p (a b) n")).then_inc(x_loaded, 16)
                sp.wait_ge(out_made.sem, out_made.at(B, t))
                sp.dma_start(x_out.rearrange("b (p t) n -> t p b n", t=CT)[bass.ds(t, 1)].rearrange("a p b n -> p (a b) n"), xb[:, :, :]).then_inc(stored, 16)
            sp.wait_ge(stored, 16 * CT + 16)

        @block.gpsimd
        def _(pool):
            pool.sem_inc(convolved.sem, convolved.head)
            with pool.Fori(0, CT) as t:
                for g in range(GROUPS_T):
                    pool.wait_ge(convolved.sem, convolved.at((g - 1) * PAIRS, t))
                    for q in range(4):
                        target = bands[q * S:(q + 1) * S, g % 2, :, :, q * S:(q + 1) * S].rearrange("p a b c -> p (a b) c")
                        row = padded_dram[bass.ds(t, 1), q * S + g * GROUP:q * S + (g + 1) * GROUP, :, 0:S]
                        row = row.rearrange("e c a b -> (e c a) b")
                        source = bass.AP(tensor=row.tensor, offset=row.offset, ap=[[1, S], *row.ap])
                        pool.dma_start(target, source).then_inc(band_loaded[g % 2], 16)
            for s in band_loaded:
                pool.wait_ge(s, CT * GROUPS_T // 2 * 4 * 16)

        @block.scalar
        def _(act):
            with act.Fori(0, CT) as t:
                act.wait_ge(x_loaded, t * 16 + 16)
                for b in range(B):
                    if b >= 2:
                        act.wait_ge(turned.sem, turned.at(b - 1, t))
                    nc.scalar.activation(xn[:, b % 2, :], xb[:, b, :], ACT.Identity,
                                                          scale=rstd[:, b:b + 1], bias=shift[:, b:b + 1]).then_inc(normed.next(), 1)
                for n in range(S // 2):
                    act.wait_ge(convolved.sem, convolved.at(n + 1, t))
                    nc.scalar.copy(yt[:, 2 * n:2 * n + 2, :, :].rearrange("p c b h -> p (c b h)"),
                                                  psum[:, n % 4, :, :].rearrange("p c n -> p (c n)")).then_inc(kept.next(), 1)
            for s in (normed, kept):
                s.end_of_pass()

        @block.vector
        def _(dve):
            with dve.Fori(0, CT) as t:
                dve.wait_ge(convolved.sem, convolved.at(0, t))
                for b in range(B):
                    dve.wait_ge(normed.sem, normed.at(b + 1, t))
                    nc.vector.transpose(xt[:, :, b, :].rearrange("p j h -> p h j"),
                                                         xn[:, b % 2, :].rearrange("p (h j) -> p h j", j=S)).then_inc(turned.next(), 1)
                dve.wait_ge(kept.sem, kept.at(S // 2, t))
                for b in range(B):
                    nc.vector.transpose(yb[:, b % 2, :].rearrange("p (h j) -> p h j", j=S),
                                                       yt[:, :, b, :].rearrange("p j h -> p h j")).then_inc(back.next(), 1)
                    dve.wait_ge(back.sem, back.at(back.count, t))
                    at = xb[:, b, :].rearrange("p (h j) -> p h j", j=S)
                    nc.vector.scalar_tensor_tensor(
                        at, yb[:, b % 2, :].rearrange("p (h j) -> p h j", j=S)[:, :, ::-1], bias[:, bass.ds(t, 1)], at,
                        ALU.add, ALU.add).then_inc(out_made.next(), 1)
            for s in (turned, back, out_made):
                s.end_of_pass()

        @block.tensor
        def _(pe):
            with pe.Fori(0, CT) as t:
                pe.wait_ge(turned.sem, turned.at(B, t))
                for n in range(S // 2):
                    g = 2 * n // GROUP
                    if n % PAIRS == 0:
                        pe.wait_ge(band_loaded[g % 2], t * (GROUPS_T // 2 * 64) + (g // 2 + 1) * 64)
                    if n >= 4:
                        pe.wait_ge(kept.sem, kept.at(n - 3, t))
                    for c in range(2):
                        channel = 2 * n + c
                        out = psum[:, n % 4, c, :].rearrange("p (b h) -> p b h", h=S)
                        for k, tap in enumerate((3, 0, 1, 2, 4, 5, 6)):
                            down = tap - TAPS // 2
                            rows = slice(max(0, -down), S - max(0, down))
                            ins = nc.tensor.matmul(out[:, :, rows], bands[:, g % 2, channel % GROUP, tap, :],
                                                   xt[:, channel, :, rows.start + down:rows.stop + down],
                                                   start=(k == 0), stop=(k == TAPS - 1))
                    ins.then_inc(convolved.next(), 1)
                pe.wait_ge(kept.sem, kept.at(S // 2, t))
            convolved.end_of_pass()


def rwkv_layer(nc, const, x_in, x_out, w):
    S, CAP, LN_EPS, NEG = 32, 40.0, 1e-5, -1e38
    with ExitStack() as ctx:
        def sb(name, shape, dt=F32):
            return ctx.enter_context(nc.sbuf_tensor(name, shape, dt))

        def signal(name, per=None, head=0):
            return Signal(ctx.enter_context(nc.semaphore(name)), per, head)

        lin_w = {n: sb(n + "_t", [P, CT, C]) for n in ("Wk", "Wv", "Wr", "Wo")}
        conv_w = sb("conv_t", [P, CT, 9, C])
        names = ("ln_g", "ln_b", "w_param", "u", "bn_g", "bn_b", "gamma_g", "gamma_s")
        cols = {n: sb(n + "_3", [P, CT]) for n in names}
        decay = sb("decay3", [P, CT])
        cap = sb("cap3", [P, CT])
        bn_scale = sb("bn_scale", [P, CT])
        eps = sb("eps3", [P, 1])
        with nc.sbuf_tensor("conv_rows", [P, CT, C * 9], F32) as conv_rows, \
                nc.sbuf_tensor("lin_rows", [P, 4, CT, C], F32) as lin_rows:
            pieces, loads = [], [(conv_rows[:, :, :], w["conv_w"].rearrange("(p m) c a b -> p m (c a b)", m=CT))]
            for n, name in enumerate(lin_w):
                loads.append((lin_rows[:, n, :, :], w[name].rearrange("(p m) c -> p m c", m=CT)))
                for t in range(CT):
                    pieces.append(([lin_rows[:, n, m, t::CT] for m in range(CT)], lin_w[name][:, t, :]))
            for name in names:
                source = w[name] if len(w[name].shape) == 1 else w[name].rearrange("a c b d -> (a c b d)")
                loads.append((cols[name][:, :], source.rearrange("(p t) -> p t", t=CT)))
            for tap in range(9):
                for t in range(CT):
                    first = t * 9 + tap
                    pieces.append(([conv_rows[:, m, first:C * 9:CT * 9] for m in range(CT)], conv_w[:, t, tap, :]))
            turn_weights(nc, "w3", const["ident"], pieces, loads)
        with nc.semaphore("decay_made") as decay_made, nc.Block() as block:
            @block.scalar
            def _(act):
                nc.scalar.activation(decay[:, :], cols["w_param"][:, :], ACT.Exp).then_inc(decay_made, 1)

            @block.vector
            def _(dve):
                nc.vector.memset(eps[:, :], LN_EPS)
                nc.vector.tensor_scalar(cap[:, :], cols["u"][:, :], -1.0, CAP, ALU.mult, ALU.add)
                nc.vector.tensor_scalar(bn_scale[:, :], cols["bn_g"][:, :], 1.0 / np.sqrt(1.0 + 1e-5), None, ALU.mult)
                dve.wait_ge(decay_made, 1)
                nc.vector.tensor_scalar(decay[:, :], decay[:, :], -1.0, None, ALU.mult)

        gn = GroupNorm(nc, sb, ctx.enter_context(nc.semaphore("gn3_turn")), "gn3")
        xin = sb("xin3", [P, CT * T])
        xres = sb("xres3", [P, CT, T])
        xp = sb("xp", [P, CT, S + 2, S + 2])
        k = sb("k3", [P, CT, T])
        v = sb("v3", [P, CT, T])
        h = sb("h3", [P, CT, T])
        p = sb("p3", [P, T + 2])
        to_a = sb("to_a", [P, 2, T])
        to_f = sb("to_f", [P, 2, T])
        to_e = sb("to_e", [P, 2, T])
        kv = sb("kv3", [P, T])
        num = sb("num3", [P, T + 2])
        den = sb("den3", [P, T + 2])
        ev = sb("ev3", [P, T])
        side = sb("side3", [P, 2, HALF])
        psum = ctx.enter_context(nc.psum_tensor("psum3", [P, 4, HALF], F32))
        mean_psum = ctx.enter_context(nc.psum_tensor("mean3", [P, 2, HALF], F32))
        var_psum = ctx.enter_context(nc.psum_tensor("var3", [P, 2, HALF], F32))
        norm = ChannelNorm(nc, sb, "ln3", mean_psum, var_psum, const["col_mean"], eps[:, :])

        ITEMS = 2 * CT
        LOW, KV, CONV, GATE = 2 * CT, 4 * CT, 6 * CT, 8 * CT
        x_loaded, res_loaded, stored = (ctx.enter_context(nc.semaphore(n)) for n in ("x_loaded3", "res_loaded3", "stored3"))
        xin_free = signal("xin_free3")
        framed = signal("framed")
        step = signal("step3", 10 + 2)
        act_step = signal("act_step3", 1 + 2 + ITEMS)
        gn_moments, gn_groups, gn_var, gn_rstd, xp_made = (signal(n + "3", 1) for n in ("gn_moments", "gn_groups", "gn_var", "gn_rstd", "xp_made"))
        product = signal("product3", GATE)
        emptied = signal("emptied3", GATE)
        max_made = signal("max_made", ITEMS)
        fall = signal("fall", ITEMS)
        rise = signal("rise", ITEMS)
        jump = signal("jump", ITEMS)
        jump_capped = signal("jump_capped", ITEMS)
        a_exped = signal("a_exped", ITEMS)
        f_exped = signal("f_exped", ITEMS)
        e_exped = signal("e_exped", ITEMS)
        kv_made = signal("kv_made", ITEMS)
        ev_made = signal("ev_made", ITEMS)
        num_made = signal("num_made", ITEMS)
        den_made = signal("den_made", ITEMS)
        num_out = signal("num_out", ITEMS)
        den_out = signal("den_out", ITEMS)
        den_inv = signal("den_inv", ITEMS)
        h_made = signal("h_made", ITEMS + 2 * CT)
        side_used = signal("side_used", 2 * CT)
        quot = signal("quot", CT)
        leaked = signal("leaked", 2 * CT)
        averaged, centred, squared, varied, inv_made = (signal(n + "3", 2) for n in ("averaged", "centred", "squared", "varied", "inv_made"))
        hn_made = signal("hn_made", 2 * CT)
        mixed = signal("mixed", 2 * CT)
        out_made = signal("out_made3", 2 * CT)

        def half_of(ap, half):
            return ap[:, :, half * HALF:(half + 1) * HALF] if len(ap.shape) == 3 else ap[:, half * HALF:(half + 1) * HALF]

        def way(ap, backwards):
            return ap[:, ::-1] if backwards else ap

        def now(ap):
            return ap[:, 1:T + 1]

        def before(ap, backwards):
            return ap[:, 2:T + 2] if backwards else ap[:, 0:T]

        def rows_of(t, half, down, across):
            top = 1 + half * S // 2 + down
            return xp[:, t, top:top + S // 2, 1 + across:1 + across + S]

        block = ctx.enter_context(nc.Block())

        @block.sync
        def _(sp):
            sp.sem_inc(stored, 16)
            sp.dma_start(xin[:, :], x_in[0:1].rearrange("a (p t) n -> p (a t n)", t=CT)).then_inc(x_loaded, 16)
            with sp.Fori(0, B) as i:
                sp.wait_ge(stored, i * 16 + 16)
                sp.dma_start(xres[:, :, :].rearrange("p t n -> p (t n)"), x_in[bass.ds(i, 1)].rearrange("a (p t) n -> p (a t n)", t=CT)).then_inc(res_loaded, 16)
                sp.wait_ge(xin_free.sem, i + 1)
                sp.dma_start(xin[:, :], x_in[bass.ds((i + 1) % B, 1)].rearrange("a (p t) n -> p (a t n)", t=CT)).then_inc(x_loaded, 16)
                sp.wait_ge(out_made.sem, out_made.at(2 * CT, i))
                sp.dma_start(x_out[bass.ds(i, 1)].rearrange("a (p t) n -> p (a t n)", t=CT), xres[:, :, :].rearrange("p t n -> p (t n)")).then_inc(stored, 16)
            sp.wait_ge(stored, 16 * B + 16)
            sp.wait_ge(x_loaded, 16 * B + 16)

        @block.gpsimd
        def _(pool):
            pool.memset(xp[:, :, :, :], 0.0).then_inc(framed.next(), 1)
            for tile, value in ((p, NEG), (num, 0.0), (den, 0.0)):
                pool.memset(tile[:, 0:1], value).then_inc(framed.next(), 1)
                pool.memset(tile[:, T + 1:T + 2], value).then_inc(framed.next(), 1)
            with pool.Fori(0, B) as i:
                for n in range(ITEMS):
                    t, backwards = n // 2, n % 2
                    pool.wait_ge(max_made.sem, max_made.at(n + 1, i))
                    pool.tensor_tensor(to_a[:, n % 2, :], k[:, t, :], now(p), ALU.subtract).then_inc(rise.next(), 1)
                    pool.tensor_tensor(to_e[:, n % 2, :], k[:, t, :], before(p, backwards), ALU.subtract).then_inc(jump.next(), 1)
                    pool.wait_ge(jump.sem, jump.at(jump.count, i))
                    pool.sem_inc(gn.turn, 1)
                    pool.tensor_scalar(to_e[:, n % 2, :], to_e[:, n % 2, :], cap[:, t:t + 1], None, ALU.min).then_inc(jump_capped.next(), 1)
                    pool.wait_ge(ev_made.sem, ev_made.at(n + 1, i))
                    pool.wait_ge(den_made.sem, den_made.at(n + 1, i))
                    pool.tensor_tensor(to_e[:, n % 2, :], to_e[:, n % 2, :], before(den, backwards), ALU.add).then_inc(den_out.next(), 1)
            for s in (rise, jump, jump_capped, den_out):
                s.end_of_pass()

        @block.scalar
        def _(act):
            with act.Fori(0, B) as i:
                act.wait_ge(gn_var.sem, gn_var.at(1, i))
                gn.scalar_rstd(act, act_step, i, gn_rstd)
                for n in range(KV):
                    act.wait_ge(product.sem, product.at(n + 1, i))
                    target = half_of((k if n < LOW else v)[:, (n % LOW) // 2, :], n % 2)
                    nc.scalar.copy(target, psum[:, n % 4, :]).then_inc(emptied.next(), 1)

                def leaky(n):
                    m = n // 2
                    if n >= 2:
                        act.wait_ge(side_used.sem, side_used.at(n - 1, i))
                    act.wait_ge(product.sem, product.at(KV + n + 1, i))
                    nc.scalar.activation(side[:, n % 2, :], psum[:, (KV + n) % 4, :], ACT.Identity,
                                                           scale=bn_scale[:, m:m + 1], bias=cols["bn_b"][:, m:m + 1]).then_inc(emptied.next(), 1)

                def exps(n):
                    t = n // 2
                    act.wait_ge(rise.sem, rise.at(n + 1, i))
                    nc.scalar.activation(to_a[:, n % 2, :], to_a[:, n % 2, :], ACT.Exp).then_inc(a_exped.next(), 1)
                    act.wait_ge(fall.sem, fall.at(n + 1, i))
                    nc.scalar.activation(to_f[:, n % 2, :], to_f[:, n % 2, :], ACT.Exp, bias=decay[:, t:t + 1]).then_inc(f_exped.next(), 1)
                    act.wait_ge(jump_capped.sem, jump_capped.at(n + 1, i))
                    nc.scalar.activation(to_e[:, n % 2, :], to_e[:, n % 2, :], ACT.Exp, bias=cols["u"][:, t:t + 1]).then_inc(e_exped.next(), 1)

                def inverse(n):
                    at = to_e[:, n % 2, :]
                    act.wait_ge(den_out.sem, den_out.at(n + 1, i))
                    nc.scalar.activation(at, at, ACT.Ln).then_inc(act_step.next(), 1)
                    act.wait_ge(act_step.sem, act_step.at(act_step.count, i))
                    nc.scalar.activation(at, at, ACT.Exp, scale=-1.0).then_inc(den_inv.next(), 1)

                for n in range(ITEMS + 1):
                    if n < ITEMS:
                        exps(n)
                    if n > 0:
                        inverse(n - 1)
                    if n in (3, 5):
                        leaky(n // 2 - 1)
                for n in range(2, 2 * CT):
                    leaky(n)
                for n in range(2 * CT):
                    if n < 2:
                        act.wait_ge(side_used.sem, side_used.at(2 * CT - 1 + n, i))
                    else:
                        act.wait_ge(h_made.sem, h_made.at(ITEMS + n - 1, i))
                    act.wait_ge(product.sem, product.at(CONV + n + 1, i))
                    nc.scalar.activation(side[:, n % 2, :], psum[:, (CONV + n) % 4, :], ACT.Sigmoid).then_inc(emptied.next(), 1)
                for half in range(2):
                    act.wait_ge(centred.sem, centred.at(half + 1, i))
                    norm.scalar_square(v, h, half).then_inc(squared.next(), 1)
                for half in range(2):
                    act.wait_ge(varied.sem, varied.at(half + 1, i))
                    norm.scalar_inverse(act, half, act_step, i, inv_made)
            for s in (act_step, gn_rstd, emptied, a_exped, f_exped, e_exped, den_inv, squared, inv_made):
                s.end_of_pass()

        @block.vector
        def _(dve):
            dve.wait_ge(framed.sem, framed.at(7))
            with dve.Fori(0, B) as i:
                dve.wait_ge(x_loaded, i * 16 + 16)
                gn.vector_moments(dve, xin[:, :], step, i, gn_moments)
                dve.wait_ge(gn_groups.sem, gn_groups.at(1, i))
                gn.vector_variance(dve, psum[:, 0, 0:2], step, i, gn_var)
                dve.wait_ge(gn_rstd.sem, gn_rstd.at(1, i))
                gn.vector_shift(dve, step, i)
                for t in range(CT):
                    ins = nc.vector.tensor_scalar(xp[:, t, 1:S + 1, 1:S + 1], xin[:, t * T:(t + 1) * T].rearrange("p (a b) -> p a b", b=S),
                                                  gn.rstd[:, :], gn.shift[:, :], ALU.mult, ALU.add)
                ins.then_inc(xp_made.next(), 1)
                dve.wait_ge(xp_made.sem, xp_made.at(1, i))
                dve.sem_inc(xin_free.sem, 1)

                def maxima(n):
                    t, backwards = n // 2, n % 2
                    if backwards == 0:
                        dve.wait_ge(emptied.sem, emptied.at(2 * (t + 1), i))
                    if n > 0:
                        dve.wait_ge(jump.sem, jump.at(n, i))
                        dve.wait_ge(fall.sem, fall.at(n, i))
                    if n > 1:
                        dve.wait_ge(kv_made.sem, kv_made.at(n - 1, i))
                    nc.vector.tensor_tensor_scan(
                        way(now(p), backwards), decay[:, t:t + 1].broadcast_to([P, T]), way(k[:, t, :], backwards),
                        NEG, ALU.add, ALU.max).then_inc(max_made.next(), 1)
                    dve.wait_ge(max_made.sem, max_made.at(max_made.count, i))
                    nc.vector.tensor_tensor(to_f[:, n % 2, :], before(p, backwards), now(p), ALU.subtract).then_inc(fall.next(), 1)

                def scans(n):
                    t, backwards = n // 2, n % 2
                    dve.wait_ge(a_exped.sem, a_exped.at(n + 1, i))
                    if backwards == 0:
                        dve.wait_ge(emptied.sem, emptied.at(LOW + 2 * (t + 1), i))
                    nc.vector.tensor_tensor(kv[:, :], to_a[:, n % 2, :], v[:, t, :], ALU.mult).then_inc(kv_made.next(), 1)
                    dve.wait_ge(kv_made.sem, kv_made.at(kv_made.count, i))
                    dve.wait_ge(f_exped.sem, f_exped.at(n + 1, i))
                    if n > 0:
                        dve.wait_ge(num_out.sem, num_out.at(n, i))
                        dve.wait_ge(den_out.sem, den_out.at(n, i))
                    nc.vector.tensor_tensor_scan(
                        way(now(num), backwards), way(to_f[:, n % 2, :], backwards), way(kv[:, :], backwards), 0.0, ALU.mult, ALU.add).then_inc(num_made.next(), 1)
                    nc.vector.tensor_tensor_scan(
                        way(now(den), backwards), way(to_f[:, n % 2, :], backwards), way(to_a[:, n % 2, :], backwards), 0.0, ALU.mult, ALU.add).then_inc(den_made.next(), 1)
                    dve.wait_ge(e_exped.sem, e_exped.at(n + 1, i))
                    nc.vector.tensor_tensor(ev[:, :], to_e[:, n % 2, :], v[:, t, :], ALU.mult).then_inc(ev_made.next(), 1)
                    dve.wait_ge(ev_made.sem, ev_made.at(ev_made.count, i))
                    nc.vector.tensor_tensor(ev[:, :], ev[:, :], before(num, backwards), ALU.add).then_inc(num_out.next(), 1)

                def quotient(n):
                    t, backwards = n // 2, n % 2
                    dve.wait_ge(den_inv.sem, den_inv.at(n + 1, i))
                    dve.wait_ge(num_out.sem, num_out.at(n + 1, i))
                    at = h[:, t, :]
                    if backwards == 0:
                        nc.vector.tensor_tensor(at, ev[:, :], to_e[:, n % 2, :], ALU.mult).then_inc(h_made.next(), 1)
                    else:
                        nc.vector.tensor_tensor(ev[:, :], ev[:, :], to_e[:, n % 2, :], ALU.mult).then_inc(quot.next(), 1)
                        dve.wait_ge(quot.sem, quot.at(quot.count, i))
                        dve.wait_ge(h_made.sem, h_made.at(n, i))
                        nc.vector.tensor_tensor(at, at, ev[:, :], ALU.add).then_inc(h_made.next(), 1)

                def add_side(n):
                    m = n // 2
                    if n == 0:
                        dve.wait_ge(res_loaded, i * 16 + 16)
                    dve.wait_ge(emptied.sem, emptied.at(KV + n + 1, i))
                    at = half_of(xres[:, m, :], n % 2)
                    nc.vector.scalar_tensor_tensor(side[:, n % 2, :], side[:, n % 2, :], 0.01, side[:, n % 2, :],
                                                                    ALU.mult, ALU.max).then_inc(leaked.next(), 1)
                    dve.wait_ge(leaked.sem, leaked.at(leaked.count, i))
                    nc.vector.scalar_tensor_tensor(at, side[:, n % 2, :], cols["gamma_s"][:, m:m + 1], at,
                                                                       ALU.mult, ALU.add).then_inc(side_used.next(), 1)

                maxima(0)
                for n in range(ITEMS):
                    if n + 1 < ITEMS:
                        maxima(n + 1)
                    scans(n)
                    quotient(n)
                    if n in (4, 5):
                        add_side(n - 4)
                for n in range(2, 2 * CT):
                    add_side(n)
                dve.wait_ge(h_made.sem, h_made.at(ITEMS, i))
                for n in range(2 * CT):
                    at = half_of(h[:, n // 2, :], n % 2)
                    dve.wait_ge(emptied.sem, emptied.at(CONV + n + 1, i))
                    nc.vector.scalar_tensor_tensor(at, side[:, n % 2, :], 0.5, at, ALU.mult, ALU.mult).then_inc(h_made.next(), 1)
                for half in range(2):
                    dve.wait_ge(averaged.sem, averaged.at(half + 1, i))
                    norm.vector_centre(h, half).then_inc(centred.next(), 1)
                for half in range(2):
                    dve.wait_ge(inv_made.sem, inv_made.at(half + 1, i))
                    norm.vector_scale(h, half).then_inc(step.next(), 1)
                    dve.wait_ge(step.sem, step.at(step.count, i))
                    for t in range(CT):
                        at = half_of(h[:, t, :], half)
                        nc.vector.tensor_scalar(at, at, cols["ln_g"][:, t:t + 1], cols["ln_b"][:, t:t + 1],
                                                                  ALU.mult, ALU.add).then_inc(hn_made.next(), 1)
                for n in range(2 * CT):
                    m, half = n // 2, n % 2
                    dve.wait_ge(mixed.sem, mixed.at(n + 1, i))
                    at = half_of(xres[:, m, :], half)
                    nc.vector.scalar_tensor_tensor(at, psum[:, (GATE + n) % 4, :], cols["gamma_g"][:, m:m + 1],
                                                                      at, ALU.mult, ALU.add).then_inc(out_made.next(), 1)
            for s in (step, gn_moments, gn_var, xp_made, max_made, fall, kv_made, num_made, den_made, ev_made, num_out,
                      h_made, quot, leaked, side_used, centred, hn_made, out_made):
                s.end_of_pass()

        @block.tensor
        def _(pe):
            with pe.Fori(0, B) as i:
                pe.wait_ge(gn_moments.sem, gn_moments.at(1, i))
                gn.tensor_groups(pe, psum[:, 0, 0:2], const["group_mean"]).then_inc(gn_groups.next(), 1)
                pe.wait_ge(xp_made.sem, xp_made.at(1, i))

                def project(n, weights, taps):
                    m, half = (n % LOW) // 2, n % 2
                    if n >= 4:
                        pe.wait_ge(emptied.sem, emptied.at(n - 3, i))
                    parts = [(tap, t) for tap in taps for t in range(CT)]
                    for q, (tap, t) in enumerate(parts):
                        ins = nc.tensor.matmul(psum[:, n % 4, :].rearrange("p (a b) -> p a b", b=S), weights(t, tap)[:, m * P:(m + 1) * P],
                                               rows_of(t, half, tap // 3 - 1, tap % 3 - 1),
                                               start=(q == 0), stop=(q == len(parts) - 1))
                    ins.then_inc(product.next(), 1)

                for n in range(KV):
                    project(n, lambda t, tap: lin_w["Wk" if n < LOW else "Wv"][:, t, :], [4])
                for n in range(KV, CONV):
                    project(n, lambda t, tap: conv_w[:, t, tap, :], range(9))
                for n in range(CONV, GATE):
                    project(n, lambda t, tap: lin_w["Wr"][:, t, :], [4])
                for half in range(2):
                    pe.wait_ge(h_made.sem, h_made.at(ITEMS + 2 * CT - 1 + half, i))
                    norm.tensor_sum(mean_psum, h, half).then_inc(averaged.next(), 1)
                for half in range(2):
                    pe.wait_ge(squared.sem, squared.at(half + 1, i))
                    norm.tensor_sum(var_psum, v, half).then_inc(varied.next(), 1)
                pe.wait_ge(emptied.sem, emptied.at(GATE, i))
                for n in range(2 * CT):
                    m, half = n // 2, n % 2
                    if n == 0:
                        pe.wait_ge(hn_made.sem, hn_made.at(CT, i))
                    if n == 1:
                        pe.wait_ge(hn_made.sem, hn_made.at(2 * CT, i))
                    if n >= 4:
                        pe.wait_ge(out_made.sem, out_made.at(n - 3, i))
                    for t in range(CT):
                        ins = nc.tensor.matmul(psum[:, (GATE + n) % 4, :], lin_w["Wo"][:, t, m * P:(m + 1) * P],
                                               half_of(h[:, t, :], half), start=(t == 0), stop=(t == CT - 1))
                    ins.then_inc(mixed.next(), 1)
                pe.wait_ge(out_made.sem, out_made.at(2 * CT, i))
            for s in (gn_groups, product, averaged, varied, mixed):
                s.end_of_pass()


def build(nc, args, x_out):
    with ExitStack() as ctx:
        tiles = {name: ctx.enter_context(nc.sbuf_tensor(name, shape, F32)) for name, shape in
                 (("ident", [P, P]), ("group_mean", [P, P]), ("head_mask", [P, 1]), ("col_mean", [P, P]))}
        const = {name: tile[:, :] for name, tile in tiles.items()}
        make_constants(nc, const["ident"], const["group_mean"], const["head_mask"], const["col_mean"])
        x = args["x"].rearrange("b c h w -> b c (h w)")
        y = x_out.rearrange("b c h w -> b c (h w)")
        x1 = nc.dram_tensor("x1", [B, C, T], F32).ap()
        x2 = nc.dram_tensor("x2", [B, C, T], F32).ap()
        x3 = nc.dram_tensor("x3", [B, C, T], F32).ap()
        attention_layer(nc, const, x, x1, args["L0_conv_w_qkv"], args["L0_conv_w_proj"], args["L0_conv_b_proj"])
        s5_layer(nc, const, x1, x2, {k[8:]: v for k, v in args.items() if k.startswith("L1_conv_")})
        depthwise_layer(nc, const, x2, x3, {k[8:]: v for k, v in args.items() if k.startswith("L2_conv_")})
        rwkv_layer(nc, const, x3, y, {k[8:]: v for k, v in args.items() if k.startswith("L3_conv_")})


def kernel(**inputs):
    import numpy as _np
    import concourse.bacc as _bacc
    from concourse.bass_utils import run_bass_kernel_spmd as _run

    nc = _bacc.Bacc("TRN2", target_bir_lowering=False, num_devices=1)
    arrays, args = {}, {}
    for name, value in inputs.items():
        a = _np.ascontiguousarray(value)
        arrays[f"in_{name}"] = a
        args[name] = nc.dram_tensor(f"in_{name}", a.shape, mybir.dt.from_np(a.dtype), kind="ExternalInput").ap()
    out = nc.dram_tensor("out", inputs["x"].shape, F32, kind="ExternalOutput").ap()
    build(nc, args, out)
    r = _run(nc, [arrays], core_ids=[0])
    return r.results[0]["out"]
```

```python
from contextlib import ExitStack

import numpy as np

import concourse.bass as bass
from concourse import mybir

F32 = mybir.dt.float32
F32R = mybir.dt.float32r
ALU = mybir.AluOpType
ACT = mybir.ActivationFunctionType
AX = mybir.AxisListType

P = 128
HALF = 512
BANKS = 8
GROUPS = 32
GN_EPS = 1e-5


class Signal:

    def __init__(self, sem, per=None, head=0):
        self.sem, self.per, self.head, self.count = sem, per, head, 0

    def next(self):
        self.count += 1
        return self.sem

    def lead(self):
        self.count += self.head
        return self.sem, self.head

    def at(self, nth, i=None):
        assert self.per is None or nth <= self.per
        if i is None:
            return nth
        assert nth + self.head >= 1
        return i * self.per + nth + self.head

    def now(self, i=None):
        return self.count if i is None else i * self.per + self.count

    def end_of_pass(self):
        assert self.per is None or self.count == self.head + self.per, (self.sem, self.count, self.head, self.per)


def as_f32(ap):
    return ap.bitcast(F32)


def turn_weights(nc, name, ident, pieces, loads):
    with ExitStack() as ctx:
        turned_psum = ctx.enter_context(nc.psum_tensor(name + "_turning", [P, 4, HALF], F32))
        loaded = ctx.enter_context(nc.semaphore(name + "_loaded"))
        turned = Signal(ctx.enter_context(nc.semaphore(name + "_turned")))
        kept = [Signal(ctx.enter_context(nc.semaphore(f"{name}_kept{n}"))) for n in range(2)]
        block = ctx.enter_context(nc.Block())

        @block.sync
        def _(sp):
            for tile, source in loads:
                sp.dma_start(tile, source).then_inc(loaded, 16)

        @block.tensor
        def _(pe):
            pe.wait_ge(loaded, 16 * len(loads))
            for n, (blocks, _) in enumerate(pieces):
                if n >= 4:
                    pe.wait_ge(kept[n % 2].sem, kept[n % 2].at((n - 4) // 2 + 1))
                for j, source in enumerate(blocks):
                    rows, cols = source.shape
                    ins = nc.tensor.transpose(turned_psum[0:cols, n % 4, j * rows:(j + 1) * rows], source,
                                              ident[0:rows, 0:rows])
                ins.then_inc(turned.next(), 1)

        def keep(eng, copy, parity):
            for n, (blocks, target) in enumerate(pieces):
                if n % 2 == parity:
                    eng.wait_ge(turned.sem, turned.at(n + 1))
                    rows, cols = blocks[0].shape
                    source = turned_psum[0:cols, n % 4, 0:len(blocks) * rows]
                    if len(target.shape) == 3:
                        source = source.rearrange("p (a b) -> p a b", b=target.shape[2])
                    copy(target, source).then_inc(kept[parity].next(), 1)

        @block.scalar
        def _(act):
            act.wait_ge(loaded, 16 * len(loads))
            keep(act, nc.scalar.copy, 0)

        @block.vector
        def _(dve):
            keep(dve, nc.vector.tensor_copy, 1)


def make_constants(nc, ident, group_mean, head_mask, col_mean):
    with ExitStack() as ctx:
        filled = Signal(ctx.enter_context(nc.semaphore("filled")))
        block = ctx.enter_context(nc.Block())

        @block.gpsimd
        def _(pool):
            pool.memset(ident, 0.0).then_inc(filled.next(), 1)
            pool.memset(group_mean, GROUPS / P).then_inc(filled.next(), 1)
            pool.memset(head_mask, -1.0).then_inc(filled.next(), 1)
            pool.memset(col_mean, 1.0 / (3 * P)).then_inc(filled.next(), 1)
            pool.wait_ge(filled.sem, filled.at(filled.count))
            pool.affine_select(out=ident, in_=ident, compare_op=ALU.not_equal, fill=1.0, base=0,
                                                pattern=[[-1, P]], channel_multiplier=1).then_inc(filled.next(), 1)
            pool.affine_select(out=head_mask, in_=head_mask, compare_op=ALU.is_ge, fill=0.0,
                                                base=-HEAD, pattern=[[0, 1]], channel_multiplier=1).then_inc(filled.next(), 1)
            view = group_mean.rearrange("p (g e) -> p g e", e=4)
            pool.affine_select(out=view, in_=view, compare_op=ALU.is_ge, fill=0.0, base=0,
                                                 pattern=[[-4, GROUPS], [0, 4]], channel_multiplier=1).then_inc(filled.next(), 1)
            pool.wait_ge(filled.sem, filled.at(filled.count))
            pool.affine_select(out=view, in_=view, compare_op=ALU.is_ge, fill=0.0, base=3,
                                                 pattern=[[4, GROUPS], [0, 4]], channel_multiplier=-1).then_inc(filled.next(), 1)
            pool.wait_ge(filled.sem, filled.at(filled.count))


class GroupNorm:

    STEPS = 15

    def __init__(self, nc, sb, turn, name):
        self.nc, self.turn = nc, turn
        self.stats = sb(name + "_stats", [P, 6, 6], F32)
        self.both = sb(name + "_both", [P, 2], F32)
        self.moments = sb(name + "_moments", [P, 2], F32)
        self.var = sb(name + "_var", [P, 1], F32)
        self.log = sb(name + "_log", [P, 1], F32)
        self.rstd = sb(name + "_rstd", [P, 1], F32)
        self.shift = sb(name + "_shift", [P, 1], F32)

    def vector_moments(self, dve, x, step, i, ready):
        nc, both = self.nc, self.both
        chunks = x.shape[1] // HALF
        for n in range(chunks):
            nc.vector.bn_stats(self.stats[:, n, :], x[:, n * HALF:(n + 1) * HALF]).then_inc(step.next(), 1)
        dve.wait_ge(step.sem, step.now(i))
        dve.sem_inc(self.turn, 1)
        nc.vector.bn_aggr(both[:, :], self.stats[:, 0:chunks, :].rearrange("p a b -> p (a b)")).then_inc(step.next(), 1)
        dve.wait_ge(step.sem, step.now(i))
        nc.vector.scalar_tensor_tensor(both[:, 1:2], both[:, 0:1], both[:, 0:1], both[:, 1:2],
                                                       ALU.mult, ALU.add).then_inc(ready.next(), 1)

    def tensor_groups(self, pe, psum, group_mean):
        return self.nc.tensor.matmul(psum, group_mean, self.both[:, :], start=True, stop=True)

    def vector_variance(self, dve, psum, step, i, ready):
        nc, m = self.nc, self.moments
        nc.vector.tensor_copy(m[:, :], psum).then_inc(step.next(), 1)
        dve.wait_ge(step.sem, step.now(i))
        nc.vector.tensor_tensor(self.var[:, :], m[:, 0:1], m[:, 0:1], ALU.mult).then_inc(step.next(), 1)
        dve.wait_ge(step.sem, step.now(i))
        nc.vector.scalar_tensor_tensor(self.var[:, :], m[:, 1:2], GN_EPS, self.var[:, :],
                                                       ALU.add, ALU.subtract).then_inc(ready.next(), 1)

    def scalar_rstd(self, act, step, i, ready):
        self.nc.scalar.activation(self.log[:, :], self.var[:, :], ACT.Ln).then_inc(step.next(), 1)
        act.wait_ge(step.sem, step.now(i))
        self.nc.scalar.activation(self.rstd[:, :], self.log[:, :], ACT.Exp, scale=-0.5).then_inc(ready.next(), 1)

    def vector_shift(self, dve, step, i):
        self.nc.vector.scalar_tensor_tensor(self.shift[:, :], self.moments[:, 0:1], -1.0,
                                                           self.rstd[:, :], ALU.mult, ALU.mult).then_inc(step.next(), 1)
        dve.wait_ge(step.sem, step.now(i))


HEAD = 48
HEADS = 8
B, C, T = 8, 384, 1024
CT = C // P


def attention_layer(nc, const, x_in, x_out, w_qkv, w_proj, b_proj):
    SCALE = HEAD ** -0.5
    KEYS = T // P
    UNITS = 2 * KEYS
    N = HEADS * UNITS
    RING, SLOTS, LAG = 4, 4, 2
    PAIRS = HEADS // 2
    Q_AT, K_AT, ROWS_AT, TURN_AT = 0, 1, 3, 11
    INV_AT = (0, 1, 2, 4, 6, 8, 10, 11)
    with ExitStack() as ctx:
        def sb(name, shape, dt=F32):
            return ctx.enter_context(nc.sbuf_tensor(name, shape, dt))

        def signal(name, per=None, head=0):
            return Signal(ctx.enter_context(nc.semaphore(name)), per, head)

        q_w = sb("q_w", [P, CT, PAIRS, P])
        k_w = sb("k_w", [P, CT, PAIRS, P])
        v_w = sb("v_w", [P, CT, C])
        proj_w = sb("proj_w", [P, PAIRS, C])
        proj_b = sb("proj_b", [P, CT])
        with nc.sbuf_tensor("qk_rows", [P, 2 * PAIRS, C], F32) as qk_rows, \
                nc.sbuf_tensor("v_rows", [P, CT, C], F32) as v_rows, \
                nc.sbuf_tensor("proj_rows", [P, CT, HEADS, 64], F32) as proj_rows:
            with nc.semaphore("pad_zero") as pad_zero, nc.Block() as block:
                @block.vector
                def _(dve):
                    nc.vector.memset(proj_rows[:, :, :, :], 0.0).then_inc(pad_zero, 1)
                    nc.vector.memset(qk_rows[:, :, :], 0.0).then_inc(pad_zero, 1)
                    dve.wait_ge(pad_zero, 2)
            pieces, loads = [], [(v_rows[:, :, :], w_qkv[2 * C:3 * C].rearrange("(r p) c -> p r c", p=P)),
                                 (proj_b[:, :], b_proj.rearrange("(p t) -> p t", t=CT))]
            for which in range(2):
                for odd in range(2):
                    loads.append((qk_rows[64 * odd:64 * odd + HEAD, which * PAIRS:(which + 1) * PAIRS, :],
                                  w_qkv[which * C:(which + 1) * C].rearrange("(j s d) c -> s d j c", s=2, d=HEAD)[odd]))
            for m in range(CT):
                loads.append((proj_rows[:, m, :, 0:HEAD], w_proj.rearrange("(p m) (h d) -> m p h d", m=CT, d=HEAD)[m]))
            for t in range(CT):
                for w, first in ((q_w, 0), (k_w, PAIRS)):
                    pieces.append(([qk_rows[:, first + j, t::CT] for j in range(PAIRS)],
                                   w[:, t, :, :].rearrange("p a b -> p (a b)")))
                pieces.append(([v_rows[:, r, t::CT] for r in range(CT)], v_w[:, t, :]))
            for pair in range(PAIRS):
                pieces.append(([proj_rows[:, m, 2 * pair:2 * pair + 2, :].rearrange("p a b -> p (a b)")
                                for m in range(CT)], proj_w[:, pair, :]))
            turn_weights(nc, "w0", const["ident"], pieces, loads)

        gn = GroupNorm(nc, sb, ctx.enter_context(nc.semaphore("gn0_turn")), "gn0")
        xin = sb("xin", [P, CT * T])
        xres = sb("xres", [P, CT * T])
        xn = sb("xn", [P, CT, T])
        q_all = sb("q_all", [P, SLOTS, T], F32R)
        k_hi = sb("k_hi", [P, SLOTS, T], F32R)
        k_lo = sb("k_lo", [P, SLOTS, T], F32R)
        v = sb("v", [P, KEYS, PAIRS, 3, 64])
        MAX_ROW = 96
        maxima = sb("maxima", [P, MAX_ROW + KEYS], F32R)
        max_row = sb("max_row", [P, T], F32R)
        probs = sb("probs", [P, RING, HALF])
        o_raw = sb("o_raw", [P, T])
        o_inv = sb("o_inv", [P, T])
        heads_out = sb("heads_out", [P, PAIRS, T])
        ident_r = sb("ident_r", [P, P], F32R)

        s_psum = ctx.enter_context(nc.psum_tensor("s_psum", [P, 2, HALF], F32))
        o_psum = ctx.enter_context(nc.psum_tensor("o_psum", [P, 2, HALF], F32))
        m_psum = ctx.enter_context(nc.psum_tensor("m_psum", [P, 4, HALF], F32))

        x_loaded, res_loaded, stored, max_placed = (ctx.enter_context(nc.semaphore(n)) for n in
                                                    ("x_loaded", "res_loaded", "stored", "max_placed"))
        xin_free = signal("xin_free")
        step = signal("step", 10, 10)
        act_step = signal("act_step", 1, 1)
        gn_moments, gn_groups, gn_var, gn_rstd, xn_ready = (signal(n, 1, 1) for n in
                                                            ("gn_moments", "gn_groups", "gn_var", "gn_rstd", "xn_ready"))
        v_made = signal("v_made", KEYS, KEYS)
        v_kept = signal("v_kept", KEYS, KEYS)
        qk_made = signal("qk_made", 2 * PAIRS, 2)
        qk_high = signal("qk_high", 6 * PAIRS, 6)
        qk_low = signal("qk_low", 4 * PAIRS, 4)
        rows_made = signal("rows_made", KEYS * HEADS, KEYS)
        rows_max = signal("rows_max", KEYS * HEADS, KEYS)
        max_turned = signal("max_turned", HEADS, 1)
        max_copied = signal("max_copied", HEADS, 1)
        scored = signal("scored", N, LAG)
        exped = signal("exped", N)
        weighed = signal("weighed", N, RING)
        o_copied = signal("o_copied", 2 * HEADS, 2)
        inverted = signal("inverted", KEYS * HEADS)
        head_done = signal("head_done", HEADS, 1)
        projected = signal("projected", 2 * CT)
        y_made = signal("y_made", 2 * CT, 2 * CT)
        filled = signal("filled")
        turned_ident = signal("turned_ident")

        def slot(n):
            return m_psum[:, 2 * n:2 * n + 2, :].rearrange("p a b -> p (a b)")

        def nth(number, per_one, i):
            return (number - (i is not None)) * per_one

        block = ctx.enter_context(nc.Block())

        @block.sync
        def _(sp):
            sp.sem_inc(stored, 16)

            def place_max(g, i):
                sp.wait_ge(max_copied.sem, max_copied.at(nth(g, 1, i) + 1, i))
                sp.dma_start(as_f32(q_all[HEAD:HEAD + 1, g % SLOTS, :]), as_f32(max_row[MAX_ROW:MAX_ROW + 1, :])).then_inc(max_placed, 16)

            place_max(0, None)
            with sp.Fori(0, B) as i:
                sp.wait_ge(stored, i * 16 + 16)
                sp.dma_start(xres[:, :], x_in[bass.ds(i, 1)].rearrange("a (p t) n -> p (a t n)", t=CT)).then_inc(res_loaded, 16)
                for g in range(1, HEADS + 1):
                    place_max(g, i)
                sp.wait_ge(y_made.sem, y_made.at(2 * CT, i))
                sp.dma_start(x_out[bass.ds(i, 1)].rearrange("a (p t) n -> p (a t n)", t=CT), xres[:, :]).then_inc(stored, 16)
            sp.wait_ge(stored, 16 * B + 16)
            sp.wait_ge(max_placed, 16 * (HEADS * B + 1))

        @block.gpsimd
        def _(pool):
            pool.dma_start(xin[:, :], x_in[0:1].rearrange("a (p t) n -> p (a t n)", t=CT)).then_inc(x_loaded, 16)
            pool.memset(as_f32(k_lo[:, :, :]), 0.0).then_inc(filled.next(), 1)
            pool.memset(as_f32(maxima[:, :]), 0.0).then_inc(filled.next(), 1)
            pool.memset(v[:, :, :, :, :], 1.0).then_inc(filled.next(), 1)
            pool.memset(heads_out[:, :, :], 0.0).then_inc(filled.next(), 1)
            pool.wait_ge(filled.sem, filled.at(4))
            pool.memset(as_f32(k_lo[32:64, :, :]), 1.0).then_inc(filled.next(), 1)
            pool.wait_ge(xin_free.sem, 1)
            pool.dma_start(xin[:, :], x_in[1 % B:1 % B + 1].rearrange("a (p t) n -> p (a t n)", t=CT)).then_inc(x_loaded, 16)
            with pool.Fori(0, B) as i:
                pool.wait_ge(xin_free.sem, i + 2)
                pool.dma_start(xin[:, :], x_in[bass.ds((i + 2) % B, 1)].rearrange("a (p t) n -> p (a t n)", t=CT)).then_inc(x_loaded, 16)
            pool.wait_ge(x_loaded, 16 * (B + 2))

        @block.scalar
        def _(act):
            act.sem_inc(*o_copied.lead())

            def split(pair, part, i):
                at = nth(pair, 1, i)
                if part == 2:
                    act.wait_ge(qk_high.sem, qk_high.at(6 * at + 4, i))
                else:
                    act.wait_ge(qk_made.sem, qk_made.at(2 * at + part + 1, i))
                for odd in range(2):
                    s = (2 * pair + odd) % SLOTS
                    if part == 0:
                        nc.scalar.copy(q_all[0:64, s, :], slot(0)[64 * odd:64 * odd + 64, :]).then_inc(qk_high.next(), 1)
                    elif part == 1:
                        nc.scalar.copy(k_hi[0:64, s, :], slot(1)[64 * odd:64 * odd + 64, :]).then_inc(qk_high.next(), 1)
                    else:
                        nc.scalar.copy(k_hi[64:128, s, :], as_f32(k_hi[0:64, s, :])).then_inc(qk_high.next(), 1)

            def copy_max(g, i):
                at = nth(g, 1, i)
                act.wait_ge(max_turned.sem, max_turned.at(at + 1, i))
                if i is not None:
                    act.wait_ge(max_placed, (i * HEADS + g) * 16)
                nc.scalar.copy(max_row[MAX_ROW:MAX_ROW + 1, :], slot(0)[MAX_ROW:MAX_ROW + 1, :]).then_inc(max_copied.next(), 1)

            def copy_out(h, half, i):
                act.wait_ge(weighed.sem, weighed.at((h + 1) * UNITS - 1 + half, i))
                if half == 0:
                    act.wait_ge(head_done.sem, head_done.at(h, i))
                nc.scalar.copy(o_raw[:, half * HALF:(half + 1) * HALF], o_psum[:, half, :]).then_inc(o_copied.next(), 1)

            def keep_values(i):
                for tile in range(KEYS):
                    act.wait_ge(v_made.sem, v_made.at(tile + 1, i))
                    nc.scalar.copy(v[:, tile, :, 0::2, 0:HEAD], m_psum[:, 2 * (tile % 2), 0:C].rearrange(
                        "p (a b d) -> p a b d", b=2, d=HEAD)).then_inc(v_kept.next(), 1)

            def group_rstd(i):
                act.wait_ge(gn_var.sem, gn_var.at(1, i))
                gn.scalar_rstd(act, act_step, i, gn_rstd)

            nc.scalar.copy(ident_r[:, :], const["ident"]).then_inc(turned_ident.next(), 1)
            group_rstd(None)
            for part in range(3):
                split(0, part, None)
            copy_max(0, None)
            act.wait_ge(filled.sem, filled.at(5))
            keep_values(None)
            with act.Fori(0, B) as i:
                for h in range(HEADS):
                    for n in range(UNITS):
                        u = h * UNITS + n
                        act.wait_ge(scored.sem, scored.at(u + 1 - LAG, i))
                        act.wait_ge(weighed.sem, weighed.at(u + 1 - RING, i))
                        nc.scalar.activation(probs[:, u % RING, :], s_psum[:, u % 2, :], ACT.Exp, scale=SCALE).then_inc(exped.next(), 1)
                        late = h == HEADS - 1
                        if h % 2 and n in (Q_AT + late, K_AT + late, K_AT + 1 + late):
                            split((h + 1) // 2, n - late, i)
                        if n == TURN_AT + late:
                            copy_max(h + 1, i)
                        if n == 1 and h > 0:
                            copy_out(h - 1, 1, i)
                        if n == 0 and h > 0:
                            copy_out(h - 1, 0, i)
                        if h == HEADS - 2 and n == UNITS - 2:
                            group_rstd(i)
                copy_out(HEADS - 1, 0, i)
                copy_out(HEADS - 1, 1, i)
                keep_values(i)
            for s in (act_step, gn_rstd, v_kept, qk_high, max_copied, exped, o_copied):
                s.end_of_pass()

        @block.vector
        def _(dve):
            dve.sem_inc(*head_done.lead())
            dve.sem_inc(*y_made.lead())
            dve.wait_ge(filled.sem, filled.at(5))

            def moments(i):
                dve.wait_ge(x_loaded, 16 if i is None else i * 16 + 32)
                gn.vector_moments(dve, xin[:, :], step, i, gn_moments)

            def variance(i):
                dve.wait_ge(gn_groups.sem, gn_groups.at(1, i))
                gn.vector_variance(dve, m_psum[:, 2, 0:2], step, i, gn_var)

            def normalise(i):
                dve.wait_ge(gn_rstd.sem, gn_rstd.at(1, i))
                gn.vector_shift(dve, step, i)
                nc.vector.tensor_scalar(xn[:, :, :].rearrange("p t n -> p (t n)"), xin[:, :],
                                        gn.rstd[:, :], gn.shift[:, :], ALU.mult, ALU.add).then_inc(xn_ready.next(), 1)
                dve.wait_ge(xn_ready.sem, xn_ready.at(1, i))
                dve.sem_inc(xin_free.sem, 1)

            def split(pair, part, i):
                at = nth(pair, 1, i)
                for odd in range(2):
                    s = (2 * pair + odd) % SLOTS
                    dve.wait_ge(qk_high.sem, qk_high.at(6 * at + 2 * part + odd + 1, i))
                    rows = 64 if part == 0 else HEAD
                    source = slot(part)[64 * odd:64 * odd + rows, :]
                    if part == 0:
                        nc.vector.tensor_tensor(q_all[64:128, s, :], source, as_f32(q_all[0:64, s, :]),
                                                ALU.subtract).then_inc(qk_low.next(), 1)
                    else:
                        nc.vector.tensor_tensor(k_lo[0:HEAD, s, :], source, as_f32(k_hi[0:HEAD, s, :]),
                                                ALU.subtract).then_inc(qk_low.next(), 1)

            def row_max(g, tile, i):
                dve.wait_ge(rows_made.sem, rows_made.at(nth(g, KEYS, i) + tile + 1, i))
                nc.vector.tensor_reduce(maxima[:, MAX_ROW + tile:MAX_ROW + tile + 1], slot(tile % 2),
                                        AX.X, ALU.max, negate=True).then_inc(rows_max.next(), 1)

            def invert(h, part, i):
                cols = slice(part * P, (part + 1) * P)
                dve.wait_ge(o_copied.sem, o_copied.at(2 * h + part // (KEYS // 2) + 1, i))
                values, sums = 64 * (h % 2), 64 * (1 - h % 2)
                nc.vector.reciprocal(o_inv[values:values + HEAD, cols], o_raw[sums:sums + HEAD, cols]).then_inc(inverted.next(), 1)

            def divide(h, i):
                row = 64 * (h % 2)
                dve.wait_ge(inverted.sem, inverted.at(KEYS * (h + 1), i))
                nc.vector.tensor_tensor(heads_out[row:row + HEAD, h // 2, :], o_raw[row:row + HEAD, :],
                                        o_inv[row:row + HEAD, :], ALU.mult).then_inc(head_done.next(), 1)

            moments(None)
            variance(None)
            normalise(None)
            split(0, 0, None)
            split(0, 1, None)
            for tile in range(KEYS):
                row_max(0, tile, None)
            with dve.Fori(0, B) as i:
                for h in range(HEADS):
                    late = h == HEADS - 1
                    for n in range(UNITS):
                        if h == HEADS - 2 and n == 0:
                            moments(i)
                        if h == HEADS - 2 and n == UNITS - 3:
                            variance(i)
                        if h == HEADS - 2 and n == UNITS - 1:
                            normalise(i)
                        if h % 2 and n in (Q_AT + late, K_AT + late):
                            split((h + 1) // 2, n - late, i)
                        if 0 <= n - ROWS_AT - late < KEYS:
                            row_max(h + 1, n - ROWS_AT - late, i)
                        if h > 0 and n in INV_AT:
                            invert(h - 1, INV_AT.index(n), i)
                        if h > 0 and n == INV_AT[-1] + 1:
                            divide(h - 1, i)
                for part in range(KEYS):
                    invert(HEADS - 1, part, i)
                divide(HEADS - 1, i)
                dve.wait_ge(res_loaded, i * 16 + 16)
                for n in range(2 * CT):
                    m, half = n // 2, n % 2
                    dve.wait_ge(projected.sem, projected.at(n + 1, i))
                    cols = slice(m * T + half * HALF, m * T + (half + 1) * HALF)
                    nc.vector.scalar_tensor_tensor(xres[:, cols], m_psum[:, n % 4, :], proj_b[:, m:m + 1], xres[:, cols],
                                                   ALU.add, ALU.add).then_inc(y_made.next(), 1)
            for s in (step, gn_moments, gn_var, xn_ready, qk_low, rows_max, inverted, head_done, y_made):
                s.end_of_pass()

        @block.tensor
        def _(pe):
            pe.sem_inc(*weighed.lead())
            pe.wait_ge(filled.sem, filled.at(5))
            pe.wait_ge(turned_ident.sem, turned_ident.at(1))

            def groups(i):
                pe.wait_ge(gn_moments.sem, gn_moments.at(1, i))
                gn.tensor_groups(pe, m_psum[:, 2, 0:2], const["group_mean"]).then_inc(gn_groups.next(), 1)

            def values(i):
                for tile in range(KEYS):
                    if tile >= 2:
                        pe.wait_ge(v_kept.sem, v_kept.at(tile - 1, i))
                    for t in range(CT):
                        ins = nc.tensor.matmul(m_psum[:, 2 * (tile % 2), 0:C], xn[:, t, tile * P:(tile + 1) * P],
                                               v_w[:, t, :], start=(t == 0), stop=(t == CT - 1))
                    ins.then_inc(v_made.next(), 1)

            def project_qk(pair, part, i):
                w = q_w if part == 0 else k_w
                for half in range(2):
                    for t in range(CT):
                        ins = nc.tensor.matmul(m_psum[:, 2 * part + half, :], w[:, t, pair % PAIRS, :],
                                               xn[:, t, half * HALF:(half + 1) * HALF], start=(t == 0), stop=(t == CT - 1))
                ins.then_inc(qk_made.next(), 1)

            def row_scores(g, tile, i):
                if tile == 0:
                    pair = nth(g // 2, 1, i)
                    pe.wait_ge(qk_low.sem, qk_low.at(4 * pair + 4, i))
                    pe.wait_ge(qk_high.sem, qk_high.at(6 * pair + 6, i))
                if tile >= 2:
                    pe.wait_ge(rows_max.sem, rows_max.at(nth(g, KEYS, i) + tile - 1, i))
                for half in range(2):
                    ins = nc.tensor.matmul(m_psum[:, 2 * (tile % 2) + half, :],
                                           q_all[:, g % SLOTS, tile * P:(tile + 1) * P],
                                           k_hi[:, g % SLOTS, half * HALF:(half + 1) * HALF], start=True, stop=True)
                ins.then_inc(rows_made.next(), 1)

            def turn_max(g, i):
                pe.wait_ge(rows_max.sem, rows_max.at(nth(g, KEYS, i) + KEYS, i))
                for tile in range(KEYS):
                    ins = nc.tensor.matmul(m_psum[0:MAX_ROW + 1, tile // 4, (tile % 4) * P:(tile % 4 + 1) * P],
                                           maxima[:, tile:tile + MAX_ROW + 1], ident_r[:, :], start=True, stop=True)
                ins.then_inc(max_turned.next(), 1)

            def scores(u, i):
                h, n = u // UNITS, u % UNITS
                tile, half = n // 2, n % 2
                if n == 0:
                    pe.wait_ge(max_placed, 16 if i is None else (i * HEADS + h + 1) * 16)
                if i is not None:
                    pe.wait_ge(exped.sem, exped.at(u - 1, i))
                q = q_all[:, h % SLOTS, half * HALF:(half + 1) * HALF]
                keys = slice(tile * P, (tile + 1) * P)
                nc.tensor.matmul(s_psum[:, u % 2, :], k_hi[:, h % SLOTS, keys], q, start=True, stop=False)
                nc.tensor.matmul(s_psum[:, u % 2, :], k_lo[:, h % SLOTS, keys], q, start=False, stop=True).then_inc(scored.next(), 1)

            def weigh(u, i):
                h, n = u // UNITS, u % UNITS
                tile, half = n // 2, n % 2
                if n < 2:
                    pe.wait_ge(o_copied.sem, o_copied.at(2 * (h - 1) + n + 1, i))
                if u == 0:
                    pe.wait_ge(v_kept.sem, v_kept.at(0, i))
                pe.wait_ge(exped.sem, exped.at(u + 1, i))
                nc.tensor.matmul(o_psum[:, half, :], v[:, tile, h // 2, h % 2:h % 2 + 2, :].rearrange("p a b -> p (a b)"),
                                 probs[:, u % RING, :], start=(tile == 0), stop=(tile == KEYS - 1)).then_inc(weighed.next(), 1)

            groups(None)
            pe.wait_ge(xn_ready.sem, xn_ready.at(1))
            project_qk(0, 0, None)
            project_qk(0, 1, None)
            for tile in range(KEYS):
                row_scores(0, tile, None)
            turn_max(0, None)
            pe.wait_ge(max_copied.sem, max_copied.at(1))
            values(None)
            for u in range(LAG):
                scores(u, None)
            with pe.Fori(0, B) as i:
                for u in range(N):
                    h, n = u // UNITS, u % UNITS
                    late = h == HEADS - 1
                    if h % 2 and n in (Q_AT + late, K_AT + late):
                        if n == Q_AT + late:
                            pe.wait_ge(max_copied.sem, max_copied.at(h, i))
                            if late:
                                pe.wait_ge(xn_ready.sem, xn_ready.at(1, i))
                        project_qk((h + 1) // 2, n - late, i)
                    if 0 <= n - ROWS_AT - late < KEYS:
                        if n == ROWS_AT and h == 0:
                            pe.wait_ge(y_made.sem, y_made.at(0, i))
                        if n == ROWS_AT and h % 2 == 0:
                            pe.wait_ge(max_copied.sem, max_copied.at(h, i))
                        row_scores(h + 1, n - ROWS_AT - late, i)
                    if n == TURN_AT + late:
                        turn_max(h + 1, i)
                    if h == HEADS - 2 and n == UNITS - 4:
                        groups(i)
                    scores(u + LAG, i)
                    weigh(u, i)
                pe.wait_ge(max_copied.sem, max_copied.at(HEADS, i))
                values(i)
                pe.wait_ge(v_kept.sem, v_kept.at(KEYS, i))
                pe.wait_ge(head_done.sem, head_done.at(HEADS, i))
                for n in range(2 * CT):
                    m, half = n // 2, n % 2
                    if n >= 4:
                        pe.wait_ge(y_made.sem, y_made.at(n - 3, i))
                    for pair in range(PAIRS):
                        ins = nc.tensor.matmul(m_psum[:, n % 4, :], proj_w[:, pair, m * P:(m + 1) * P],
                                               heads_out[:, pair, half * HALF:(half + 1) * HALF],
                                               start=(pair == 0), stop=(pair == PAIRS - 1))
                    ins.then_inc(projected.next(), 1)
            for s in (gn_groups, v_made, qk_made, rows_made, max_turned, scored, weighed, projected):
                s.end_of_pass()


class ChannelNorm:

    def __init__(self, nc, sb, name, mean_psum, var_psum, col_mean, eps):
        self.nc, self.mean_psum, self.var_psum, self.col_mean = nc, mean_psum, var_psum, col_mean
        self.log = sb(name + "_log", [P, 2, HALF])
        self.inv = sb(name + "_inv", [P, 2, HALF])
        self.eps = eps

    def tensor_sum(self, psum, x, half):
        for t in range(CT):
            ins = self.nc.tensor.matmul(psum[:, half, :], self.col_mean, x[:, t, half * HALF:(half + 1) * HALF],
                                        start=(t == 0), stop=(t == CT - 1))
        return ins

    def over_tiles(self, ap):
        return ap.unsqueeze(1).broadcast_to([P, CT, HALF])

    def vector_centre(self, x, half):
        cols = x[:, :, half * HALF:(half + 1) * HALF]
        return self.nc.vector.tensor_tensor(cols, cols, self.over_tiles(self.mean_psum[:, half, :]), ALU.subtract)

    def scalar_square(self, squares, x, half):
        cols = slice(half * HALF, (half + 1) * HALF)
        return self.nc.scalar.activation(squares[:, :, cols], x[:, :, cols], ACT.Square)

    def scalar_inverse(self, act, half, step, i, ready):
        self.nc.scalar.activation(self.log[:, half, :], self.var_psum[:, half, :], ACT.Ln, bias=self.eps).then_inc(step.next(), 1)
        act.wait_ge(step.sem, step.now(i))
        self.nc.scalar.activation(self.inv[:, half, :], self.log[:, half, :], ACT.Exp, scale=-0.5).then_inc(ready.next(), 1)

    def vector_scale(self, x, half):
        cols = x[:, :, half * HALF:(half + 1) * HALF]
        return self.nc.vector.tensor_tensor(cols, cols, self.over_tiles(self.inv[:, half, :]), ALU.mult)


def s5_constants(nc, lam, log_step, tables, decay, gain, keep):
    Q, J = lam.shape[0], 2
    TURN = 6.283185
    TO_ONE = 12582912.0
    TO_HIGH = 1536.0
    with ExitStack() as ctx:
        def sb(name, shape, dt=F32):
            return ctx.enter_context(nc.sbuf_tensor(name, shape, dt))[tuple(slice(None) for _ in shape)]
        count = sb("count", [Q, T], mybir.dt.int32)
        t = sb("times", [Q, T])
        high, low, whole = (sb(n, [Q, T]) for n in ("turn_high", "turn_low", "turn_whole"))
        step, a, f, f_high, f_low, r, s1, s2 = (sb("s5_" + n, [Q, J]) for n in ("step", "a", "f", "fh", "fl", "r", "s1", "s2"))
        trig = sb("s5_trig", [Q, 2, J])
        eps = sb("s5_c", [Q, 4, J])
        counted = Signal(ctx.enter_context(nc.semaphore("counted")))
        v = Signal(ctx.enter_context(nc.semaphore("s5_v")))
        s = Signal(ctx.enter_context(nc.semaphore("s5_s")))
        block = ctx.enter_context(nc.Block())
        V, re, im = nc.vector, lam[:, :, 0], lam[:, :, 1]

        @block.gpsimd
        def _(pool):
            pool.iota(count, pattern=[[1, T]], base=0, channel_multiplier=0).then_inc(counted.next(), 1)

        TRIG = 10
        table_ready = [TRIG + 1 + 10 * (n // 2) + 4 + 3 * (n % 2 + 1) for n in range(2 * J)]

        @block.scalar
        def _(act):
            nc.scalar.activation(step, log_step, ACT.Exp).then_inc(s.next(), 1)
            act.wait_ge(s.sem, s.at(s.count))
            act.wait_ge(v.sem, v.at(1))
            nc.scalar.activation(r, a, ACT.Exp).then_inc(s.next(), 1)
            act.wait_ge(s.sem, s.at(s.count))
            act.wait_ge(v.sem, v.at(TRIG))
            nc.scalar.activation(trig, trig, ACT.Sin, scale=TURN).then_inc(s.next(), 1)
            act.wait_ge(s.sem, s.at(s.count))
            for n in range(2 * J):
                act.wait_ge(v.sem, v.at(table_ready[n]))
                nc.scalar.activation(tables[:, n % 2, n // 2, :], tables[:, n % 2, n // 2, :], ACT.Sin, scale=TURN).then_inc(s.next(), 1)

        @block.vector
        def _(dve):
            def do(ins):
                ins.then_inc(v.next(), 1)
                dve.wait_ge(v.sem, v.at(v.count))
            dve.wait_ge(s.sem, s.at(1))
            do(V.tensor_tensor(a, re, step, ALU.mult))
            do(V.tensor_tensor(f, im, step, ALU.mult))
            do(V.tensor_scalar(f, f, 1.0 / (2.0 * np.pi), None, ALU.mult))
            do(V.tensor_scalar(trig[:, 0, :], f, 0.25, None, ALU.add))
            do(V.tensor_scalar(s1, trig[:, 0, :], TO_ONE, TO_ONE, ALU.add, ALU.subtract))
            do(V.tensor_tensor(trig[:, 0, :], trig[:, 0, :], s1, ALU.subtract))
            do(V.tensor_scalar(s1, f, TO_ONE, TO_ONE, ALU.add, ALU.subtract))
            do(V.tensor_tensor(trig[:, 1, :], f, s1, ALU.subtract))
            do(V.tensor_scalar(f_high, f, TO_HIGH, TO_HIGH, ALU.add, ALU.subtract))
            do(V.tensor_tensor(f_low, f, f_high, ALU.subtract))
            assert v.count == TRIG
            dve.wait_ge(counted.sem, counted.at(1))
            do(V.tensor_copy(t, count))
            for j in range(J):
                do(V.tensor_scalar(high, t, f_high[:, j:j + 1], None, ALU.mult))
                do(V.tensor_scalar(whole, high, TO_ONE, TO_ONE, ALU.add, ALU.subtract))
                do(V.tensor_tensor(high, high, whole, ALU.subtract))
                do(V.scalar_tensor_tensor(high, t, f_low[:, j:j + 1], high, ALU.mult, ALU.add))
                for n, quarter in enumerate((0.25, 0.0)):
                    do(V.tensor_scalar(low, high, quarter, None, ALU.add))
                    do(V.tensor_scalar(whole, low, TO_ONE, TO_ONE, ALU.add, ALU.subtract))
                    do(V.tensor_tensor(tables[:, n, j, :], low, whole, ALU.subtract))
                    assert v.count == table_ready[2 * j + n]
            dve.wait_ge(s.sem, s.at(3))
            do(V.tensor_copy(decay, r))
            nr, ni, den = eps[:, 0, :], eps[:, 1, :], eps[:, 2, :]
            do(V.tensor_tensor(nr, r, trig[:, 0, :], ALU.mult))
            do(V.tensor_scalar(nr, nr, -1.0, None, ALU.add))
            do(V.tensor_tensor(ni, r, trig[:, 1, :], ALU.mult))
            do(V.tensor_tensor(s1, re, re, ALU.mult))
            do(V.tensor_tensor(s2, im, im, ALU.mult))
            do(V.tensor_tensor(den, s1, s2, ALU.add))
            do(V.reciprocal(den, den))
            do(V.tensor_tensor(s1, nr, re, ALU.mult))
            do(V.tensor_tensor(s2, ni, im, ALU.mult))
            do(V.tensor_tensor(s1, s1, s2, ALU.add))
            do(V.tensor_tensor(gain[:, 0, :], s1, den, ALU.mult))
            do(V.tensor_tensor(s1, ni, re, ALU.mult))
            do(V.tensor_tensor(s2, nr, im, ALU.mult))
            do(V.tensor_tensor(s1, s1, s2, ALU.subtract))
            do(V.tensor_tensor(gain[:, 1, :], s1, den, ALU.mult))
            do(V.tensor_tensor(s1, f, f, ALU.mult))
            do(V.tensor_scalar(keep[:, 0, :], s1, 0.0625, 2.0, ALU.is_lt, ALU.mult))
            do(V.tensor_scalar(keep[:, 1, :], s1, 0.0625, -2.0, ALU.is_lt, ALU.mult))


def s5_layer(nc, const, x_in, x_out, w):
    J = 2
    Q = w["log_step"].shape[0] // J
    LN_EPS = 1e-5
    with ExitStack() as ctx:
        def sb(name, shape, dt=F32):
            return ctx.enter_context(nc.sbuf_tensor(name, shape, dt))

        def signal(name, per=None):
            return Signal(ctx.enter_context(nc.semaphore(name)), per)

        b_w = sb("b_w", [P, CT, 2, J, Q])
        c_w = sb("c_w", [Q, 2, J, C])
        enc_w = sb("enc_w", [P, CT, 2 * C])
        dec_w = sb("dec_w", [P, CT, C])
        rows = {n: sb(n + "_c", [P, CT]) for n in ("ln1_g", "ln1_b", "ln2_g", "ln2_b", "D")}
        tables = sb("tables", [Q, 2, J, T])
        decay = sb("decay", [Q, J])
        gain = sb("gain", [Q, 2, J])
        keep = sb("keep", [Q, 2, J])
        lam = sb("lam", [Q, J, 2])
        log_step = sb("log_step", [Q, J])
        eps = sb("eps", [P, 1])
        with nc.semaphore("params") as params, nc.Block() as block:
            small = [(lam[:, :, :], w["Lambda"].rearrange("(j q) e -> q j e", j=J)),
                     (log_step[:, :], w["log_step"].rearrange("(j q) -> q j", j=J)),
                     *[(rows[n][:, :], w[n].rearrange("(p t) -> p t", t=CT)) for n in rows]]

            @block.sync
            def _(sp):
                for tile, source in small:
                    sp.dma_start(tile, source, allow_slow_non_contiguous=True).then_inc(params, 16)
                sp.wait_ge(params, 16 * len(small))

            @block.vector
            def _(dve):
                nc.vector.memset(eps[:, :], LN_EPS)
        s5_constants(nc, lam[:, :, :], log_step[:, :], tables[:, :, :, :], decay[:, :], gain[:, :, :], keep[:, :, :])

        with nc.sbuf_tensor("b_rows", [Q, J, C, 2], F32) as b_rows, nc.sbuf_tensor("b_bar", [Q, 2, J, C], F32) as b_bar, \
                nc.sbuf_tensor("b_part", [Q, J, C], F32) as b_part, \
                nc.sbuf_tensor("c_rows", [P, CT, 2 * J * Q], F32) as c_rows, \
                nc.sbuf_tensor("enc_rows", [P, 2, CT, C], F32) as enc_rows, nc.sbuf_tensor("dec_rows", [P, CT, C], F32) as dec_rows:
            with nc.semaphore("b_loaded") as b_loaded, nc.semaphore("b_step") as b_step, nc.Block() as block:
                @block.sync
                def _(sp):
                    sp.dma_start(b_rows[:, :, :, :], w["Bmat"].rearrange("(j q) c e -> q j c e", j=J)).then_inc(b_loaded, 16)

                @block.vector
                def _(dve):
                    dve.wait_ge(b_loaded, 16)
                    n = 0
                    for j in range(J):
                        re, im = b_rows[:, j, :, 0], b_rows[:, j, :, 1]
                        g_re, g_im = gain[:, 0, j:j + 1], gain[:, 1, j:j + 1]
                        for part, a, b, sign in ((0, re, im, ALU.subtract), (1, im, re, ALU.add)):
                            nc.vector.tensor_scalar(b_part[:, j, :], b, g_im, None, ALU.mult).then_inc(b_step, 1)
                            n += 1
                            dve.wait_ge(b_step, n)
                            nc.vector.scalar_tensor_tensor(b_bar[:, part, j, :], a, g_re, b_part[:, j, :],
                                                           ALU.mult, sign).then_inc(b_step, 1)
                            n += 1
                            dve.wait_ge(b_step, n)
            pieces = []
            for t in range(CT):
                pieces.append(([b_bar[:, part, j, t::CT] for part in range(2) for j in range(J)],
                               b_w[:, t, :, :, :].rearrange("p a b c -> p (a b c)")))
                for half in range(2):
                    pieces.append(([enc_rows[:, half, m, t::CT] for m in range(CT)], enc_w[:, t, half * C:(half + 1) * C]))
                pieces.append(([dec_rows[:, m, t::CT] for m in range(CT)], dec_w[:, t, :]))
            for part in range(2):
                for j in range(J):
                    first = 2 * j * Q + part
                    pieces.append(([c_rows[:, m, first:first + 2 * Q - 1:2] for m in range(CT)], c_w[:, part, j, :]))
            loads = [(c_rows[:, :, :], w["Cmat"].rearrange("(p m) s e -> p m (s e)", m=CT)),
                     (dec_rows[:, :, :], w["W_dec"].rearrange("(p m) c -> p m c", m=CT)),
                     *[(enc_rows[:, half, :, :], w["W_enc"].rearrange("(h p m) c -> h p m c", h=2, m=CT)[half]) for half in range(2)]]
            turn_weights(nc, "w1", const["ident"], pieces, loads)
        with nc.semaphore("c_kept") as c_kept, nc.Block() as block:
            @block.vector
            def _(dve):
                for part in range(2):
                    for j in range(J):
                        nc.vector.tensor_scalar(c_w[:, part, j, :], c_w[:, part, j, :], keep[:, part, j:j + 1], None, ALU.mult)

        gn = GroupNorm(nc, sb, ctx.enter_context(nc.semaphore("gn1_turn")), "gn1")
        xin = sb("xin1", [P, CT * T])
        xres = sb("xres1", [P, CT, T])
        a = sb("a1", [P, CT, T])
        sq = sb("sq1", [P, CT, T])
        f = sb("f1", [P, CT, T])
        u = sb("u1", [Q, 2, J, T])
        z = sb("z1", [Q, 2, J, T])
        prod = sb("prod1", [Q, 2, 2, HALF])
        gate = sb("gate1", [P, 2, HALF])
        psum = ctx.enter_context(nc.psum_tensor("psum1", [P, 4, HALF], F32))
        mean_psum = ctx.enter_context(nc.psum_tensor("mean1", [P, 2, HALF], F32))
        var_psum = ctx.enter_context(nc.psum_tensor("var1", [P, 2, HALF], F32))
        norm = ChannelNorm(nc, sb, "ln", mean_psum, var_psum, const["col_mean"], eps[:, :])

        x_loaded, res_loaded, stored = (ctx.enter_context(nc.semaphore(n)) for n in ("x_loaded1", "res_loaded1", "stored1"))
        xin_free = signal("xin_free1")
        step = signal("step1", 10 + 4)
        act_step = signal("act_step1", 1 + 4)
        gn_moments, gn_groups, gn_var, gn_rstd = (signal(n + "1", 1) for n in ("gn_moments", "gn_groups", "gn_var", "gn_rstd"))
        a_made = signal("a_made", 1 + 2 * CT)
        averaged = signal("averaged", 4)
        centred = signal("centred", 4)
        squared = signal("squared", 4)
        varied = signal("varied", 4)
        inv_made = signal("inv_made", 4)
        f_made = signal("f_made", 4 * CT)
        u_product = signal("u_product", 2 * J)
        products = signal("products", 4 * 2 * J)
        sums = signal("sums", 4 * 2 * J)
        scanned = signal("scanned", 2 * J)
        y_product = signal("y_product", 2 * CT)
        y_plain = signal("y_plain", 2 * CT)
        y_gelu = signal("y_gelu", 2 * CT)
        hidden = signal("hidden", 4 * CT)
        gated = signal("gated", 2 * CT)
        hid_made = signal("hid_made", 2 * CT)
        res_added = signal("res_added", 2)
        decoded = signal("decoded", 2 * CT)
        out_made = signal("out_made", 2 * CT)

        def cols(half):
            return slice(half * HALF, (half + 1) * HALF)

        block = ctx.enter_context(nc.Block())

        @block.sync
        def _(sp):
            sp.sem_inc(stored, 16)
            sp.dma_start(xin[:, :], x_in[0:1].rearrange("a (p t) n -> p (a t n)", t=CT)).then_inc(x_loaded, 16)
            with sp.Fori(0, B) as i:
                sp.wait_ge(stored, i * 16 + 16)
                sp.dma_start(xres[:, :, :].rearrange("p t n -> p (t n)"), x_in[bass.ds(i, 1)].rearrange("a (p t) n -> p (a t n)", t=CT)).then_inc(res_loaded, 16)
                sp.wait_ge(xin_free.sem, i + 1)
                sp.dma_start(xin[:, :], x_in[bass.ds((i + 1) % B, 1)].rearrange("a (p t) n -> p (a t n)", t=CT)).then_inc(x_loaded, 16)
                sp.wait_ge(out_made.sem, out_made.at(2 * CT, i))
                sp.dma_start(x_out[bass.ds(i, 1)].rearrange("a (p t) n -> p (a t n)", t=CT), xres[:, :, :].rearrange("p t n -> p (t n)")).then_inc(stored, 16)
            sp.wait_ge(stored, 16 * B + 16)
            sp.wait_ge(x_loaded, 16 * B + 16)

        @block.gpsimd
        def _(pool):
            with pool.Fori(0, B) as i:
                for way in range(2):
                    for j in range(J):
                        for half in range(2):
                            for part in range(2):
                                n = ((way * J + j) * 2 + half) * 2 + part
                                pool.wait_ge(products.sem, products.at(n + 1, i))
                                pool.tensor_tensor(u[:, part, j, cols(half)], prod[:, part, 0, :],
                                                                  prod[:, part, 1, :], ALU.add if part == way else ALU.subtract).then_inc(sums.next(), 1)
                pool.wait_ge(res_loaded, i * 16 + 16)
                for half in range(2):
                    pool.wait_ge(f_made.sem, f_made.at(2 * CT + CT * (half + 1), i))
                    pool.tensor_tensor(xres[:, :, cols(half)], xres[:, :, cols(half)], f[:, :, cols(half)], ALU.add).then_inc(res_added.next(), 1)
            for s in (sums, res_added):
                s.end_of_pass()

        @block.scalar
        def _(act):
            with act.Fori(0, B) as i:
                act.wait_ge(gn_var.sem, gn_var.at(1, i))
                gn.scalar_rstd(act, act_step, i, gn_rstd)

                def normalise(first):
                    for half in range(2):
                        act.wait_ge(centred.sem, centred.at(first + half + 1, i))
                        norm.scalar_square(sq, a, half).then_inc(squared.next(), 1)
                    for half in range(2):
                        act.wait_ge(varied.sem, varied.at(first + half + 1, i))
                        norm.scalar_inverse(act, half, act_step, i, inv_made)

                normalise(0)
                for n in range(2 * CT):
                    act.wait_ge(y_plain.sem, y_plain.at(n + 1, i))
                    at = a[:, n // 2, cols(n % 2)]
                    nc.scalar.activation(at, at, ACT.Gelu).then_inc(y_gelu.next(), 1)
                normalise(2)
                for n in range(2 * CT):
                    act.wait_ge(hidden.sem, hidden.at(2 * n + 1, i))
                    if n >= 2:
                        act.wait_ge(hid_made.sem, hid_made.at(n - 1, i))
                    nc.scalar.activation(gate[:, n % 2, :], psum[:, 2 * (n % 2), :], ACT.Gelu).then_inc(gated.next(), 1)
            for s in (act_step, gn_rstd, squared, inv_made, y_gelu, gated):
                s.end_of_pass()

        @block.vector
        def _(dve):
            with dve.Fori(0, B) as i:
                dve.wait_ge(x_loaded, i * 16 + 16)
                gn.vector_moments(dve, xin[:, :], step, i, gn_moments)
                dve.wait_ge(gn_groups.sem, gn_groups.at(1, i))
                gn.vector_variance(dve, psum[:, 0, 0:2], step, i, gn_var)
                dve.wait_ge(gn_rstd.sem, gn_rstd.at(1, i))
                gn.vector_shift(dve, step, i)
                nc.vector.tensor_scalar(a[:, :, :].rearrange("p t n -> p (t n)"), xin[:, :],
                                                         gn.rstd[:, :], gn.shift[:, :], ALU.mult, ALU.add).then_inc(a_made.next(), 1)
                dve.wait_ge(a_made.sem, a_made.at(1, i))
                dve.sem_inc(xin_free.sem, 1)

                def normalise(first, g, b):
                    for half in range(2):
                        dve.wait_ge(averaged.sem, averaged.at(first + half + 1, i))
                        norm.vector_centre(a, half).then_inc(centred.next(), 1)
                    for half in range(2):
                        dve.wait_ge(inv_made.sem, inv_made.at(first + half + 1, i))
                        norm.vector_scale(a, half).then_inc(step.next(), 1)
                        dve.wait_ge(step.sem, step.now(i))
                        for t in range(CT):
                            nc.vector.tensor_scalar(f[:, t, cols(half)], a[:, t, cols(half)],
                                                                     g[:, t:t + 1], b[:, t:t + 1], ALU.mult, ALU.add).then_inc(f_made.next(), 1)

                def turn(n, re, im, sin_first):
                    j, half = (n // 2) % J, n % 2
                    cos, sin = tables[:, 0, j, cols(half)], tables[:, 1, j, cols(half)]
                    for part, (x0, x1) in enumerate(((re, im), (im, re))):
                        if n > 0:
                            dve.wait_ge(sums.sem, sums.at(2 * (n - 1) + part + 1, i))
                        nc.vector.tensor_tensor(prod[:, part, 0, :], x0, cos, ALU.mult)
                        nc.vector.tensor_tensor(prod[:, part, 1, :], x1, sin, ALU.mult).then_inc(products.next(), 1)

                normalise(0, rows["ln1_g"], rows["ln1_b"])
                for n in range(2 * J):
                    dve.wait_ge(u_product.sem, u_product.at(n + 1, i))
                    turn(n, psum[0:Q, 2 * (n % 2), :], psum[0:Q, 2 * (n % 2) + 1, :], False)
                for j in range(J):
                    for part in range(2):
                        dve.wait_ge(sums.sem, sums.at(4 * (j + 1), i))
                        nc.vector.tensor_tensor_scan(
                            z[:, part, j, :], decay[:, j:j + 1].broadcast_to([Q, T]), u[:, part, j, :], 0.0, ALU.mult, ALU.add).then_inc(scanned.next(), 1)
                for n in range(2 * J):
                    j, half = n // 2, n % 2
                    dve.wait_ge(scanned.sem, scanned.at(2 * (j + 1), i))
                    turn(2 * J + n, z[:, 0, j, cols(half)], z[:, 1, j, cols(half)], True)
                for n in range(2 * CT):
                    m, half = n // 2, n % 2
                    dve.wait_ge(y_product.sem, y_product.at(n + 1, i))
                    nc.vector.scalar_tensor_tensor(a[:, m, cols(half)], f[:, m, cols(half)],
                                                                     rows["D"][:, m:m + 1], psum[:, n % 4, :], ALU.mult, ALU.add).then_inc(y_plain.next(), 1)
                for n in range(2 * CT):
                    m, half = n // 2, n % 2
                    dve.wait_ge(y_gelu.sem, y_gelu.at(n + 1, i))
                    nc.vector.tensor_tensor(a[:, m, cols(half)], a[:, m, cols(half)], f[:, m, cols(half)], ALU.add).then_inc(a_made.next(), 1)
                dve.wait_ge(a_made.sem, a_made.at(1 + 2 * CT, i))
                normalise(2, rows["ln2_g"], rows["ln2_b"])
                for n in range(2 * CT):
                    m, half = n // 2, n % 2
                    dve.wait_ge(gated.sem, gated.at(n + 1, i))
                    dve.wait_ge(hidden.sem, hidden.at(2 * n + 2, i))
                    nc.vector.tensor_tensor(sq[:, m, cols(half)], gate[:, n % 2, :],
                                                               psum[:, 2 * (n % 2) + 1, :], ALU.mult).then_inc(hid_made.next(), 1)
                dve.wait_ge(res_added.sem, res_added.at(2, i))
                for n in range(2 * CT):
                    m, half = n // 2, n % 2
                    dve.wait_ge(decoded.sem, decoded.at(n + 1, i))
                    nc.vector.tensor_tensor(xres[:, m, cols(half)], xres[:, m, cols(half)],
                                                               psum[:, n % 4, :], ALU.add).then_inc(out_made.next(), 1)
            for s in (step, gn_moments, gn_var, a_made, centred, f_made, products, scanned, y_plain, hid_made, out_made):
                s.end_of_pass()

        @block.tensor
        def _(pe):
            with pe.Fori(0, B) as i:
                pe.wait_ge(gn_moments.sem, gn_moments.at(1, i))
                gn.tensor_groups(pe, psum[:, 0, 0:2], const["group_mean"]).then_inc(gn_groups.next(), 1)

                def normalise(first):
                    for half in range(2):
                        norm.tensor_sum(mean_psum, a, half).then_inc(averaged.next(), 1)
                    for half in range(2):
                        pe.wait_ge(squared.sem, squared.at(first + half + 1, i))
                        norm.tensor_sum(var_psum, sq, half).then_inc(varied.next(), 1)

                pe.wait_ge(a_made.sem, a_made.at(1, i))
                normalise(0)
                for n in range(2 * J):
                    j, half = n // 2, n % 2
                    if half == 0 and j == 0:
                        pe.wait_ge(f_made.sem, f_made.at(CT, i))
                    if half == 1 and j == 0:
                        pe.wait_ge(f_made.sem, f_made.at(2 * CT, i))
                    if n >= 2:
                        pe.wait_ge(products.sem, products.at(2 * (n - 1), i))
                    for part in range(2):
                        for t in range(CT):
                            ins = nc.tensor.matmul(psum[0:Q, 2 * (n % 2) + part, :], b_w[:, t, part, j, :],
                                                   f[:, t, cols(half)], start=(t == 0), stop=(t == CT - 1))
                    ins.then_inc(u_product.next(), 1)
                for n in range(2 * CT):
                    m, half = n // 2, n % 2
                    if n < 2:
                        pe.wait_ge(sums.sem, sums.at(4 * J + 4 * (J - 1) + 2 * (half + 1), i))
                    if n >= 4:
                        pe.wait_ge(y_plain.sem, y_plain.at(n - 3, i))
                    k = 0
                    for part in range(2):
                        for j in range(J):
                            ins = nc.tensor.matmul(psum[:, n % 4, :], c_w[:, part, j, m * P:(m + 1) * P],
                                                   u[:, part, j, cols(half)], start=(k == 0), stop=(k == 2 * J - 1))
                            k += 1
                    ins.then_inc(y_product.next(), 1)
                pe.wait_ge(a_made.sem, a_made.at(1 + 2 * CT, i))
                normalise(2)
                for n in range(2 * CT):
                    m, half = n // 2, n % 2
                    if n == 0:
                        pe.wait_ge(f_made.sem, f_made.at(4 * CT, i))
                    if n >= 2:
                        pe.wait_ge(hid_made.sem, hid_made.at(n - 1, i))
                    for k, first in enumerate((C, 0)):
                        for t in range(CT):
                            ins = nc.tensor.matmul(psum[:, 2 * (n % 2) + k, :], enc_w[:, t, first + m * P:first + (m + 1) * P],
                                                   f[:, t, cols(half)], start=(t == 0), stop=(t == CT - 1))
                        ins.then_inc(hidden.next(), 1)
                pe.wait_ge(hid_made.sem, hid_made.at(2 * CT, i))
                for n in range(2 * CT):
                    m, half = n // 2, n % 2
                    if n >= 4:
                        pe.wait_ge(out_made.sem, out_made.at(n - 3, i))
                    for t in range(CT):
                        ins = nc.tensor.matmul(psum[:, n % 4, :], dec_w[:, t, m * P:(m + 1) * P], sq[:, t, cols(half)],
                                               start=(t == 0), stop=(t == CT - 1))
                    ins.then_inc(decoded.next(), 1)
                pe.wait_ge(out_made.sem, out_made.at(2 * CT, i))
            for s in (gn_groups, averaged, varied, u_product, y_product, hidden, decoded):
                s.end_of_pass()


def depthwise_layer(nc, const, x_in, x_out, w):
    S = 32
    TAPS = 7
    PAD = 2 * S - 1
    mid = S - 1 - TAPS // 2
    GROUP = 8
    N = B * S
    with ExitStack() as ctx:
        def sb(name, shape, dt=F32):
            return ctx.enter_context(nc.sbuf_tensor(name, shape, dt))

        def signal(name, per=None, head=0):
            return Signal(ctx.enter_context(nc.semaphore(name)), per, head)

        both = sb("both2", [P, B, 2])
        moments = sb("moments2", [P, B, 2])
        var, rstd, shift = (sb(n + "2", [P, B]) for n in ("var", "rstd", "shift"))
        stats = sb("stats2", [P, 6, 6])
        taps = {n: sb(n + "_c", [P, CT, w[n].shape[2], w[n].shape[3]]) for n in ("w77", "w53", "w35", "w7w", "w7h", "w5w", "w5h")}
        biases = {n: sb(n + "_c", [P, CT]) for n in ("b77", "b53", "b35")}
        padded = sb("padded", [P, CT, TAPS, PAD])
        padded_dram = nc.dram_tensor("padded_dram", [CT, P, TAPS, PAD], F32).ap()
        bias = sb("bias2", [P, CT])
        bands = sb("bands", [P, 2, GROUP, TAPS, P])
        psum = ctx.enter_context(nc.psum_tensor("psum2", [P, 4, 2, N], F32))

        with nc.sbuf_tensor("x_pair", [P, 2, CT * T], F32) as x_pair, ExitStack() as inner:
            sem = lambda n: inner.enter_context(nc.semaphore(n))
            loaded = [sem("stat_loaded0"), sem("stat_loaded1")]
            small_loaded, tap_written = sem("small_loaded"), sem("tap_written")
            read, v = Signal(sem("stat_read")), Signal(sem("stat_v"))
            grouped, var_made, rstd_made, tap_made = (Signal(sem(n)) for n in ("grouped2", "var_made2", "rstd_made2", "tap_made"))
            act_step = Signal(sem("act_step2"))
            zeroed = Signal(sem("zeroed2"))
            block = inner.enter_context(nc.Block())

            @block.sync
            def _(sp):
                for n in range(B):
                    if n >= 2:
                        sp.wait_ge(read.sem, read.at(n - 1))
                    sp.dma_start(x_pair[:, n % 2, :], x_in[n].rearrange("(p t) n -> p (t n)", t=CT)).then_inc(loaded[n % 2], 16)
                sp.wait_ge(tap_made.sem, tap_made.at(1))
                sp.dma_start(padded_dram.rearrange("t p a b -> p t (a b)"),
                             padded[:, :, :, :].rearrange("p t a b -> p t (a b)")).then_inc(tap_written, 16)
                sp.wait_ge(tap_written, 16)

            @block.scalar
            def _(act):
                for n, tile in taps.items():
                    act.dma_start(tile[:, :, :, :].rearrange("p t a b -> p (t a b)"),
                                  w[n].rearrange("(p t) e a b -> p (t e a b)", t=CT)).then_inc(small_loaded, 16)
                for n, tile in biases.items():
                    act.dma_start(tile[:, :], w[n].rearrange("(p t) -> p t", t=CT)).then_inc(small_loaded, 16)
                act.wait_ge(small_loaded, 16 * 10)
                act.wait_ge(var_made.sem, var_made.at(1))
                nc.scalar.activation(rstd[:, :], var[:, :], ACT.Ln).then_inc(act_step.next(), 1)
                act.wait_ge(act_step.sem, act_step.at(act_step.count))
                nc.scalar.activation(rstd[:, :], rstd[:, :], ACT.Exp, scale=-0.5).then_inc(rstd_made.next(), 1)

            @block.gpsimd
            def _(pool):
                pool.memset(bands[:, :, :, :, :], 0.0).then_inc(zeroed.next(), 1)

            @block.tensor
            def _(pe):
                pe.wait_ge(read.sem, read.at(B))
                nc.tensor.matmul(psum[:, 0, 0, 0:2 * B], const["group_mean"],
                                                   both[:, :, :].rearrange("p b e -> p (b e)"), start=True, stop=True).then_inc(grouped.next(), 1)

            @block.vector
            def _(dve):
                V = nc.vector
                V.memset(padded[:, :, :, :], 0.0).then_inc(v.next(), 1)
                dve.wait_ge(v.sem, v.at(v.count))
                dve.wait_ge(small_loaded, 16 * 10)
                V.tensor_tensor(bias[:, :], biases["b77"][:, :], biases["b53"][:, :], ALU.add).then_inc(v.next(), 1)
                dve.wait_ge(v.sem, v.at(v.count))
                V.tensor_tensor(bias[:, :], bias[:, :], biases["b35"][:, :], ALU.add).then_inc(v.next(), 1)
                dve.wait_ge(v.sem, v.at(v.count))
                V.tensor_copy(padded[:, :, :, mid:mid + 7], taps["w77"][:, :, :, :]).then_inc(v.next(), 1)
                dve.wait_ge(v.sem, v.at(v.count))
                for n, rows, columns in (("w53", 5, 3), ("w35", 3, 5)):
                    at = padded[:, :, 3 - rows // 2:4 + rows // 2, mid + 3 - columns // 2:mid + 4 + columns // 2]
                    V.tensor_tensor(at, at, taps[n][:, :, :, :], ALU.add).then_inc(v.next(), 1)
                    dve.wait_ge(v.sem, v.at(v.count))
                for down, across, size in (("w7h", "w7w", 7), ("w5h", "w5w", 5)):
                    for t in range(CT):
                        for r in range(size):
                            at = padded[:, t, 3 - size // 2 + r, mid + 3 - size // 2:mid + 4 + size // 2]
                            V.scalar_tensor_tensor(at, taps[across][:, t, 0, :], taps[down][:, t, r, :], at,
                                                               ALU.mult, ALU.add).then_inc(v.next(), 1)
                    dve.wait_ge(v.sem, v.at(v.count))
                V.tensor_copy(padded[:, :, :, 0:1], padded[:, :, :, 0:1]).then_inc(tap_made.next(), 1)
                for n in range(B):
                    dve.wait_ge(loaded[n % 2], 16 * (n // 2 + 1))
                    for c in range(6):
                        V.bn_stats(stats[:, c, :], x_pair[:, n % 2, c * HALF:(c + 1) * HALF]).then_inc(v.next(), 1)
                    dve.wait_ge(v.sem, v.at(v.count))
                    V.bn_aggr(both[:, n, :], stats[:, :, :].rearrange("p a b -> p (a b)")).then_inc(v.next(), 1)
                    dve.wait_ge(v.sem, v.at(v.count))
                    V.scalar_tensor_tensor(both[:, n, 1:2], both[:, n, 0:1], both[:, n, 0:1],
                                                          both[:, n, 1:2], ALU.mult, ALU.add).then_inc(read.next(), 1)
                dve.wait_ge(grouped.sem, grouped.at(1))
                V.tensor_copy(moments[:, :, :].rearrange("p b e -> p (b e)"), psum[:, 0, 0, 0:2 * B]).then_inc(v.next(), 1)
                dve.wait_ge(v.sem, v.at(v.count))
                V.tensor_tensor(var[:, :], moments[:, :, 0], moments[:, :, 0], ALU.mult).then_inc(v.next(), 1)
                dve.wait_ge(v.sem, v.at(v.count))
                V.scalar_tensor_tensor(var[:, :], moments[:, :, 1], GN_EPS, var[:, :], ALU.add, ALU.subtract).then_inc(var_made.next(), 1)
                dve.wait_ge(rstd_made.sem, rstd_made.at(1))
                V.scalar_tensor_tensor(shift[:, :], moments[:, :, 0], -1.0, rstd[:, :], ALU.mult, ALU.mult).then_inc(v.next(), 1)
                dve.wait_ge(v.sem, v.at(v.count))

        xb = sb("xb", [P, B, T])
        xt = sb("xt", [P, S, B, S])
        yt = sb("yt", [P, S, B, S])
        xn = sb("xn2", [P, 2, T])
        yb = sb("yb", [P, 2, T])
        bias_t = sb("bias_t", [P, 1])
        GROUPS_T = S // GROUP
        x_loaded, stored = (ctx.enter_context(nc.semaphore(n)) for n in ("x_loaded2", "stored2"))
        band_loaded = [ctx.enter_context(nc.semaphore(f"band_loaded{n}")) for n in range(2)]
        normed = signal("normed", B)
        turned = signal("turned", B)
        PAIRS = GROUP // 2
        convolved = signal("convolved", S // 2, head=2 * PAIRS)
        kept = signal("kept2", S // 2)
        back = signal("back2", B)
        out_made = signal("out_made2", B)
        block = ctx.enter_context(nc.Block())

        @block.sync
        def _(sp):
            sp.sem_inc(stored, 16)
            with sp.Fori(0, CT) as t:
                sp.wait_ge(stored, t * 16 + 16)
                sp.dma_start(xb[:, :, :], x_in.rearrange("b (p t) n -> t p b n", t=CT)[bass.ds(t, 1)].rearrange("a p b n -> p (a b) n")).then_inc(x_loaded, 16)
                sp.wait_ge(out_made.sem, out_made.at(B, t))
                sp.dma_start(x_out.rearrange("b (p t) n -> t p b n", t=CT)[bass.ds(t, 1)].rearrange("a p b n -> p (a b) n"), xb[:, :, :]).then_inc(stored, 16)
            sp.wait_ge(stored, 16 * CT + 16)

        @block.gpsimd
        def _(pool):
            pool.sem_inc(*convolved.lead())
            with pool.Fori(0, CT) as t:
                for g in range(GROUPS_T):
                    pool.wait_ge(convolved.sem, convolved.at((g - 1) * PAIRS, t))
                    for q in range(4):
                        target = bands[q * S:(q + 1) * S, g % 2, :, :, q * S:(q + 1) * S].rearrange("p a b c -> p (a b) c")
                        row = padded_dram[bass.ds(t, 1), q * S + g * GROUP:q * S + (g + 1) * GROUP, :, 0:S]
                        row = row.rearrange("e c a b -> (e c a) b")
                        source = bass.AP(tensor=row.tensor, offset=row.offset, ap=[[1, S], *row.ap])
                        pool.dma_start(target, source).then_inc(band_loaded[g % 2], 16)
            for s in band_loaded:
                pool.wait_ge(s, CT * GROUPS_T // 2 * 4 * 16)

        @block.scalar
        def _(act):
            with act.Fori(0, CT) as t:
                act.wait_ge(x_loaded, t * 16 + 16)
                for b in range(B):
                    if b >= 2:
                        act.wait_ge(turned.sem, turned.at(b - 1, t))
                    nc.scalar.activation(xn[:, b % 2, :], xb[:, b, :], ACT.Identity,
                                                          scale=rstd[:, b:b + 1], bias=shift[:, b:b + 1]).then_inc(normed.next(), 1)
                for n in range(S // 2):
                    act.wait_ge(convolved.sem, convolved.at(n + 1, t))
                    nc.scalar.copy(yt[:, 2 * n:2 * n + 2, :, :].rearrange("p c b h -> p (c b h)"),
                                                  psum[:, n % 4, :, :].rearrange("p c n -> p (c n)")).then_inc(kept.next(), 1)
            for s in (normed, kept):
                s.end_of_pass()

        @block.vector
        def _(dve):
            with dve.Fori(0, CT) as t:
                dve.wait_ge(convolved.sem, convolved.at(0, t))
                for b in range(B):
                    dve.wait_ge(normed.sem, normed.at(b + 1, t))
                    nc.vector.transpose(xt[:, :, b, :].rearrange("p j h -> p h j"),
                                                         xn[:, b % 2, :].rearrange("p (h j) -> p h j", j=S)).then_inc(turned.next(), 1)
                dve.wait_ge(kept.sem, kept.at(S // 2, t))
                for b in range(B):
                    nc.vector.transpose(yb[:, b % 2, :].rearrange("p (h j) -> p h j", j=S),
                                                       yt[:, :, b, :].rearrange("p j h -> p h j")).then_inc(back.next(), 1)
                    dve.wait_ge(back.sem, back.now(t))
                    at = xb[:, b, :].rearrange("p (h j) -> p h j", j=S)
                    nc.vector.scalar_tensor_tensor(
                        at, yb[:, b % 2, :].rearrange("p (h j) -> p h j", j=S)[:, :, ::-1], bias[:, bass.ds(t, 1)], at,
                        ALU.add, ALU.add).then_inc(out_made.next(), 1)
            for s in (turned, back, out_made):
                s.end_of_pass()

        @block.tensor
        def _(pe):
            with pe.Fori(0, CT) as t:
                pe.wait_ge(turned.sem, turned.at(B, t))
                for n in range(S // 2):
                    g = 2 * n // GROUP
                    if n % PAIRS == 0:
                        pe.wait_ge(band_loaded[g % 2], t * (GROUPS_T // 2 * 64) + (g // 2 + 1) * 64)
                    if n >= 4:
                        pe.wait_ge(kept.sem, kept.at(n - 3, t))
                    for c in range(2):
                        channel = 2 * n + c
                        out = psum[:, n % 4, c, :].rearrange("p (b h) -> p b h", h=S)
                        for k, tap in enumerate((3, 0, 1, 2, 4, 5, 6)):
                            down = tap - TAPS // 2
                            rows = slice(max(0, -down), S - max(0, down))
                            ins = nc.tensor.matmul(out[:, :, rows], bands[:, g % 2, channel % GROUP, tap, :],
                                                   xt[:, channel, :, rows.start + down:rows.stop + down],
                                                   start=(k == 0), stop=(k == TAPS - 1))
                    ins.then_inc(convolved.next(), 1)
                pe.wait_ge(kept.sem, kept.at(S // 2, t))
            convolved.end_of_pass()


def rwkv_layer(nc, const, x_in, x_out, w):
    S, CAP, LN_EPS, NEG = 32, 40.0, 1e-5, -1e38
    with ExitStack() as ctx:
        def sb(name, shape, dt=F32):
            return ctx.enter_context(nc.sbuf_tensor(name, shape, dt))

        def signal(name, per=None, head=0):
            return Signal(ctx.enter_context(nc.semaphore(name)), per, head)

        lin_w = {n: sb(n + "_t", [P, CT, C]) for n in ("Wk", "Wv", "Wr", "Wo")}
        conv_w = sb("conv_t", [P, CT, 9, C])
        names = ("ln_g", "ln_b", "w_param", "u", "bn_g", "bn_b", "gamma_g", "gamma_s")
        cols = {n: sb(n + "_3", [P, CT]) for n in names}
        decay = sb("decay3", [P, CT])
        cap = sb("cap3", [P, CT])
        bn_scale = sb("bn_scale", [P, CT])
        eps = sb("eps3", [P, 1])
        with nc.sbuf_tensor("conv_rows", [P, CT, C * 9], F32) as conv_rows, \
                nc.sbuf_tensor("lin_rows", [P, 4, CT, C], F32) as lin_rows:
            pieces, loads = [], [(conv_rows[:, :, :], w["conv_w"].rearrange("(p m) c a b -> p m (c a b)", m=CT))]
            for n, name in enumerate(lin_w):
                loads.append((lin_rows[:, n, :, :], w[name].rearrange("(p m) c -> p m c", m=CT)))
                for t in range(CT):
                    pieces.append(([lin_rows[:, n, m, t::CT] for m in range(CT)], lin_w[name][:, t, :]))
            for name in names:
                source = w[name] if len(w[name].shape) == 1 else w[name].rearrange("a c b d -> (a c b d)")
                loads.append((cols[name][:, :], source.rearrange("(p t) -> p t", t=CT)))
            for tap in range(9):
                for t in range(CT):
                    first = t * 9 + tap
                    pieces.append(([conv_rows[:, m, first:C * 9:CT * 9] for m in range(CT)], conv_w[:, t, tap, :]))
            turn_weights(nc, "w3", const["ident"], pieces, loads)
        with nc.semaphore("decay_made") as decay_made, nc.Block() as block:
            @block.scalar
            def _(act):
                nc.scalar.activation(decay[:, :], cols["w_param"][:, :], ACT.Exp).then_inc(decay_made, 1)

            @block.vector
            def _(dve):
                nc.vector.memset(eps[:, :], LN_EPS)
                nc.vector.tensor_scalar(cap[:, :], cols["u"][:, :], -1.0, CAP, ALU.mult, ALU.add)
                nc.vector.tensor_scalar(bn_scale[:, :], cols["bn_g"][:, :], 1.0 / np.sqrt(1.0 + 1e-5), None, ALU.mult)
                dve.wait_ge(decay_made, 1)
                nc.vector.tensor_scalar(decay[:, :], decay[:, :], -1.0, None, ALU.mult)

        gn = GroupNorm(nc, sb, ctx.enter_context(nc.semaphore("gn3_turn")), "gn3")
        xin = sb("xin3", [P, CT * T])
        xres = sb("xres3", [P, CT, T])
        xp = sb("xp", [P, CT, S + 2, S + 2])
        k = sb("k3", [P, CT, T])
        v = sb("v3", [P, CT, T])
        h = sb("h3", [P, CT, T])
        p = sb("p3", [P, T + 2])
        to_a = sb("to_a", [P, 2, T])
        to_f = sb("to_f", [P, 2, T])
        to_e = sb("to_e", [P, 2, T])
        kv = sb("kv3", [P, T])
        num = sb("num3", [P, T + 2])
        den = sb("den3", [P, T + 2])
        ev = sb("ev3", [P, T])
        side = sb("side3", [P, 2, HALF])
        psum = ctx.enter_context(nc.psum_tensor("psum3", [P, 4, HALF], F32))
        mean_psum = ctx.enter_context(nc.psum_tensor("mean3", [P, 2, HALF], F32))
        var_psum = ctx.enter_context(nc.psum_tensor("var3", [P, 2, HALF], F32))
        norm = ChannelNorm(nc, sb, "ln3", mean_psum, var_psum, const["col_mean"], eps[:, :])

        ITEMS = 2 * CT
        LOW, KV, CONV, GATE = 2 * CT, 4 * CT, 6 * CT, 8 * CT
        x_loaded, res_loaded, stored = (ctx.enter_context(nc.semaphore(n)) for n in ("x_loaded3", "res_loaded3", "stored3"))
        xin_free = signal("xin_free3")
        framed = signal("framed")
        step = signal("step3", 10 + 2)
        act_step = signal("act_step3", 1 + 2 + ITEMS)
        gn_moments, gn_groups, gn_var, gn_rstd, xp_made = (signal(n + "3", 1) for n in ("gn_moments", "gn_groups", "gn_var", "gn_rstd", "xp_made"))
        product = signal("product3", GATE)
        emptied = signal("emptied3", GATE)
        max_made = signal("max_made", ITEMS)
        fall = signal("fall", ITEMS)
        rise = signal("rise", ITEMS)
        jump = signal("jump", ITEMS)
        jump_capped = signal("jump_capped", ITEMS)
        a_exped = signal("a_exped", ITEMS)
        f_exped = signal("f_exped", ITEMS)
        e_exped = signal("e_exped", ITEMS)
        kv_made = signal("kv_made", ITEMS)
        ev_made = signal("ev_made", ITEMS)
        num_made = signal("num_made", ITEMS)
        den_made = signal("den_made", ITEMS)
        num_out = signal("num_out", ITEMS)
        den_out = signal("den_out", ITEMS)
        den_inv = signal("den_inv", ITEMS)
        h_made = signal("h_made", ITEMS + 2 * CT)
        side_used = signal("side_used", 2 * CT)
        quot = signal("quot", CT)
        leaked = signal("leaked", 2 * CT)
        averaged, centred, squared, varied, inv_made = (signal(n + "3", 2) for n in ("averaged", "centred", "squared", "varied", "inv_made"))
        hn_made = signal("hn_made", 2 * CT)
        mixed = signal("mixed", 2 * CT)
        out_made = signal("out_made3", 2 * CT)

        def half_of(ap, half):
            return ap[:, :, half * HALF:(half + 1) * HALF] if len(ap.shape) == 3 else ap[:, half * HALF:(half + 1) * HALF]

        def way(ap, backwards):
            return ap[:, ::-1] if backwards else ap

        def now(ap):
            return ap[:, 1:T + 1]

        def before(ap, backwards):
            return ap[:, 2:T + 2] if backwards else ap[:, 0:T]

        def rows_of(t, half, down, across):
            top = 1 + half * S // 2 + down
            return xp[:, t, top:top + S // 2, 1 + across:1 + across + S]

        block = ctx.enter_context(nc.Block())

        @block.sync
        def _(sp):
            sp.sem_inc(stored, 16)
            sp.dma_start(xin[:, :], x_in[0:1].rearrange("a (p t) n -> p (a t n)", t=CT)).then_inc(x_loaded, 16)
            with sp.Fori(0, B) as i:
                sp.wait_ge(stored, i * 16 + 16)
                sp.dma_start(xres[:, :, :].rearrange("p t n -> p (t n)"), x_in[bass.ds(i, 1)].rearrange("a (p t) n -> p (a t n)", t=CT)).then_inc(res_loaded, 16)
                sp.wait_ge(xin_free.sem, i + 1)
                sp.dma_start(xin[:, :], x_in[bass.ds((i + 1) % B, 1)].rearrange("a (p t) n -> p (a t n)", t=CT)).then_inc(x_loaded, 16)
                sp.wait_ge(out_made.sem, out_made.at(2 * CT, i))
                sp.dma_start(x_out[bass.ds(i, 1)].rearrange("a (p t) n -> p (a t n)", t=CT), xres[:, :, :].rearrange("p t n -> p (t n)")).then_inc(stored, 16)
            sp.wait_ge(stored, 16 * B + 16)
            sp.wait_ge(x_loaded, 16 * B + 16)

        @block.gpsimd
        def _(pool):
            pool.memset(xp[:, :, :, :], 0.0).then_inc(framed.next(), 1)
            for tile, value in ((p, NEG), (num, 0.0), (den, 0.0)):
                pool.memset(tile[:, 0:1], value).then_inc(framed.next(), 1)
                pool.memset(tile[:, T + 1:T + 2], value).then_inc(framed.next(), 1)
            with pool.Fori(0, B) as i:
                for n in range(ITEMS):
                    t, backwards = n // 2, n % 2
                    pool.wait_ge(max_made.sem, max_made.at(n + 1, i))
                    pool.tensor_tensor(to_a[:, n % 2, :], k[:, t, :], now(p), ALU.subtract).then_inc(rise.next(), 1)
                    pool.tensor_tensor(to_e[:, n % 2, :], k[:, t, :], before(p, backwards), ALU.subtract).then_inc(jump.next(), 1)
                    pool.wait_ge(jump.sem, jump.now(i))
                    pool.sem_inc(gn.turn, 1)
                    pool.tensor_scalar(to_e[:, n % 2, :], to_e[:, n % 2, :], cap[:, t:t + 1], None, ALU.min).then_inc(jump_capped.next(), 1)
                    pool.wait_ge(ev_made.sem, ev_made.at(n + 1, i))
                    pool.wait_ge(den_made.sem, den_made.at(n + 1, i))
                    pool.tensor_tensor(to_e[:, n % 2, :], to_e[:, n % 2, :], before(den, backwards), ALU.add).then_inc(den_out.next(), 1)
            for s in (rise, jump, jump_capped, den_out):
                s.end_of_pass()

        @block.scalar
        def _(act):
            with act.Fori(0, B) as i:
                act.wait_ge(gn_var.sem, gn_var.at(1, i))
                gn.scalar_rstd(act, act_step, i, gn_rstd)
                for n in range(KV):
                    act.wait_ge(product.sem, product.at(n + 1, i))
                    target = half_of((k if n < LOW else v)[:, (n % LOW) // 2, :], n % 2)
                    nc.scalar.copy(target, psum[:, n % 4, :]).then_inc(emptied.next(), 1)

                def leaky(n):
                    m = n // 2
                    if n >= 2:
                        act.wait_ge(side_used.sem, side_used.at(n - 1, i))
                    act.wait_ge(product.sem, product.at(KV + n + 1, i))
                    nc.scalar.activation(side[:, n % 2, :], psum[:, (KV + n) % 4, :], ACT.Identity,
                                                           scale=bn_scale[:, m:m + 1], bias=cols["bn_b"][:, m:m + 1]).then_inc(emptied.next(), 1)

                def exps(n):
                    t = n // 2
                    act.wait_ge(rise.sem, rise.at(n + 1, i))
                    nc.scalar.activation(to_a[:, n % 2, :], to_a[:, n % 2, :], ACT.Exp).then_inc(a_exped.next(), 1)
                    act.wait_ge(fall.sem, fall.at(n + 1, i))
                    nc.scalar.activation(to_f[:, n % 2, :], to_f[:, n % 2, :], ACT.Exp, bias=decay[:, t:t + 1]).then_inc(f_exped.next(), 1)
                    act.wait_ge(jump_capped.sem, jump_capped.at(n + 1, i))
                    nc.scalar.activation(to_e[:, n % 2, :], to_e[:, n % 2, :], ACT.Exp, bias=cols["u"][:, t:t + 1]).then_inc(e_exped.next(), 1)

                def inverse(n):
                    at = to_e[:, n % 2, :]
                    act.wait_ge(den_out.sem, den_out.at(n + 1, i))
                    nc.scalar.activation(at, at, ACT.Ln).then_inc(act_step.next(), 1)
                    act.wait_ge(act_step.sem, act_step.now(i))
                    nc.scalar.activation(at, at, ACT.Exp, scale=-1.0).then_inc(den_inv.next(), 1)

                for n in range(ITEMS + 1):
                    if n < ITEMS:
                        exps(n)
                    if n > 0:
                        inverse(n - 1)
                    if n in (3, 5):
                        leaky(n // 2 - 1)
                for n in range(2, 2 * CT):
                    leaky(n)
                for n in range(2 * CT):
                    if n < 2:
                        act.wait_ge(side_used.sem, side_used.at(2 * CT - 1 + n, i))
                    else:
                        act.wait_ge(h_made.sem, h_made.at(ITEMS + n - 1, i))
                    act.wait_ge(product.sem, product.at(CONV + n + 1, i))
                    nc.scalar.activation(side[:, n % 2, :], psum[:, (CONV + n) % 4, :], ACT.Sigmoid).then_inc(emptied.next(), 1)
                for half in range(2):
                    act.wait_ge(centred.sem, centred.at(half + 1, i))
                    norm.scalar_square(v, h, half).then_inc(squared.next(), 1)
                for half in range(2):
                    act.wait_ge(varied.sem, varied.at(half + 1, i))
                    norm.scalar_inverse(act, half, act_step, i, inv_made)
            for s in (act_step, gn_rstd, emptied, a_exped, f_exped, e_exped, den_inv, squared, inv_made):
                s.end_of_pass()

        @block.vector
        def _(dve):
            dve.wait_ge(framed.sem, framed.at(7))
            with dve.Fori(0, B) as i:
                dve.wait_ge(x_loaded, i * 16 + 16)
                gn.vector_moments(dve, xin[:, :], step, i, gn_moments)
                dve.wait_ge(gn_groups.sem, gn_groups.at(1, i))
                gn.vector_variance(dve, psum[:, 0, 0:2], step, i, gn_var)
                dve.wait_ge(gn_rstd.sem, gn_rstd.at(1, i))
                gn.vector_shift(dve, step, i)
                for t in range(CT):
                    ins = nc.vector.tensor_scalar(xp[:, t, 1:S + 1, 1:S + 1], xin[:, t * T:(t + 1) * T].rearrange("p (a b) -> p a b", b=S),
                                                  gn.rstd[:, :], gn.shift[:, :], ALU.mult, ALU.add)
                ins.then_inc(xp_made.next(), 1)
                dve.wait_ge(xp_made.sem, xp_made.at(1, i))
                dve.sem_inc(xin_free.sem, 1)

                def maxima(n):
                    t, backwards = n // 2, n % 2
                    if backwards == 0:
                        dve.wait_ge(emptied.sem, emptied.at(2 * (t + 1), i))
                    if n > 0:
                        dve.wait_ge(jump.sem, jump.at(n, i))
                        dve.wait_ge(fall.sem, fall.at(n, i))
                    if n > 1:
                        dve.wait_ge(kv_made.sem, kv_made.at(n - 1, i))
                    nc.vector.tensor_tensor_scan(
                        way(now(p), backwards), decay[:, t:t + 1].broadcast_to([P, T]), way(k[:, t, :], backwards),
                        NEG, ALU.add, ALU.max).then_inc(max_made.next(), 1)
                    dve.wait_ge(max_made.sem, max_made.now(i))
                    nc.vector.tensor_tensor(to_f[:, n % 2, :], before(p, backwards), now(p), ALU.subtract).then_inc(fall.next(), 1)

                def scans(n):
                    t, backwards = n // 2, n % 2
                    dve.wait_ge(a_exped.sem, a_exped.at(n + 1, i))
                    if backwards == 0:
                        dve.wait_ge(emptied.sem, emptied.at(LOW + 2 * (t + 1), i))
                    nc.vector.tensor_tensor(kv[:, :], to_a[:, n % 2, :], v[:, t, :], ALU.mult).then_inc(kv_made.next(), 1)
                    dve.wait_ge(kv_made.sem, kv_made.now(i))
                    dve.wait_ge(f_exped.sem, f_exped.at(n + 1, i))
                    if n > 0:
                        dve.wait_ge(num_out.sem, num_out.at(n, i))
                        dve.wait_ge(den_out.sem, den_out.at(n, i))
                    nc.vector.tensor_tensor_scan(
                        way(now(num), backwards), way(to_f[:, n % 2, :], backwards), way(kv[:, :], backwards), 0.0, ALU.mult, ALU.add).then_inc(num_made.next(), 1)
                    nc.vector.tensor_tensor_scan(
                        way(now(den), backwards), way(to_f[:, n % 2, :], backwards), way(to_a[:, n % 2, :], backwards), 0.0, ALU.mult, ALU.add).then_inc(den_made.next(), 1)
                    dve.wait_ge(e_exped.sem, e_exped.at(n + 1, i))
                    nc.vector.tensor_tensor(ev[:, :], to_e[:, n % 2, :], v[:, t, :], ALU.mult).then_inc(ev_made.next(), 1)
                    dve.wait_ge(ev_made.sem, ev_made.now(i))
                    nc.vector.tensor_tensor(ev[:, :], ev[:, :], before(num, backwards), ALU.add).then_inc(num_out.next(), 1)

                def quotient(n):
                    t, backwards = n // 2, n % 2
                    dve.wait_ge(den_inv.sem, den_inv.at(n + 1, i))
                    dve.wait_ge(num_out.sem, num_out.at(n + 1, i))
                    at = h[:, t, :]
                    if backwards == 0:
                        nc.vector.tensor_tensor(at, ev[:, :], to_e[:, n % 2, :], ALU.mult).then_inc(h_made.next(), 1)
                    else:
                        nc.vector.tensor_tensor(ev[:, :], ev[:, :], to_e[:, n % 2, :], ALU.mult).then_inc(quot.next(), 1)
                        dve.wait_ge(quot.sem, quot.now(i))
                        dve.wait_ge(h_made.sem, h_made.at(n, i))
                        nc.vector.tensor_tensor(at, at, ev[:, :], ALU.add).then_inc(h_made.next(), 1)

                def add_side(n):
                    m = n // 2
                    if n == 0:
                        dve.wait_ge(res_loaded, i * 16 + 16)
                    dve.wait_ge(emptied.sem, emptied.at(KV + n + 1, i))
                    at = half_of(xres[:, m, :], n % 2)
                    nc.vector.scalar_tensor_tensor(side[:, n % 2, :], side[:, n % 2, :], 0.01, side[:, n % 2, :],
                                                                    ALU.mult, ALU.max).then_inc(leaked.next(), 1)
                    dve.wait_ge(leaked.sem, leaked.now(i))
                    nc.vector.scalar_tensor_tensor(at, side[:, n % 2, :], cols["gamma_s"][:, m:m + 1], at,
                                                                       ALU.mult, ALU.add).then_inc(side_used.next(), 1)

                maxima(0)
                for n in range(ITEMS):
                    if n + 1 < ITEMS:
                        maxima(n + 1)
                    scans(n)
                    quotient(n)
                    if n in (4, 5):
                        add_side(n - 4)
                for n in range(2, 2 * CT):
                    add_side(n)
                dve.wait_ge(h_made.sem, h_made.at(ITEMS, i))
                for n in range(2 * CT):
                    at = half_of(h[:, n // 2, :], n % 2)
                    dve.wait_ge(emptied.sem, emptied.at(CONV + n + 1, i))
                    nc.vector.scalar_tensor_tensor(at, side[:, n % 2, :], 0.5, at, ALU.mult, ALU.mult).then_inc(h_made.next(), 1)
                for half in range(2):
                    dve.wait_ge(averaged.sem, averaged.at(half + 1, i))
                    norm.vector_centre(h, half).then_inc(centred.next(), 1)
                for half in range(2):
                    dve.wait_ge(inv_made.sem, inv_made.at(half + 1, i))
                    norm.vector_scale(h, half).then_inc(step.next(), 1)
                    dve.wait_ge(step.sem, step.now(i))
                    for t in range(CT):
                        at = half_of(h[:, t, :], half)
                        nc.vector.tensor_scalar(at, at, cols["ln_g"][:, t:t + 1], cols["ln_b"][:, t:t + 1],
                                                                  ALU.mult, ALU.add).then_inc(hn_made.next(), 1)
                for n in range(2 * CT):
                    m, half = n // 2, n % 2
                    dve.wait_ge(mixed.sem, mixed.at(n + 1, i))
                    at = half_of(xres[:, m, :], half)
                    nc.vector.scalar_tensor_tensor(at, psum[:, (GATE + n) % 4, :], cols["gamma_g"][:, m:m + 1],
                                                                      at, ALU.mult, ALU.add).then_inc(out_made.next(), 1)
            for s in (step, gn_moments, gn_var, xp_made, max_made, fall, kv_made, num_made, den_made, ev_made, num_out,
                      h_made, quot, leaked, side_used, centred, hn_made, out_made):
                s.end_of_pass()

        @block.tensor
        def _(pe):
            with pe.Fori(0, B) as i:
                pe.wait_ge(gn_moments.sem, gn_moments.at(1, i))
                gn.tensor_groups(pe, psum[:, 0, 0:2], const["group_mean"]).then_inc(gn_groups.next(), 1)
                pe.wait_ge(xp_made.sem, xp_made.at(1, i))

                def project(n, weights, taps):
                    m, half = (n % LOW) // 2, n % 2
                    if n >= 4:
                        pe.wait_ge(emptied.sem, emptied.at(n - 3, i))
                    parts = [(tap, t) for tap in taps for t in range(CT)]
                    for q, (tap, t) in enumerate(parts):
                        ins = nc.tensor.matmul(psum[:, n % 4, :].rearrange("p (a b) -> p a b", b=S), weights(t, tap)[:, m * P:(m + 1) * P],
                                               rows_of(t, half, tap // 3 - 1, tap % 3 - 1),
                                               start=(q == 0), stop=(q == len(parts) - 1))
                    ins.then_inc(product.next(), 1)

                for n in range(KV):
                    project(n, lambda t, tap: lin_w["Wk" if n < LOW else "Wv"][:, t, :], [4])
                for n in range(KV, CONV):
                    project(n, lambda t, tap: conv_w[:, t, tap, :], range(9))
                for n in range(CONV, GATE):
                    project(n, lambda t, tap: lin_w["Wr"][:, t, :], [4])
                for half in range(2):
                    pe.wait_ge(h_made.sem, h_made.at(ITEMS + 2 * CT - 1 + half, i))
                    norm.tensor_sum(mean_psum, h, half).then_inc(averaged.next(), 1)
                for half in range(2):
                    pe.wait_ge(squared.sem, squared.at(half + 1, i))
                    norm.tensor_sum(var_psum, v, half).then_inc(varied.next(), 1)
                pe.wait_ge(emptied.sem, emptied.at(GATE, i))
                for n in range(2 * CT):
                    m, half = n // 2, n % 2
                    if n == 0:
                        pe.wait_ge(hn_made.sem, hn_made.at(CT, i))
                    if n == 1:
                        pe.wait_ge(hn_made.sem, hn_made.at(2 * CT, i))
                    if n >= 4:
                        pe.wait_ge(out_made.sem, out_made.at(n - 3, i))
                    for t in range(CT):
                        ins = nc.tensor.matmul(psum[:, (GATE + n) % 4, :], lin_w["Wo"][:, t, m * P:(m + 1) * P],
                                               half_of(h[:, t, :], half), start=(t == 0), stop=(t == CT - 1))
                    ins.then_inc(mixed.next(), 1)
                pe.wait_ge(out_made.sem, out_made.at(2 * CT, i))
            for s in (gn_groups, product, averaged, varied, mixed):
                s.end_of_pass()


def build(nc, args, x_out):
    with ExitStack() as ctx:
        tiles = {name: ctx.enter_context(nc.sbuf_tensor(name, shape, F32)) for name, shape in
                 (("ident", [P, P]), ("group_mean", [P, P]), ("head_mask", [P, 1]), ("col_mean", [P, P]))}
        const = {name: tile[:, :] for name, tile in tiles.items()}
        make_constants(nc, const["ident"], const["group_mean"], const["head_mask"], const["col_mean"])
        x = args["x"].rearrange("b c h w -> b c (h w)")
        y = x_out.rearrange("b c h w -> b c (h w)")
        x1 = nc.dram_tensor("x1", [B, C, T], F32).ap()
        x2 = nc.dram_tensor("x2", [B, C, T], F32).ap()
        x3 = nc.dram_tensor("x3", [B, C, T], F32).ap()
        attention_layer(nc, const, x, x1, args["L0_conv_w_qkv"], args["L0_conv_w_proj"], args["L0_conv_b_proj"])
        s5_layer(nc, const, x1, x2, {k[8:]: v for k, v in args.items() if k.startswith("L1_conv_")})
        depthwise_layer(nc, const, x2, x3, {k[8:]: v for k, v in args.items() if k.startswith("L2_conv_")})
        rwkv_layer(nc, const, x3, y, {k[8:]: v for k, v in args.items() if k.startswith("L3_conv_")})


def kernel(**inputs):
    import numpy as _np
    import concourse.bacc as _bacc
    from concourse.bass_utils import run_bass_kernel_spmd as _run

    nc = _bacc.Bacc("TRN2", target_bir_lowering=False, num_devices=1)
    arrays, args = {}, {}
    for name, value in inputs.items():
        a = _np.ascontiguousarray(value)
        arrays[f"in_{name}"] = a
        args[name] = nc.dram_tensor(f"in_{name}", a.shape, mybir.dt.from_np(a.dtype), kind="ExternalInput").ap()
    out = nc.dram_tensor("out", inputs["x"].shape, F32, kind="ExternalOutput").ap()
    build(nc, args, out)
    r = _run(nc, [arrays], core_ids=[0])
    return r.results[0]["out"]
```

```python
from contextlib import ExitStack

import numpy as np

import concourse.bass as bass
from concourse import mybir

F32 = mybir.dt.float32
F32R = mybir.dt.float32r
ALU = mybir.AluOpType
ACT = mybir.ActivationFunctionType
AX = mybir.AxisListType

P = 128
HALF = 512
BANKS = 8
GROUPS = 32
GN_EPS = 1e-5


class Signal:

    def __init__(self, sem, per=None, head=0):
        self.sem, self.per, self.head, self.count = sem, per, head, 0

    def next(self):
        self.count += 1
        return self.sem

    def lead(self):
        self.count += self.head
        return self.sem, self.head

    def at(self, nth, i=None):
        assert self.per is None or nth <= self.per
        if i is None:
            return nth
        assert nth + self.head >= 1
        return i * self.per + nth + self.head

    def now(self, i=None):
        return self.count if i is None else i * self.per + self.count

    def start_pass(self):
        self.count = self.head

    def end_of_pass(self):
        assert self.per is None or self.count == self.head + self.per, (self.sem, self.count, self.head, self.per)


def as_f32(ap):
    return ap.bitcast(F32)


def turn_weights(nc, name, ident, pieces, loads):
    with ExitStack() as ctx:
        turned_psum = ctx.enter_context(nc.psum_tensor(name + "_turning", [P, 4, HALF], F32))
        loaded = ctx.enter_context(nc.semaphore(name + "_loaded"))
        turned = Signal(ctx.enter_context(nc.semaphore(name + "_turned")))
        kept = [Signal(ctx.enter_context(nc.semaphore(f"{name}_kept{n}"))) for n in range(2)]
        block = ctx.enter_context(nc.Block())

        @block.sync
        def _(sp):
            for tile, source in loads:
                sp.dma_start(tile, source).then_inc(loaded, 16)

        @block.tensor
        def _(pe):
            pe.wait_ge(loaded, 16 * len(loads))
            for n, (blocks, _) in enumerate(pieces):
                if n >= 4:
                    pe.wait_ge(kept[n % 2].sem, kept[n % 2].at((n - 4) // 2 + 1))
                for j, source in enumerate(blocks):
                    rows, cols = source.shape
                    ins = nc.tensor.transpose(turned_psum[0:cols, n % 4, j * rows:(j + 1) * rows], source,
                                              ident[0:rows, 0:rows])
                ins.then_inc(turned.next(), 1)

        def keep(eng, copy, parity):
            for n, (blocks, target) in enumerate(pieces):
                if n % 2 == parity:
                    eng.wait_ge(turned.sem, turned.at(n + 1))
                    rows, cols = blocks[0].shape
                    source = turned_psum[0:cols, n % 4, 0:len(blocks) * rows]
                    if len(target.shape) == 3:
                        source = source.rearrange("p (a b) -> p a b", b=target.shape[2])
                    copy(target, source).then_inc(kept[parity].next(), 1)

        @block.scalar
        def _(act):
            act.wait_ge(loaded, 16 * len(loads))
            keep(act, nc.scalar.copy, 0)

        @block.vector
        def _(dve):
            keep(dve, nc.vector.tensor_copy, 1)


def make_constants(nc, ident, group_mean, col_mean):
    with ExitStack() as ctx:
        filled = Signal(ctx.enter_context(nc.semaphore("filled")))
        block = ctx.enter_context(nc.Block())

        @block.gpsimd
        def _(pool):
            pool.memset(ident, 0.0).then_inc(filled.next(), 1)
            pool.memset(group_mean, GROUPS / P).then_inc(filled.next(), 1)
            pool.memset(col_mean, 1.0 / (3 * P)).then_inc(filled.next(), 1)
            pool.wait_ge(filled.sem, filled.at(filled.count))
            pool.affine_select(out=ident, in_=ident, compare_op=ALU.not_equal, fill=1.0, base=0,
                                                pattern=[[-1, P]], channel_multiplier=1).then_inc(filled.next(), 1)
            view = group_mean.rearrange("p (g e) -> p g e", e=4)
            pool.affine_select(out=view, in_=view, compare_op=ALU.is_ge, fill=0.0, base=0,
                                                 pattern=[[-4, GROUPS], [0, 4]], channel_multiplier=1).then_inc(filled.next(), 1)
            pool.wait_ge(filled.sem, filled.at(filled.count))
            pool.affine_select(out=view, in_=view, compare_op=ALU.is_ge, fill=0.0, base=3,
                                                 pattern=[[4, GROUPS], [0, 4]], channel_multiplier=-1).then_inc(filled.next(), 1)
            pool.wait_ge(filled.sem, filled.at(filled.count))


class GroupNorm:

    STEPS = 15

    def __init__(self, nc, sb, turn, name):
        self.nc, self.turn = nc, turn
        self.stats = sb(name + "_stats", [P, 6, 6], F32)
        self.both = sb(name + "_both", [P, 2], F32)
        self.moments = sb(name + "_moments", [P, 2], F32)
        self.var = sb(name + "_var", [P, 1], F32)
        self.log = sb(name + "_log", [P, 1], F32)
        self.rstd = sb(name + "_rstd", [P, 1], F32)
        self.shift = sb(name + "_shift", [P, 1], F32)

    def vector_moments(self, dve, x, step, i, ready):
        nc, both = self.nc, self.both
        chunks = x.shape[1] // HALF
        for n in range(chunks):
            nc.vector.bn_stats(self.stats[:, n, :], x[:, n * HALF:(n + 1) * HALF]).then_inc(step.next(), 1)
        dve.wait_ge(step.sem, step.now(i))
        dve.sem_inc(self.turn, 1)
        nc.vector.bn_aggr(both[:, :], self.stats[:, 0:chunks, :].rearrange("p a b -> p (a b)")).then_inc(step.next(), 1)
        dve.wait_ge(step.sem, step.now(i))
        nc.vector.scalar_tensor_tensor(both[:, 1:2], both[:, 0:1], both[:, 0:1], both[:, 1:2],
                                                       ALU.mult, ALU.add).then_inc(ready.next(), 1)

    def tensor_groups(self, pe, psum, group_mean):
        return self.nc.tensor.matmul(psum, group_mean, self.both[:, :], start=True, stop=True)

    def vector_variance(self, dve, psum, step, i, ready):
        nc, m = self.nc, self.moments
        nc.vector.tensor_copy(m[:, :], psum).then_inc(step.next(), 1)
        dve.wait_ge(step.sem, step.now(i))
        nc.vector.tensor_tensor(self.var[:, :], m[:, 0:1], m[:, 0:1], ALU.mult).then_inc(step.next(), 1)
        dve.wait_ge(step.sem, step.now(i))
        nc.vector.scalar_tensor_tensor(self.var[:, :], m[:, 1:2], GN_EPS, self.var[:, :],
                                                       ALU.add, ALU.subtract).then_inc(ready.next(), 1)

    def scalar_rstd(self, act, step, i, ready):
        self.nc.scalar.activation(self.log[:, :], self.var[:, :], ACT.Ln).then_inc(step.next(), 1)
        act.wait_ge(step.sem, step.now(i))
        self.nc.scalar.activation(self.rstd[:, :], self.log[:, :], ACT.Exp, scale=-0.5).then_inc(ready.next(), 1)

    def vector_shift(self, dve, step, i):
        self.nc.vector.scalar_tensor_tensor(self.shift[:, :], self.moments[:, 0:1], -1.0,
                                                           self.rstd[:, :], ALU.mult, ALU.mult).then_inc(step.next(), 1)
        dve.wait_ge(step.sem, step.now(i))


HEAD = 48
HEADS = 8
B, C, T = 8, 384, 1024
CT = C // P


def attention_layer(nc, const, x_in, x_out, w_qkv, w_proj, b_proj):
    SCALE = HEAD ** -0.5
    KEYS = T // P
    UNITS = 2 * KEYS
    N = HEADS * UNITS
    RING, SLOTS, LAG = 4, 4, 2
    PAIRS = HEADS // 2
    ALL_FILLED = 10
    ROW_UNITS = (2, 3, 4, 5, 6, 7, 8, 9)
    ROWS_AT, TURN_AT, K_AT, Q_AT = ROW_UNITS[0], 11, 12, 14
    GN_AT = HEADS - 3
    VECTOR_LOWS = (0, 12, 14)
    POOL_LOWS = [n for n in range(UNITS) if n not in VECTOR_LOWS]
    ADD_AT, INV_AT, SPREAD_AT = 1, 6, 0
    with ExitStack() as ctx:
        def sb(name, shape, dt=F32):
            return ctx.enter_context(nc.sbuf_tensor(name, shape, dt))

        def signal(name, per=None, head=0):
            return Signal(ctx.enter_context(nc.semaphore(name)), per, head)

        q_w = sb("q_w", [P, CT, PAIRS, P])
        k_w = sb("k_w", [P, CT, PAIRS, P])
        v_w = sb("v_w", [P, CT, C])
        proj_w = sb("proj_w", [P, PAIRS, C])
        proj_b = sb("proj_b", [P, CT])
        with nc.sbuf_tensor("qk_rows", [P, 2 * PAIRS, C], F32) as qk_rows, \
                nc.sbuf_tensor("v_rows", [P, CT, C], F32) as v_rows, \
                nc.sbuf_tensor("proj_rows", [P, CT, HEADS, 64], F32) as proj_rows:
            with nc.semaphore("pad_zero") as pad_zero, nc.Block() as block:
                @block.vector
                def _(dve):
                    nc.vector.memset(proj_rows[:, :, :, :], 0.0).then_inc(pad_zero, 1)
                    nc.vector.memset(qk_rows[:, :, :], 0.0).then_inc(pad_zero, 1)
                    dve.wait_ge(pad_zero, 2)
            pieces, loads = [], [(v_rows[:, :, :], w_qkv[2 * C:3 * C].rearrange("(r p) c -> p r c", p=P)),
                                 (proj_b[:, :], b_proj.rearrange("(p t) -> p t", t=CT))]
            for which in range(2):
                for odd in range(2):
                    loads.append((qk_rows[64 * odd:64 * odd + HEAD, which * PAIRS:(which + 1) * PAIRS, :],
                                  w_qkv[which * C:(which + 1) * C].rearrange("(j s d) c -> s d j c", s=2, d=HEAD)[odd]))
            for m in range(CT):
                loads.append((proj_rows[:, m, :, 0:HEAD], w_proj.rearrange("(p m) (h d) -> m p h d", m=CT, d=HEAD)[m]))
            for t in range(CT):
                for w, first in ((q_w, 0), (k_w, PAIRS)):
                    pieces.append(([qk_rows[:, first + j, t::CT] for j in range(PAIRS)],
                                   w[:, t, :, :].rearrange("p a b -> p (a b)")))
                pieces.append(([v_rows[:, r, t::CT] for r in range(CT)], v_w[:, t, :]))
            for pair in range(PAIRS):
                pieces.append(([proj_rows[:, m, 2 * pair:2 * pair + 2, :].rearrange("p a b -> p (a b)")
                                for m in range(CT)], proj_w[:, pair, :]))
            turn_weights(nc, "w0", const["ident"], pieces, loads)

        gn = GroupNorm(nc, sb, const["turn"], "gn0")
        xin = sb("xin", [P, CT * T])
        xres = sb("xres", [P, CT * T])
        xn = sb("xn", [P, CT, T])
        q_all = sb("q_all", [P, SLOTS, T], F32R)
        k_hi = sb("k_hi", [P, SLOTS, T], F32R)
        k_lo = sb("k_lo", [P, SLOTS, T], F32R)
        v = sb("v", [P, KEYS, HEADS, P], F32R)
        MAX_ROW = 96
        maxima = sb("maxima", [P, MAX_ROW + KEYS], F32R)
        max_row = sb("max_row", [P, T], F32R)
        probs = sb("probs", [P, RING, HALF])
        probs_hi = sb("probs_hi", [P, RING, HALF], F32R)
        probs_lo = sb("probs_lo", [P, RING, HALF], F32R)
        o_raw = sb("o_raw", [P, 2, T])
        sums_cols = sb("sums_cols", [P, KEYS])
        inv_cols = sb("inv_cols", [P, KEYS])
        inv_rows = sb("inv_rows", [P, T])
        spread = sb("spread", [P, P])
        heads_out = sb("heads_out", [P, PAIRS, T])
        ident_r = sb("ident_r", [P, P], F32R)

        s_psum = ctx.enter_context(nc.psum_tensor("s_psum", [P, 2, HALF], F32))
        o_psum = ctx.enter_context(nc.psum_tensor("o_psum", [P, 2, HALF], F32))
        m_psum = ctx.enter_context(nc.psum_tensor("m_psum", [P, 4, HALF], F32))

        x_loaded, res_loaded, stored, max_placed = (ctx.enter_context(nc.semaphore(n)) for n in
                                                    ("x_loaded", "res_loaded", "stored", "max_placed"))
        sums_moved, inv_moved = (ctx.enter_context(nc.semaphore(n)) for n in ("sums_moved", "inv_moved"))
        xin_free = signal("xin_free")
        step = signal("step", 10, 10)
        act_step = signal("act_step", 1, 1)
        gn_moments, gn_groups, gn_var, gn_rstd = (signal(n, 1, 1) for n in ("gn_moments", "gn_groups", "gn_var", "gn_rstd"))
        xn_ready = signal("xn_ready", CT, CT)
        v_made = signal("v_made", KEYS, KEYS)
        v_kept = signal("v_kept", KEYS, KEYS)
        qk_made = signal("qk_made", 2 * PAIRS, 2)
        qk_high = signal("qk_high", 4 * PAIRS, 4)
        k_again = signal("k_again", 2 * PAIRS, 2)
        qk_low = signal("qk_low", 4 * PAIRS, 4)
        rows_made = signal("rows_made", KEYS * HEADS, KEYS)
        rows_max = signal("rows_max", KEYS * HEADS, KEYS)
        max_turned = signal("max_turned", HEADS, 1)
        max_copied = signal("max_copied", HEADS, 1)
        scored = signal("scored", N, LAG)
        exped = signal("exped", N)
        vector_low = signal("vector_low", HEADS * len(VECTOR_LOWS))
        pool_low = signal("pool_low", HEADS * len(POOL_LOWS))
        weighed = signal("weighed", N, RING)
        o_copied = signal("o_copied", 2 * HEADS)
        o_added = signal("o_added", 2 * HEADS, 2)
        inverted = signal("inverted", HEADS)
        inv_spread = signal("inv_spread", PAIRS)
        pair_done = signal("pair_done", PAIRS, 2)
        v_low = signal("v_low", KEYS, KEYS)
        projected = signal("projected", 2 * CT)
        y_made = signal("y_made", 2 * CT, 2 * CT)
        filled = signal("filled")
        turned_ident = signal("turned_ident")

        def slot(n):
            return m_psum[:, 2 * n:2 * n + 2, :].rearrange("p a b -> p (a b)")

        def nth(number, per_one, i):
            return (number - (i is not None)) * per_one

        block = ctx.enter_context(nc.Block())

        @block.sync
        def _(sp):
            sp.sem_inc(stored, 16)

            def place_max(g, i):
                sp.wait_ge(max_copied.sem, max_copied.at(nth(g, 1, i) + 1, i))
                sp.dma_start(as_f32(q_all[HEAD:HEAD + 1, g % SLOTS, :]), as_f32(max_row[MAX_ROW:MAX_ROW + 1, :])).then_inc(max_placed, 16)

            def move_sums(h, i):
                row = 64 * (h % 2)
                sp.wait_ge(o_added.sem, o_added.at(2 * h + 2, i))
                sp.dma_start(sums_cols[:, :], o_raw[row + HEAD:row + HEAD + 1, h // 2 % 2, :].rearrange("a (p j) -> a p j", j=KEYS)).then_inc(sums_moved, 16)
                sp.wait_ge(inverted.sem, inverted.at(h + 1, i))
                sp.dma_start(inv_rows[row:row + 1, :].rearrange("a (p j) -> a p j", j=KEYS), inv_cols[:, :]).then_inc(inv_moved, 16)

            place_max(0, None)
            with sp.Fori(0, B) as i:
                sp.wait_ge(stored, i * 16 + 16)
                sp.dma_start(xres[:, :], x_in[bass.ds(i, 1)].rearrange("a (p t) n -> p (a t n)", t=CT)).then_inc(res_loaded, 16)
                for h in range(HEADS):
                    if h > 0:
                        move_sums(h - 1, i)
                    place_max(h + 1, i)
                move_sums(HEADS - 1, i)
                sp.wait_ge(y_made.sem, y_made.at(2 * CT, i))
                sp.dma_start(x_out[bass.ds(i, 1)].rearrange("a (p t) n -> p (a t n)", t=CT), xres[:, :]).then_inc(stored, 16)
            sp.wait_ge(stored, 16 * B + 16)
            sp.wait_ge(max_placed, 16 * (HEADS * B + 1))
            sp.wait_ge(sums_moved, 16 * HEADS * B)
            sp.wait_ge(inv_moved, 16 * HEADS * B)

        @block.gpsimd
        def _(pool):
            pool.dma_start(xin[:, :], x_in[0:1].rearrange("a (p t) n -> p (a t n)", t=CT)).then_inc(x_loaded, 16)
            pool.memset(as_f32(k_lo[:, :, :]), 0.0).then_inc(filled.next(), 1)
            pool.memset(as_f32(maxima[:, :]), 0.0).then_inc(filled.next(), 1)
            pool.memset(as_f32(v[:, :, :, :]), 0.0).then_inc(filled.next(), 1)
            pool.memset(spread[:, :], 0.0).then_inc(filled.next(), 1)
            pool.memset(inv_rows[:, :], 0.0).then_inc(filled.next(), 1)
            pool.memset(heads_out[:, :, :], 0.0).then_inc(filled.next(), 1)
            pool.wait_ge(filled.sem, filled.at(6))
            pool.memset(spread[0:1, 0:64], 1.0).then_inc(filled.next(), 1)
            pool.memset(spread[64:65, 64:P], 1.0).then_inc(filled.next(), 1)
            pool.wait_ge(filled.sem, filled.at(8))
            pool.memset(as_f32(v[:, :, :, HEAD:64]), 1.0).then_inc(filled.next(), 1)
            pool.wait_ge(filled.sem, filled.at(9))
            pool.memset(as_f32(k_lo[32:64, :, :]), 1.0).then_inc(filled.next(), 1)
            pool.wait_ge(xin_free.sem, 1)
            pool.dma_start(xin[:, :], x_in[1 % B:1 % B + 1].rearrange("a (p t) n -> p (a t n)", t=CT)).then_inc(x_loaded, 16)
            with pool.Fori(0, B) as i:
                for h in range(HEADS):
                    for n in range(UNITS):
                        u = h * UNITS + n
                        if n in POOL_LOWS:
                            pool.wait_ge(exped.sem, exped.at(u + 1, i))
                            pool.tensor_tensor(probs_lo[:, u % RING, :], probs[:, u % RING, :], as_f32(probs_hi[:, u % RING, :]),
                                               ALU.subtract).then_inc(pool_low.next(), 1)
                        if h == GN_AT + 1 and n == ROWS_AT + 1:
                            pool.wait_ge(xin_free.sem, i + 2)
                            pool.dma_start(xin[:, :], x_in[bass.ds((i + 2) % B, 1)].rearrange("a (p t) n -> p (a t n)", t=CT)).then_inc(x_loaded, 16)
            assert filled.count == ALL_FILLED
            pool_low.end_of_pass()
            pool.wait_ge(x_loaded, 16 * (B + 2))

        @block.scalar
        def _(act):

            def split(pair, part, i):
                at = nth(pair, 1, i)
                act.wait_ge(qk_made.sem, qk_made.at(2 * at + part + 1, i))
                for odd in range(2):
                    target = (k_hi, q_all)[part][0:64, (2 * pair + odd) % SLOTS, :]
                    nc.scalar.copy(target, slot(part)[64 * odd:64 * odd + 64, :]).then_inc(qk_high.next(), 1)
                if part == 0:
                    act.wait_ge(qk_high.sem, qk_high.at(4 * at + 2, i))
                    for odd in range(2):
                        s = (2 * pair + odd) % SLOTS
                        nc.scalar.copy(k_hi[64:128, s, :], as_f32(k_hi[0:64, s, :])).then_inc(k_again.next(), 1)

            def copy_max(g, i):
                at = nth(g, 1, i)
                act.wait_ge(max_turned.sem, max_turned.at(at + 1, i))
                if i is not None:
                    act.wait_ge(max_placed, (i * HEADS + g) * 16)
                nc.scalar.copy(max_row[MAX_ROW:MAX_ROW + 1, :], slot(0)[MAX_ROW:MAX_ROW + 1, :]).then_inc(max_copied.next(), 1)

            def copy_out(h, half, i):
                row = 64 * (h % 2)
                act.wait_ge(weighed.sem, weighed.at((h + 1) * UNITS - 1 + half, i))
                if half == 0 and h % 2 == 0:
                    act.wait_ge(pair_done.sem, pair_done.at(h // 2 - 1, i))
                nc.scalar.copy(o_raw[row:row + 64, h // 2 % 2, half * HALF:(half + 1) * HALF], o_psum[0:64, half, :]).then_inc(o_copied.next(), 1)

            def keep_values(i):
                for tile in range(KEYS):
                    act.wait_ge(v_made.sem, v_made.at(tile + 1, i))
                    nc.scalar.copy(v[:, tile, :, 0:HEAD], m_psum[:, 2 * (tile % 2), 0:C].rearrange(
                        "p (h d) -> p h d", d=HEAD)).then_inc(v_kept.next(), 1)

            def group_rstd(i):
                act.wait_ge(gn_var.sem, gn_var.at(1, i))
                gn.scalar_rstd(act, act_step, i, gn_rstd)

            nc.scalar.copy(ident_r[:, :], const["ident"]).then_inc(turned_ident.next(), 1)
            group_rstd(None)
            for part in range(2):
                split(0, part, None)
            copy_max(0, None)
            act.wait_ge(filled.sem, filled.at(ALL_FILLED))
            keep_values(None)
            with act.Fori(0, B) as i:
                for h in range(HEADS):
                    for n in range(UNITS):
                        u = h * UNITS + n
                        act.wait_ge(scored.sem, scored.at(u + 1 - LAG, i))
                        act.wait_ge(weighed.sem, weighed.at(u + 1 - RING, i))
                        nc.scalar.activation(probs_hi[:, u % RING, :], s_psum[:, u % 2, :], ACT.Exp, scale=SCALE)
                        nc.scalar.activation(probs[:, u % RING, :], s_psum[:, u % 2, :], ACT.Exp, scale=SCALE).then_inc(exped.next(), 1)
                        if h % 2 == 0 and n in (K_AT + 1, Q_AT + 1):
                            split(h // 2 + 1, int(n == Q_AT + 1), i)
                        if n == TURN_AT:
                            copy_max(h + 1, i)
                        if n == 1 and h > 0:
                            copy_out(h - 1, 1, i)
                        if n == 0 and h > 0:
                            copy_out(h - 1, 0, i)
                        if h == GN_AT and n == UNITS - 3:
                            group_rstd(i)
                copy_out(HEADS - 1, 0, i)
                copy_out(HEADS - 1, 1, i)
                keep_values(i)
            for s in (act_step, gn_rstd, v_kept, qk_high, k_again, max_copied, exped, o_copied):
                s.end_of_pass()

        @block.vector
        def _(dve):
            dve.sem_inc(*pair_done.lead())
            dve.sem_inc(*o_added.lead())
            dve.sem_inc(*y_made.lead())
            dve.wait_ge(filled.sem, filled.at(ALL_FILLED))

            def moments(i):
                dve.wait_ge(x_loaded, 16 if i is None else i * 16 + 32)
                gn.vector_moments(dve, xin[:, :], step, i, gn_moments)

            def variance(i):
                dve.wait_ge(gn_groups.sem, gn_groups.at(1, i))
                gn.vector_variance(dve, m_psum[:, 2, 0:2], step, i, gn_var)

            def normalise(t, i):
                if t == 0:
                    dve.wait_ge(gn_rstd.sem, gn_rstd.at(1, i))
                    gn.vector_shift(dve, step, i)
                nc.vector.tensor_scalar(xn[:, t, :], xin[:, t * T:(t + 1) * T], gn.rstd[:, :], gn.shift[:, :],
                                        ALU.mult, ALU.add).then_inc(xn_ready.next(), 1)
                if t == CT - 1:
                    dve.wait_ge(xn_ready.sem, xn_ready.at(CT, i))
                    dve.sem_inc(xin_free.sem, 1)

            def split(pair, part, i):
                at = nth(pair, 1, i)
                for odd in range(2):
                    s = (2 * pair + odd) % SLOTS
                    dve.wait_ge(qk_high.sem, qk_high.at(4 * at + 2 * part + odd + 1, i))
                    rows = HEAD if part == 0 else 64
                    source = slot(part)[64 * odd:64 * odd + rows, :]
                    if part == 1:
                        nc.vector.tensor_tensor(q_all[64:128, s, :], source, as_f32(q_all[0:64, s, :]),
                                                ALU.subtract).then_inc(qk_low.next(), 1)
                    else:
                        nc.vector.tensor_tensor(k_lo[0:HEAD, s, :], source, as_f32(k_hi[0:HEAD, s, :]),
                                                ALU.subtract).then_inc(qk_low.next(), 1)

            def row_max(g, tile, i):
                dve.wait_ge(rows_made.sem, rows_made.at(nth(g, KEYS, i) + tile + 1, i))
                nc.vector.tensor_reduce(maxima[:, MAX_ROW + tile:MAX_ROW + tile + 1], slot(tile % 2),
                                        AX.X, ALU.max, negate=True).then_inc(rows_max.next(), 1)

            def low_values(tile, i):
                dve.wait_ge(v_kept.sem, v_kept.at(tile + 1, i))
                source = m_psum[:, 2 * (tile % 2), 0:C].rearrange("p (h d) -> p h d", d=HEAD)
                nc.vector.tensor_tensor(v[:, tile, :, 64:64 + HEAD], source, as_f32(v[:, tile, :, 0:HEAD]),
                                        ALU.subtract).then_inc(v_low.next(), 1)

            def add_low(h, half, i):
                row = 64 * (h % 2)
                at = o_raw[row:row + 64, h // 2 % 2, half * HALF:(half + 1) * HALF]
                dve.wait_ge(o_copied.sem, o_copied.at(2 * h + half + 1, i))
                nc.vector.tensor_tensor(at, o_psum[64:128, half, :], at, ALU.add).then_inc(o_added.next(), 1)

            def invert(h, i):
                dve.wait_ge(sums_moved, i * (16 * HEADS) + (h + 1) * 16)
                if h > 0:
                    dve.wait_ge(inv_moved, i * (16 * HEADS) + h * 16)
                nc.vector.reciprocal(inv_cols[:, :], sums_cols[:, :]).then_inc(inverted.next(), 1)

            def divide(pair, at, i):
                dve.wait_ge(inv_spread.sem, inv_spread.at(pair + 1, i))
                nc.vector.tensor_tensor(heads_out[:, pair, :], o_raw[:, pair % 2, :], slot(at), ALU.mult).then_inc(pair_done.next(), 1)

            moments(None)
            variance(None)
            for t in range(CT):
                normalise(t, None)
            split(0, 0, None)
            split(0, 1, None)
            for tile in range(KEYS):
                row_max(0, tile, None)
            for tile in range(KEYS):
                low_values(tile, None)
            with dve.Fori(0, B) as i:
                for h in range(HEADS):
                    for n in range(UNITS):
                        if h == GN_AT and n == 0:
                            moments(i)
                        if h == GN_AT and n == UNITS - 4:
                            variance(i)
                        if h == GN_AT and n in (UNITS - 2, UNITS - 1):
                            normalise(n - UNITS + 2, i)
                        if h == GN_AT + 1 and n == ROWS_AT - 1:
                            normalise(2, i)
                        if h % 2 == 0 and n in (K_AT + 1, Q_AT + 1):
                            split(h // 2 + 1, int(n == Q_AT + 1), i)
                        if h > 1 and h % 2 and n == SPREAD_AT + 1:
                            divide(h // 2 - 1, 0, i)
                        if h > 0 and n in (ADD_AT, ADD_AT + 1):
                            add_low(h - 1, n - ADD_AT, i)
                        if n in ROW_UNITS:
                            row_max(h + 1, ROW_UNITS.index(n), i)
                        if h > 0 and n == INV_AT:
                            invert(h - 1, i)
                        if n in VECTOR_LOWS:
                            u = h * UNITS + n
                            dve.wait_ge(exped.sem, exped.at(u + 1, i))
                            nc.vector.tensor_tensor(probs_lo[:, u % RING, :], probs[:, u % RING, :], as_f32(probs_hi[:, u % RING, :]),
                                                    ALU.subtract).then_inc(vector_low.next(), 1)
                add_low(HEADS - 1, 0, i)
                add_low(HEADS - 1, 1, i)
                for tile in range(KEYS):
                    low_values(tile, i)
                    if tile == KEYS // 2:
                        invert(HEADS - 1, i)
                divide(PAIRS - 1, 1, i)
                dve.wait_ge(res_loaded, i * 16 + 16)
                for n in range(2 * CT):
                    m, half = n // 2, n % 2
                    dve.wait_ge(projected.sem, projected.at(n + 1, i))
                    cols = slice(m * T + half * HALF, m * T + (half + 1) * HALF)
                    nc.vector.scalar_tensor_tensor(xres[:, cols], m_psum[:, n % 4, :], proj_b[:, m:m + 1], xres[:, cols],
                                                   ALU.add, ALU.add).then_inc(y_made.next(), 1)
            for s in (step, gn_moments, gn_var, xn_ready, qk_low, rows_max, vector_low, o_added, v_low, inverted, pair_done, y_made):
                s.end_of_pass()

        @block.tensor
        def _(pe):
            pe.sem_inc(*weighed.lead())
            pe.wait_ge(filled.sem, filled.at(ALL_FILLED))
            pe.wait_ge(turned_ident.sem, turned_ident.at(1))

            def groups(i):
                pe.wait_ge(gn_moments.sem, gn_moments.at(1, i))
                gn.tensor_groups(pe, m_psum[:, 2, 0:2], const["group_mean"]).then_inc(gn_groups.next(), 1)

            def values(i):
                for tile in range(KEYS):
                    if tile >= 2:
                        pe.wait_ge(v_low.sem, v_low.at(tile - 1, i))
                    for t in range(CT):
                        ins = nc.tensor.matmul(m_psum[:, 2 * (tile % 2), 0:C], xn[:, t, tile * P:(tile + 1) * P],
                                               v_w[:, t, :], start=(t == 0), stop=(t == CT - 1))
                    ins.then_inc(v_made.next(), 1)

            def project_qk(pair, part, i):
                w = (k_w, q_w)[part]
                for half in range(2):
                    for t in range(CT):
                        ins = nc.tensor.matmul(m_psum[:, 2 * part + half, :], w[:, t, pair % PAIRS, :],
                                               xn[:, t, half * HALF:(half + 1) * HALF], start=(t == 0), stop=(t == CT - 1))
                ins.then_inc(qk_made.next(), 1)

            def row_scores(g, tile, i):
                if tile == 0:
                    pair = nth(g // 2, 1, i)
                    pe.wait_ge(qk_low.sem, qk_low.at(4 * pair + 4, i))
                    pe.wait_ge(k_again.sem, k_again.at(2 * pair + 2, i))
                if tile >= 2:
                    pe.wait_ge(rows_max.sem, rows_max.at(nth(g, KEYS, i) + tile - 1, i))
                for half in range(2):
                    ins = nc.tensor.matmul(m_psum[:, 2 * (tile % 2) + half, :],
                                           q_all[:, g % SLOTS, tile * P:(tile + 1) * P],
                                           k_hi[:, g % SLOTS, half * HALF:(half + 1) * HALF], start=True, stop=True)
                ins.then_inc(rows_made.next(), 1)

            def turn_max(g, i):
                pe.wait_ge(rows_max.sem, rows_max.at(nth(g, KEYS, i) + KEYS, i))
                for tile in range(KEYS):
                    ins = nc.tensor.matmul(m_psum[0:MAX_ROW + 1, tile // 4, (tile % 4) * P:(tile % 4 + 1) * P],
                                           maxima[:, tile:tile + MAX_ROW + 1], ident_r[:, :], start=True, stop=True)
                ins.then_inc(max_turned.next(), 1)

            def scores(u, i):
                h, n = u // UNITS, u % UNITS
                tile, half = n // 2, n % 2
                if n == 0:
                    pe.wait_ge(max_placed, 16 if i is None else (i * HEADS + h + 1) * 16)
                if i is not None:
                    pe.wait_ge(exped.sem, exped.at(u - 1, i))
                q = q_all[:, h % SLOTS, half * HALF:(half + 1) * HALF]
                keys = slice(tile * P, (tile + 1) * P)
                nc.tensor.matmul(s_psum[:, u % 2, :], k_hi[:, h % SLOTS, keys], q, start=True, stop=False)
                nc.tensor.matmul(s_psum[:, u % 2, :], k_lo[:, h % SLOTS, keys], q, start=False, stop=True).then_inc(scored.next(), 1)

            def weigh(u, i):
                h, n = u // UNITS, u % UNITS
                tile, half = n // 2, n % 2
                if n < 2:
                    pe.wait_ge(o_added.sem, o_added.at(2 * (h - 1) + n + 1, i))
                if u == 0:
                    pe.wait_ge(v_low.sem, v_low.at(0, i))
                pe.wait_ge(exped.sem, exped.at(u + 1, i))
                nc.tensor.matmul(o_psum[:, half, :], v[:, tile, h, :], probs_hi[:, u % RING, :], start=(tile == 0), stop=False)
                if n in VECTOR_LOWS:
                    pe.wait_ge(vector_low.sem, vector_low.at(h * len(VECTOR_LOWS) + VECTOR_LOWS.index(n) + 1, i))
                else:
                    pe.wait_ge(pool_low.sem, pool_low.at(h * len(POOL_LOWS) + POOL_LOWS.index(n) + 1, i))
                nc.tensor.matmul(o_psum[:, half, :], v[:, tile, h, :], probs_lo[:, u % RING, :], start=False,
                                 stop=(tile == KEYS - 1)).then_inc(weighed.next(), 1)

            def spread_inverses(pair, at, i):
                pe.wait_ge(inv_moved, i * (16 * HEADS) + 16 * (2 * pair + 2))
                for half in range(2):
                    ins = nc.tensor.matmul(m_psum[:, 2 * at + half, :], spread[:, :], inv_rows[:, half * HALF:(half + 1) * HALF],
                                           start=True, stop=True)
                ins.then_inc(inv_spread.next(), 1)

            groups(None)
            pe.wait_ge(xn_ready.sem, xn_ready.at(CT))
            project_qk(0, 0, None)
            project_qk(0, 1, None)
            for tile in range(KEYS):
                row_scores(0, tile, None)
            turn_max(0, None)
            pe.wait_ge(max_copied.sem, max_copied.at(1))
            values(None)
            for u in range(LAG):
                scores(u, None)
            with pe.Fori(0, B) as i:
                for u in range(N):
                    h, n = u // UNITS, u % UNITS
                    if n in ROW_UNITS:
                        if n == ROWS_AT and h == 0:
                            pe.wait_ge(y_made.sem, y_made.at(0, i))
                        if n == ROWS_AT and h == GN_AT + 1:
                            pe.wait_ge(gn_var.sem, gn_var.at(1, i))
                        if n == ROWS_AT and h % 2:
                            pe.wait_ge(pair_done.sem, pair_done.at(h // 2, i))
                        if n == ROWS_AT and h % 2 == 0:
                            pe.wait_ge(max_copied.sem, max_copied.at(h, i))
                        row_scores(h + 1, ROW_UNITS.index(n), i)
                    if n == TURN_AT:
                        turn_max(h + 1, i)
                    if h % 2 == 0 and n == K_AT:
                        pe.wait_ge(max_copied.sem, max_copied.at(h + 1, i))
                        if h == HEADS - 2:
                            pe.wait_ge(xn_ready.sem, xn_ready.at(CT, i))
                        project_qk(h // 2 + 1, 0, i)
                    if h % 2 == 0 and n == Q_AT:
                        project_qk(h // 2 + 1, 1, i)
                    if h == GN_AT and n == UNITS - 5:
                        groups(i)
                    if h > 1 and h % 2 and n == SPREAD_AT:
                        pe.wait_ge(qk_low.sem, qk_low.at(4 * (h // 2) + 2, i))
                        spread_inverses(h // 2 - 1, 0, i)
                    scores(u + LAG, i)
                    if u > 0:
                        weigh(u - 1, i)
                weigh(N - 1, i)
                pe.wait_ge(max_copied.sem, max_copied.at(HEADS, i))
                values(i)
                pe.wait_ge(v_low.sem, v_low.at(KEYS, i))
                spread_inverses(PAIRS - 1, 1, i)
                for n in range(2 * CT):
                    m, half = n // 2, n % 2
                    if n == 2:
                        pe.wait_ge(pair_done.sem, pair_done.at(PAIRS, i))
                    if n >= 4:
                        pe.wait_ge(y_made.sem, y_made.at(n - 3, i))
                    for pair in range(PAIRS):
                        if n == 0 and pair == PAIRS - 1:
                            pe.wait_ge(pair_done.sem, pair_done.at(PAIRS, i))
                        ins = nc.tensor.matmul(m_psum[:, n % 4, :], proj_w[:, pair, m * P:(m + 1) * P],
                                               heads_out[:, pair, half * HALF:(half + 1) * HALF],
                                               start=(pair == 0), stop=(pair == PAIRS - 1))
                    ins.then_inc(projected.next(), 1)
            for s in (gn_groups, v_made, qk_made, rows_made, max_turned, scored, weighed, inv_spread, projected):
                s.end_of_pass()


class ChannelNorm:

    def __init__(self, nc, inv, mean_psum, var_psum, col_mean, eps):
        self.nc, self.mean_psum, self.var_psum, self.col_mean = nc, mean_psum, var_psum, col_mean
        self.inv = inv
        self.eps = eps

    def tensor_sum(self, psum, x, half):
        for t in range(CT):
            ins = self.nc.tensor.matmul(psum[:, half, :], self.col_mean, x[:, t, half * HALF:(half + 1) * HALF],
                                        start=(t == 0), stop=(t == CT - 1))
        return ins

    def over_tiles(self, ap):
        return ap.unsqueeze(1).broadcast_to([P, CT, HALF])

    def vector_centre(self, x, half):
        cols = x[:, :, half * HALF:(half + 1) * HALF]
        return self.nc.vector.tensor_tensor(cols, cols, self.over_tiles(self.mean_psum[:, half, :]), ALU.subtract)

    def scalar_square(self, squares, x, half):
        cols = slice(half * HALF, (half + 1) * HALF)
        return self.nc.scalar.activation(squares[:, :, cols], x[:, :, cols], ACT.Square)

    def scalar_log(self, half):
        return self.nc.scalar.activation(self.inv[:, half, :], self.var_psum[:, half, :], ACT.Ln, bias=self.eps)

    def scalar_exp(self, half):
        return self.nc.scalar.activation(self.inv[:, half, :], self.inv[:, half, :], ACT.Exp, scale=-0.5)

    def vector_scale(self, x, half):
        cols = x[:, :, half * HALF:(half + 1) * HALF]
        return self.nc.vector.tensor_tensor(cols, cols, self.over_tiles(self.inv[:, half, :]), ALU.mult)


def s5_constants(nc, lam, log_step, tables, decay, gain, keep):
    Q, J = lam.shape[0], 2
    TURN = 6.283185
    TO_ONE = 12582912.0
    TO_HIGH = 1536.0
    with ExitStack() as ctx:
        def sb(name, shape, dt=F32):
            return ctx.enter_context(nc.sbuf_tensor(name, shape, dt))[tuple(slice(None) for _ in shape)]
        count = sb("count", [Q, T], mybir.dt.int32)
        t = sb("times", [Q, T])
        high, low, whole = (sb(n, [Q, T]) for n in ("turn_high", "turn_low", "turn_whole"))
        step, a, f, f_high, f_low, r, s1, s2 = (sb("s5_" + n, [Q, J]) for n in ("step", "a", "f", "fh", "fl", "r", "s1", "s2"))
        trig = sb("s5_trig", [Q, 2, J])
        eps = sb("s5_c", [Q, 4, J])
        counted = Signal(ctx.enter_context(nc.semaphore("counted")))
        v = Signal(ctx.enter_context(nc.semaphore("s5_v")))
        s = Signal(ctx.enter_context(nc.semaphore("s5_s")))
        block = ctx.enter_context(nc.Block())
        V, re, im = nc.vector, lam[:, :, 0], lam[:, :, 1]

        @block.gpsimd
        def _(pool):
            pool.iota(count, pattern=[[1, T]], base=0, channel_multiplier=0).then_inc(counted.next(), 1)

        TRIG = 10
        table_ready = [TRIG + 1 + 10 * (n // 2) + 4 + 3 * (n % 2 + 1) for n in range(2 * J)]

        @block.scalar
        def _(act):
            nc.scalar.activation(step, log_step, ACT.Exp).then_inc(s.next(), 1)
            act.wait_ge(s.sem, s.at(s.count))
            act.wait_ge(v.sem, v.at(1))
            nc.scalar.activation(r, a, ACT.Exp).then_inc(s.next(), 1)
            act.wait_ge(s.sem, s.at(s.count))
            act.wait_ge(v.sem, v.at(TRIG))
            nc.scalar.activation(trig, trig, ACT.Sin, scale=TURN).then_inc(s.next(), 1)
            act.wait_ge(s.sem, s.at(s.count))
            for n in range(2 * J):
                act.wait_ge(v.sem, v.at(table_ready[n]))
                nc.scalar.activation(tables[:, n % 2, n // 2, :], tables[:, n % 2, n // 2, :], ACT.Sin, scale=TURN).then_inc(s.next(), 1)

        @block.vector
        def _(dve):
            def do(ins):
                ins.then_inc(v.next(), 1)
                dve.wait_ge(v.sem, v.at(v.count))
            dve.wait_ge(s.sem, s.at(1))
            do(V.tensor_tensor(a, re, step, ALU.mult))
            do(V.tensor_tensor(f, im, step, ALU.mult))
            do(V.tensor_scalar(f, f, 1.0 / (2.0 * np.pi), None, ALU.mult))
            do(V.tensor_scalar(trig[:, 0, :], f, 0.25, None, ALU.add))
            do(V.tensor_scalar(s1, trig[:, 0, :], TO_ONE, TO_ONE, ALU.add, ALU.subtract))
            do(V.tensor_tensor(trig[:, 0, :], trig[:, 0, :], s1, ALU.subtract))
            do(V.tensor_scalar(s1, f, TO_ONE, TO_ONE, ALU.add, ALU.subtract))
            do(V.tensor_tensor(trig[:, 1, :], f, s1, ALU.subtract))
            do(V.tensor_scalar(f_high, f, TO_HIGH, TO_HIGH, ALU.add, ALU.subtract))
            do(V.tensor_tensor(f_low, f, f_high, ALU.subtract))
            assert v.count == TRIG
            dve.wait_ge(counted.sem, counted.at(1))
            do(V.tensor_copy(t, count))
            for j in range(J):
                do(V.tensor_scalar(high, t, f_high[:, j:j + 1], None, ALU.mult))
                do(V.tensor_scalar(whole, high, TO_ONE, TO_ONE, ALU.add, ALU.subtract))
                do(V.tensor_tensor(high, high, whole, ALU.subtract))
                do(V.scalar_tensor_tensor(high, t, f_low[:, j:j + 1], high, ALU.mult, ALU.add))
                for n, quarter in enumerate((0.25, 0.0)):
                    do(V.tensor_scalar(low, high, quarter, None, ALU.add))
                    do(V.tensor_scalar(whole, low, TO_ONE, TO_ONE, ALU.add, ALU.subtract))
                    do(V.tensor_tensor(tables[:, n, j, :], low, whole, ALU.subtract))
                    assert v.count == table_ready[2 * j + n]
            dve.wait_ge(s.sem, s.at(3))
            do(V.tensor_copy(decay, r))
            nr, ni, den = eps[:, 0, :], eps[:, 1, :], eps[:, 2, :]
            do(V.tensor_tensor(nr, r, trig[:, 0, :], ALU.mult))
            do(V.tensor_scalar(nr, nr, -1.0, None, ALU.add))
            do(V.tensor_tensor(ni, r, trig[:, 1, :], ALU.mult))
            do(V.tensor_tensor(s1, re, re, ALU.mult))
            do(V.tensor_tensor(s2, im, im, ALU.mult))
            do(V.tensor_tensor(den, s1, s2, ALU.add))
            do(V.reciprocal(den, den))
            do(V.tensor_tensor(s1, nr, re, ALU.mult))
            do(V.tensor_tensor(s2, ni, im, ALU.mult))
            do(V.tensor_tensor(s1, s1, s2, ALU.add))
            do(V.tensor_tensor(gain[:, 0, :], s1, den, ALU.mult))
            do(V.tensor_tensor(s1, ni, re, ALU.mult))
            do(V.tensor_tensor(s2, nr, im, ALU.mult))
            do(V.tensor_tensor(s1, s1, s2, ALU.subtract))
            do(V.tensor_tensor(gain[:, 1, :], s1, den, ALU.mult))
            do(V.tensor_tensor(s1, f, f, ALU.mult))
            do(V.tensor_scalar(keep[:, 0, :], s1, 0.0625, 2.0, ALU.is_lt, ALU.mult))
            do(V.tensor_scalar(keep[:, 1, :], s1, 0.0625, -2.0, ALU.is_lt, ALU.mult))


def s5_layer(nc, const, x_in, x_out, moments_out, w):
    J = 2
    Q = w["log_step"].shape[0] // J
    LN_EPS = 1e-5
    with ExitStack() as ctx:
        def sb(name, shape, dt=F32):
            return ctx.enter_context(nc.sbuf_tensor(name, shape, dt))

        def signal(name, per=None, head=0):
            return Signal(ctx.enter_context(nc.semaphore(name)), per, head)

        b_w = sb("b_w", [P, CT, 2, J, Q])
        c_w = sb("c_w", [Q, 2, J, C])
        enc_w = sb("enc_w", [P, CT, 2 * C])
        dec_w = sb("dec_w", [P, CT, C])
        rows = {n: sb(n + "_c", [P, CT]) for n in ("ln1_g", "ln1_b", "ln2_g", "ln2_b", "D")}
        tables = sb("tables", [Q, 2, J, T])
        decay = sb("decay", [Q, J])
        gain = sb("gain", [Q, 2, J])
        keep = sb("keep", [Q, 2, J])
        lam = sb("lam", [Q, J, 2])
        log_step = sb("log_step", [Q, J])
        eps = sb("eps", [P, 1])
        with nc.semaphore("params") as params, nc.Block() as block:
            small = [(lam[:, :, :], w["Lambda"].rearrange("(j q) e -> q j e", j=J)),
                     (log_step[:, :], w["log_step"].rearrange("(j q) -> q j", j=J)),
                     *[(rows[n][:, :], w[n].rearrange("(p t) -> p t", t=CT)) for n in rows]]

            @block.sync
            def _(sp):
                for tile, source in small:
                    sp.dma_start(tile, source, allow_slow_non_contiguous=True).then_inc(params, 16)
                sp.wait_ge(params, 16 * len(small))

            @block.vector
            def _(dve):
                nc.vector.memset(eps[:, :], LN_EPS)
        s5_constants(nc, lam[:, :, :], log_step[:, :], tables[:, :, :, :], decay[:, :], gain[:, :, :], keep[:, :, :])

        with nc.sbuf_tensor("b_rows", [Q, J, C, 2], F32) as b_rows, nc.sbuf_tensor("b_bar", [Q, 2, J, C], F32) as b_bar, \
                nc.sbuf_tensor("b_part", [Q, J, C], F32) as b_part, \
                nc.sbuf_tensor("c_rows", [P, CT, 2 * J * Q], F32) as c_rows, \
                nc.sbuf_tensor("enc_rows", [P, 2, CT, C], F32) as enc_rows, nc.sbuf_tensor("dec_rows", [P, CT, C], F32) as dec_rows:
            with nc.semaphore("b_loaded") as b_loaded, nc.semaphore("b_step") as b_step, nc.Block() as block:
                @block.sync
                def _(sp):
                    sp.dma_start(b_rows[:, :, :, :], w["Bmat"].rearrange("(j q) c e -> q j c e", j=J)).then_inc(b_loaded, 16)

                @block.vector
                def _(dve):
                    dve.wait_ge(b_loaded, 16)
                    n = 0
                    for j in range(J):
                        re, im = b_rows[:, j, :, 0], b_rows[:, j, :, 1]
                        g_re, g_im = gain[:, 0, j:j + 1], gain[:, 1, j:j + 1]
                        for part, a, b, sign in ((0, re, im, ALU.subtract), (1, im, re, ALU.add)):
                            nc.vector.tensor_scalar(b_part[:, j, :], b, g_im, None, ALU.mult).then_inc(b_step, 1)
                            n += 1
                            dve.wait_ge(b_step, n)
                            nc.vector.scalar_tensor_tensor(b_bar[:, part, j, :], a, g_re, b_part[:, j, :],
                                                           ALU.mult, sign).then_inc(b_step, 1)
                            n += 1
                            dve.wait_ge(b_step, n)
            pieces = []
            for t in range(CT):
                pieces.append(([b_bar[:, part, j, t::CT] for part in range(2) for j in range(J)],
                               b_w[:, t, :, :, :].rearrange("p a b c -> p (a b c)")))
                for half in range(2):
                    pieces.append(([enc_rows[:, half, m, t::CT] for m in range(CT)], enc_w[:, t, half * C:(half + 1) * C]))
                pieces.append(([dec_rows[:, m, t::CT] for m in range(CT)], dec_w[:, t, :]))
            for part in range(2):
                for j in range(J):
                    first = 2 * j * Q + part
                    pieces.append(([c_rows[:, m, first:first + 2 * Q - 1:2] for m in range(CT)], c_w[:, part, j, :]))
            loads = [(c_rows[:, :, :], w["Cmat"].rearrange("(p m) s e -> p m (s e)", m=CT)),
                     (dec_rows[:, :, :], w["W_dec"].rearrange("(p m) c -> p m c", m=CT)),
                     *[(enc_rows[:, half, :, :], w["W_enc"].rearrange("(h p m) c -> h p m c", h=2, m=CT)[half]) for half in range(2)]]
            turn_weights(nc, "w1", const["ident"], pieces, loads)
        with nc.semaphore("c_kept") as c_kept, nc.Block() as block:
            @block.vector
            def _(dve):
                for part in range(2):
                    for j in range(J):
                        nc.vector.tensor_scalar(c_w[:, part, j, :], c_w[:, part, j, :], keep[:, part, j:j + 1], None, ALU.mult)

        gn = GroupNorm(nc, sb, const["turn"], "gn1")
        xin = sb("xin1", [P, CT * T])
        xres = sb("xres1", [P, CT, T])
        a = sb("a1", [P, CT, T])
        sq1 = sb("sq1", [P, CT, T])
        sq = sb("sq2", [P, CT, T])
        f1 = sb("f1", [P, CT, T])
        f = sb("f2", [P, CT, T])
        u = sb("u1", [Q, 2, J, T])
        z = sb("z1", [Q, 2, J, T])
        prod = sb("prod1", [Q, 2, 2, HALF])
        gate = sb("gate1", [P, 2, HALF])
        out_stats = sb("out_stats", [P, 6, 6])
        out_both = sb("out_both", [P, 2])
        psum = ctx.enter_context(nc.psum_tensor("psum1", [P, 4, HALF], F32))
        mean_psum = ctx.enter_context(nc.psum_tensor("mean1", [P, 2, HALF], F32))
        var_psum = ctx.enter_context(nc.psum_tensor("var1", [P, 2, HALF], F32))
        norm = ChannelNorm(nc, sb("ln_inv", [P, 2, HALF]), mean_psum, var_psum, const["col_mean"], eps[:, :])

        x_loaded, res_loaded, stored = (ctx.enter_context(nc.semaphore(n)) for n in ("x_loaded1", "res_loaded1", "stored1"))
        xin_free = signal("xin_free1")
        step = signal("step1", 10 + 4 + 8, 10 + 2)
        act_step = signal("act_step1", 1 + 4, 1 + 2)
        gn_moments, gn_groups, gn_var, gn_rstd = (signal(n + "1", 1, 1) for n in ("gn_moments", "gn_groups", "gn_var", "gn_rstd"))
        a_made = signal("a_made", 3 * CT, CT)
        averaged = signal("averaged", 4, 2)
        centred = signal("centred", 4, 2)
        squared = signal("squared", 4, 2)
        varied = signal("varied", 4, 2)
        inv_made = signal("inv_made", 4, 2)
        f_made = signal("f_made", 4 * CT, 2 * CT)
        u_product = signal("u_product", 2 * J)
        products = signal("products", 4 * 2 * J)
        sums = signal("sums", 4 * 2 * J)
        scanned = signal("scanned", 2 * J)
        y_product = signal("y_product", 2 * CT)
        y_plain = signal("y_plain", 2 * CT)
        y_gelu = signal("y_gelu", 2 * CT)
        hidden = signal("hidden", 4 * CT)
        gated = signal("gated", 2 * CT)
        hid_made = signal("hid_made", 2 * CT)
        res_added = signal("res_added", 2)
        decoded = signal("decoded", 2 * CT)
        out_made = signal("out_made", 2 * CT, 2 * CT)
        out_measured = signal("out_measured", 1)

        def cols(half):
            return slice(half * HALF, (half + 1) * HALF)

        block = ctx.enter_context(nc.Block())

        @block.sync
        def _(sp):
            sp.sem_inc(stored, 16)
            sp.dma_start(xin[:, :], x_in[0:1].rearrange("a (p t) n -> p (a t n)", t=CT)).then_inc(x_loaded, 16)
            with sp.Fori(0, B) as i:
                sp.wait_ge(xin_free.sem, i + 1)
                sp.dma_start(xin[:, :], x_in[bass.ds((i + 1) % B, 1)].rearrange("a (p t) n -> p (a t n)", t=CT)).then_inc(x_loaded, 16)
                sp.wait_ge(stored, i * 16 + 16)
                sp.dma_start(xres[:, :, :].rearrange("p t n -> p (t n)"), x_in[bass.ds(i, 1)].rearrange("a (p t) n -> p (a t n)", t=CT)).then_inc(res_loaded, 16)
                sp.wait_ge(out_measured.sem, out_measured.at(1, i))
                sp.dma_start(x_out[bass.ds(i, 1)].rearrange("a (p t) n -> p (a t n)", t=CT), xres[:, :, :].rearrange("p t n -> p (t n)")).then_inc(stored, 16)
            sp.wait_ge(stored, 16 * B + 16)
            sp.wait_ge(x_loaded, 16 * B + 16)

        @block.gpsimd
        def _(pool):
            with pool.Fori(0, B) as i:
                for way in range(2):
                    for item in range(2 * J):
                        j, half = (item // 2, item % 2) if way == 0 else (item % J, item // J)
                        for part in range(2):
                            n = (way * 2 * J + item) * 2 + part
                            pool.wait_ge(products.sem, products.at(n + 1, i))
                            pool.tensor_tensor(u[:, part, j, cols(half)], prod[:, part, 0, :],
                                                              prod[:, part, 1, :], ALU.add if part == way else ALU.subtract).then_inc(sums.next(), 1)
                pool.wait_ge(res_loaded, i * 16 + 16)
                for half in range(2):
                    pool.wait_ge(f_made.sem, f_made.at(CT * (half + 1), i))
                    pool.tensor_tensor(xres[:, :, cols(half)], xres[:, :, cols(half)], f[:, :, cols(half)], ALU.add).then_inc(res_added.next(), 1)
            for s in (sums, res_added):
                s.end_of_pass()

        @block.scalar
        def _(act):
            def group_rstd(i):
                act.wait_ge(gn_var.sem, gn_var.at(1, i))
                gn.scalar_rstd(act, act_step, i, gn_rstd)

            def squares(first, target, i):
                for half in range(2):
                    act.wait_ge(centred.sem, centred.at(first + half + 1, i))
                    norm.scalar_square(target, a, half).then_inc(squared.next(), 1)

            def inverses(first, i):
                for half in range(2):
                    act.wait_ge(varied.sem, varied.at(first + half + 1, i))
                    norm.scalar_log(half).then_inc(act_step.next(), 1)
                act.wait_ge(act_step.sem, act_step.now(i))
                for half in range(2):
                    norm.scalar_exp(half).then_inc(inv_made.next(), 1)

            group_rstd(None)
            squares(0, sq1, None)
            inverses(0, None)
            with act.Fori(0, B) as i:
                for n in range(2 * CT):
                    act.wait_ge(y_plain.sem, y_plain.at(n + 1, i))
                    at = a[:, n % CT, cols(n // CT)]
                    nc.scalar.activation(at, at, ACT.Gelu).then_inc(y_gelu.next(), 1)
                group_rstd(i)
                squares(0, sq, i)
                inverses(0, i)
                for n in range(2 * CT):
                    act.wait_ge(hidden.sem, hidden.at(2 * n + 1, i))
                    if n >= 2:
                        act.wait_ge(hid_made.sem, hid_made.at(n - 1, i))
                    nc.scalar.activation(gate[:, n % 2, :], psum[:, 2 * (n % 2), :], ACT.Gelu).then_inc(gated.next(), 1)
                    if n == 1:
                        squares(2, sq1, i)
                inverses(2, i)
            for s in (act_step, gn_rstd, squared, inv_made, y_gelu, gated):
                s.end_of_pass()

        @block.vector
        def _(dve):
            dve.sem_inc(*out_made.lead())

            def moments(i):
                dve.wait_ge(x_loaded, 16 if i is None else i * 16 + 32)
                gn.vector_moments(dve, xin[:, :], step, i, gn_moments)

            def variance(i):
                dve.wait_ge(gn_groups.sem, gn_groups.at(1, i))
                gn.vector_variance(dve, var_psum[:, 0, 0:2], step, i, gn_var)

            def group_normalise(i):
                dve.wait_ge(gn_rstd.sem, gn_rstd.at(1, i))
                gn.vector_shift(dve, step, i)
                for t in range(CT):
                    nc.vector.tensor_scalar(a[:, t, :], xin[:, t * T:(t + 1) * T], gn.rstd[:, :], gn.shift[:, :],
                                            ALU.mult, ALU.add).then_inc(a_made.next(), 1)
                dve.wait_ge(a_made.sem, a_made.now(i))
                dve.sem_inc(xin_free.sem, 1)

            def centre(first, i):
                for half in range(2):
                    dve.wait_ge(averaged.sem, averaged.at(first + half + 1, i))
                    norm.vector_centre(a, half).then_inc(centred.next(), 1)

            def scale(first, target, g, b, i):
                for half in range(2):
                    dve.wait_ge(inv_made.sem, inv_made.at(first + half + 1, i))
                    norm.vector_scale(a, half).then_inc(step.next(), 1)
                    dve.wait_ge(step.sem, step.now(i))
                    for t in range(CT):
                        nc.vector.tensor_scalar(target[:, t, cols(half)], a[:, t, cols(half)],
                                                g[:, t:t + 1], b[:, t:t + 1], ALU.mult, ALU.add).then_inc(f_made.next(), 1)

            moments(None)
            variance(None)
            group_normalise(None)
            centre(0, None)
            scale(0, f1, rows["ln1_g"], rows["ln1_b"], None)
            with dve.Fori(0, B) as i:
                def turn(n, j, half, re, im):
                    cos, sin = tables[:, 0, j, cols(half)], tables[:, 1, j, cols(half)]
                    for part, (x0, x1) in enumerate(((re, im), (im, re))):
                        if n > 0:
                            dve.wait_ge(sums.sem, sums.at(2 * (n - 1) + part + 1, i))
                        nc.vector.tensor_tensor(prod[:, part, 0, :], x0, cos, ALU.mult)
                        nc.vector.tensor_tensor(prod[:, part, 1, :], x1, sin, ALU.mult).then_inc(products.next(), 1)

                for n in range(2 * J):
                    dve.wait_ge(u_product.sem, u_product.at(n + 1, i))
                    turn(n, n // 2, n % 2, psum[0:Q, 2 * (n % 2), :], psum[0:Q, 2 * (n % 2) + 1, :])
                for j in range(J):
                    for part in range(2):
                        dve.wait_ge(sums.sem, sums.at(4 * (j + 1), i))
                        nc.vector.tensor_tensor_scan(
                            z[:, part, j, :], decay[:, j:j + 1].broadcast_to([Q, T]), u[:, part, j, :], 0.0, ALU.mult, ALU.add).then_inc(scanned.next(), 1)
                for n in range(2 * J):
                    j, half = n % J, n // J
                    dve.wait_ge(scanned.sem, scanned.at(2 * (j + 1), i))
                    turn(2 * J + n, j, half, z[:, 0, j, cols(half)], z[:, 1, j, cols(half)])
                moments(i)
                for n in range(2 * CT + 2):
                    if n < 2 * CT:
                        m, half = n % CT, n // CT
                        dve.wait_ge(y_product.sem, y_product.at(n + 1, i))
                        nc.vector.scalar_tensor_tensor(a[:, m, cols(half)], f1[:, m, cols(half)], rows["D"][:, m:m + 1],
                                                       psum[:, n % 4, :], ALU.mult, ALU.add).then_inc(y_plain.next(), 1)
                    if n >= 2:
                        m, half = (n - 2) % CT, (n - 2) // CT
                        dve.wait_ge(y_gelu.sem, y_gelu.at(n - 1, i))
                        nc.vector.tensor_tensor(a[:, m, cols(half)], a[:, m, cols(half)], f1[:, m, cols(half)], ALU.add).then_inc(a_made.next(), 1)
                dve.wait_ge(a_made.sem, a_made.at(2 * CT, i))
                variance(i)
                centre(0, i)
                scale(0, f, rows["ln2_g"], rows["ln2_b"], i)
                group_normalise(i)
                for n in range(2 * CT):
                    m, half = n % CT, n // CT
                    dve.wait_ge(gated.sem, gated.at(n + 1, i))
                    dve.wait_ge(hidden.sem, hidden.at(2 * n + 2, i))
                    nc.vector.tensor_tensor(sq[:, m, cols(half)], gate[:, n % 2, :],
                                                               psum[:, 2 * (n % 2) + 1, :], ALU.mult).then_inc(hid_made.next(), 1)
                    if n == 1:
                        centre(2, i)
                scale(2, f1, rows["ln1_g"], rows["ln1_b"], i)
                dve.wait_ge(res_added.sem, res_added.at(2, i))
                for n in range(2 * CT + 1):
                    if n < 2 * CT:
                        m, half = n // 2, n % 2
                        dve.wait_ge(decoded.sem, decoded.at(n + 1, i))
                        nc.vector.tensor_tensor(xres[:, m, cols(half)], xres[:, m, cols(half)],
                                                psum[:, n % 4, :], ALU.add).then_inc(out_made.next(), 1)
                    if n > 0:
                        last = n - 1
                        dve.wait_ge(out_made.sem, out_made.at(n, i))
                        nc.vector.bn_stats(out_stats[:, last, :], xres[:, last // 2, cols(last % 2)]).then_inc(step.next(), 1)
                dve.wait_ge(step.sem, step.now(i))
                dve.sem_inc(gn.turn, 1)
                nc.vector.bn_aggr(out_both[:, :], out_stats[:, :, :].rearrange("p a b -> p (a b)")).then_inc(step.next(), 1)
                dve.wait_ge(step.sem, step.now(i))
                nc.vector.scalar_tensor_tensor(out_both[:, 1:2], out_both[:, 0:1], out_both[:, 0:1], out_both[:, 1:2],
                                               ALU.mult, ALU.add).then_inc(step.next(), 1)
                dve.wait_ge(step.sem, step.now(i))
                nc.vector.tensor_copy(moments_out[:, bass.ds(i, 1), :].rearrange("p a b -> p (a b)"), out_both[:, :]).then_inc(out_measured.next(), 1)
            for s in (step, gn_moments, gn_var, a_made, centred, f_made, products, scanned, y_plain, hid_made, out_made, out_measured):
                s.end_of_pass()

        @block.tensor
        def _(pe):
            def groups(i):
                pe.wait_ge(gn_moments.sem, gn_moments.at(1, i))
                gn.tensor_groups(pe, var_psum[:, 0, 0:2], const["group_mean"]).then_inc(gn_groups.next(), 1)

            def means(made, i):
                for half in range(2):
                    pe.wait_ge(a_made.sem, a_made.at(made[half], i))
                    norm.tensor_sum(mean_psum, a, half).then_inc(averaged.next(), 1)

            def variances(first, source, i):
                for half in range(2):
                    pe.wait_ge(squared.sem, squared.at(first + half + 1, i))
                    norm.tensor_sum(var_psum, source, half).then_inc(varied.next(), 1)

            groups(None)
            means((CT, CT), None)
            variances(0, sq1, None)
            with pe.Fori(0, B) as i:
                pe.wait_ge(out_made.sem, out_made.at(0, i))
                for n in range(2 * J):
                    j, half = n // 2, n % 2
                    if j == 0:
                        pe.wait_ge(f_made.sem, f_made.at((half - 1) * CT, i))
                    if n >= 2:
                        pe.wait_ge(products.sem, products.at(2 * (n - 1), i))
                    for part in range(2):
                        for t in range(CT):
                            ins = nc.tensor.matmul(psum[0:Q, 2 * (n % 2) + part, :], b_w[:, t, part, j, :],
                                                   f1[:, t, cols(half)], start=(t == 0), stop=(t == CT - 1))
                    ins.then_inc(u_product.next(), 1)
                for n in range(2 * CT):
                    m, half = n % CT, n // CT
                    if m == 0:
                        pe.wait_ge(sums.sem, sums.at(4 * J + 2 * J * (half + 1), i))
                    if n >= 4:
                        pe.wait_ge(y_plain.sem, y_plain.at(n - 3, i))
                    k = 0
                    for part in range(2):
                        for j in range(J):
                            ins = nc.tensor.matmul(psum[:, n % 4, :], c_w[:, part, j, m * P:(m + 1) * P],
                                                   u[:, part, j, cols(half)], start=(k == 0), stop=(k == 2 * J - 1))
                            k += 1
                    ins.then_inc(y_product.next(), 1)
                groups(i)
                means((CT, 2 * CT), i)
                pe.wait_ge(gn_var.sem, gn_var.at(1, i))
                variances(0, sq, i)
                for n in range(2 * CT):
                    m, half = n % CT, n // CT
                    if m == 0:
                        pe.wait_ge(f_made.sem, f_made.at(CT * (half + 1), i))
                    if n >= 2:
                        pe.wait_ge(hid_made.sem, hid_made.at(n - 1, i))
                    for k, first in enumerate((C, 0)):
                        for t in range(CT):
                            ins = nc.tensor.matmul(psum[:, 2 * (n % 2) + k, :], enc_w[:, t, first + m * P:first + (m + 1) * P],
                                                   f[:, t, cols(half)], start=(t == 0), stop=(t == CT - 1))
                        ins.then_inc(hidden.next(), 1)
                    if n == 1:
                        means((3 * CT, 3 * CT), i)
                    if n == 3:
                        variances(2, sq1, i)
                pe.wait_ge(hid_made.sem, hid_made.at(2 * CT, i))
                for n in range(2 * CT):
                    m, half = n // 2, n % 2
                    if n >= 4:
                        pe.wait_ge(out_made.sem, out_made.at(n - 3, i))
                    for t in range(CT):
                        ins = nc.tensor.matmul(psum[:, n % 4, :], dec_w[:, t, m * P:(m + 1) * P], sq[:, t, cols(half)],
                                               start=(t == 0), stop=(t == CT - 1))
                    ins.then_inc(decoded.next(), 1)
            for s in (gn_groups, averaged, varied, u_product, y_product, hidden, decoded):
                s.end_of_pass()


def depthwise_layer(nc, const, x_in, x_out, both, w):
    S = 32
    TAPS = 7
    PAD = 2 * S - 1
    mid = S - 1 - TAPS // 2
    GROUP = 8
    N = B * S
    with ExitStack() as ctx:
        def sb(name, shape, dt=F32):
            return ctx.enter_context(nc.sbuf_tensor(name, shape, dt))

        def signal(name, per=None, head=0):
            return Signal(ctx.enter_context(nc.semaphore(name)), per, head)

        moments = sb("moments2", [P, B, 2])
        var, rstd, shift = (sb(n + "2", [P, B]) for n in ("var", "rstd", "shift"))
        padded_dram = nc.dram_tensor("padded_dram", [CT, P, TAPS, PAD], F32).ap()
        bias = sb("bias2", [P, CT])
        bands = sb("bands", [P, 2, GROUP, TAPS, P])
        psum = ctx.enter_context(nc.psum_tensor("psum2", [P, 4, 2, N], F32))

        with ExitStack() as inner:
            def inner_sb(name, shape):
                return inner.enter_context(nc.sbuf_tensor(name, shape, F32))

            taps = {n: inner_sb(n + "_c", [P, CT, w[n].shape[2], w[n].shape[3]]) for n in ("w77", "w53", "w35", "w7w", "w7h", "w5w", "w5h")}
            biases = {n: inner_sb(n + "_c", [P, CT]) for n in ("b77", "b53", "b35")}
            padded = inner_sb("padded", [P, CT, TAPS, PAD])
            sem = lambda n: inner.enter_context(nc.semaphore(n))
            small_loaded, tap_written = sem("small_loaded"), sem("tap_written")
            v = Signal(sem("stat_v"))
            grouped, var_made, rstd_made, tap_made = (Signal(sem(n)) for n in ("grouped2", "var_made2", "rstd_made2", "tap_made"))
            act_step = Signal(sem("act_step2"))
            block = inner.enter_context(nc.Block())

            @block.sync
            def _(sp):
                sp.wait_ge(tap_made.sem, tap_made.at(1))
                sp.dma_start(padded_dram.rearrange("t p a b -> p t (a b)"),
                             padded[:, :, :, :].rearrange("p t a b -> p t (a b)")).then_inc(tap_written, 16)
                sp.wait_ge(tap_written, 16)

            @block.scalar
            def _(act):
                for n, tile in taps.items():
                    act.dma_start(tile[:, :, :, :].rearrange("p t a b -> p (t a b)"),
                                  w[n].rearrange("(p t) e a b -> p (t e a b)", t=CT)).then_inc(small_loaded, 16)
                for n, tile in biases.items():
                    act.dma_start(tile[:, :], w[n].rearrange("(p t) -> p t", t=CT)).then_inc(small_loaded, 16)
                act.wait_ge(small_loaded, 16 * 10)
                act.wait_ge(var_made.sem, var_made.at(1))
                nc.scalar.activation(rstd[:, :], var[:, :], ACT.Ln).then_inc(act_step.next(), 1)
                act.wait_ge(act_step.sem, act_step.at(act_step.count))
                nc.scalar.activation(rstd[:, :], rstd[:, :], ACT.Exp, scale=-0.5).then_inc(rstd_made.next(), 1)

            @block.gpsimd
            def _(pool):
                pool.memset(bands[:, :, :, :, :], 0.0)

            @block.tensor
            def _(pe):
                nc.tensor.matmul(psum[:, 0, 0, 0:2 * B], const["group_mean"],
                                                   both[:, :, :].rearrange("p b e -> p (b e)"), start=True, stop=True).then_inc(grouped.next(), 1)

            @block.vector
            def _(dve):
                V = nc.vector
                V.memset(padded[:, :, :, :], 0.0).then_inc(v.next(), 1)
                dve.wait_ge(v.sem, v.at(v.count))
                dve.wait_ge(small_loaded, 16 * 10)
                V.tensor_tensor(bias[:, :], biases["b77"][:, :], biases["b53"][:, :], ALU.add).then_inc(v.next(), 1)
                dve.wait_ge(v.sem, v.at(v.count))
                V.tensor_tensor(bias[:, :], bias[:, :], biases["b35"][:, :], ALU.add).then_inc(v.next(), 1)
                dve.wait_ge(v.sem, v.at(v.count))
                V.tensor_copy(padded[:, :, :, mid:mid + 7], taps["w77"][:, :, :, :]).then_inc(v.next(), 1)
                dve.wait_ge(v.sem, v.at(v.count))
                for n, rows, columns in (("w53", 5, 3), ("w35", 3, 5)):
                    at = padded[:, :, 3 - rows // 2:4 + rows // 2, mid + 3 - columns // 2:mid + 4 + columns // 2]
                    V.tensor_tensor(at, at, taps[n][:, :, :, :], ALU.add).then_inc(v.next(), 1)
                    dve.wait_ge(v.sem, v.at(v.count))
                for down, across, size in (("w7h", "w7w", 7), ("w5h", "w5w", 5)):
                    for t in range(CT):
                        for r in range(size):
                            at = padded[:, t, 3 - size // 2 + r, mid + 3 - size // 2:mid + 4 + size // 2]
                            V.scalar_tensor_tensor(at, taps[across][:, t, 0, :], taps[down][:, t, r, :], at,
                                                               ALU.mult, ALU.add).then_inc(v.next(), 1)
                    dve.wait_ge(v.sem, v.at(v.count))
                V.tensor_copy(padded[:, :, :, 0:1], padded[:, :, :, 0:1]).then_inc(tap_made.next(), 1)
                dve.wait_ge(grouped.sem, grouped.at(1))
                V.tensor_copy(moments[:, :, :].rearrange("p b e -> p (b e)"), psum[:, 0, 0, 0:2 * B]).then_inc(v.next(), 1)
                dve.wait_ge(v.sem, v.at(v.count))
                V.tensor_tensor(var[:, :], moments[:, :, 0], moments[:, :, 0], ALU.mult).then_inc(v.next(), 1)
                dve.wait_ge(v.sem, v.at(v.count))
                V.scalar_tensor_tensor(var[:, :], moments[:, :, 1], GN_EPS, var[:, :], ALU.add, ALU.subtract).then_inc(var_made.next(), 1)
                dve.wait_ge(rstd_made.sem, rstd_made.at(1))
                V.scalar_tensor_tensor(shift[:, :], moments[:, :, 0], -1.0, rstd[:, :], ALU.mult, ALU.mult).then_inc(v.next(), 1)
                dve.wait_ge(v.sem, v.at(v.count))

        xb = sb("xb", [P, 2, B, T])
        xt = sb("xt", [P, 2, S, B, S])
        xn = sb("xn2", [P, 2, T])
        yb = sb("yb", [P, 2, T])
        bias_t = sb("bias_t", [P, 1])
        GROUPS_T = S // GROUP
        x_loaded, stored = (ctx.enter_context(nc.semaphore(n)) for n in ("x_loaded2", "stored2"))
        band_loaded = [ctx.enter_context(nc.semaphore(f"band_loaded{n}")) for n in range(2)]
        normed = signal("normed", B, B)
        turned = signal("turned", B, B)
        PAIRS = GROUP // 2
        convolved = signal("convolved", S // 2, head=2 * PAIRS)
        kept = signal("kept2", S // 2, S // 2)
        back = signal("back2", B)
        out_made = signal("out_made2", B)

        def slot(ap, t):
            if isinstance(t, int):
                return ap[:, t % 2]
            names = "b c d e"[:2 * len(ap.shape) - 5]
            return ap[:, bass.ds(t % 2, 1)].rearrange(f"p a {names} -> p (a b) {names[2:]}")

        block = ctx.enter_context(nc.Block())

        @block.sync
        def _(sp):
            sp.sem_inc(stored, 16)
            x_tiles, out_tiles = (ap.rearrange("b (p t) n -> t p b n", t=CT) for ap in (x_in, x_out))
            sp.dma_start(xb[:, 0, :, :], x_tiles[0]).then_inc(x_loaded, 16)
            with sp.Fori(0, CT) as t:
                sp.wait_ge(x_loaded, t * 16 + 16)
                sp.wait_ge(stored, t * 16 + 16)
                sp.dma_start(slot(xb, t + 1), x_tiles[bass.ds((t + 1) % CT, 1)].rearrange("a p b n -> p (a b) n")).then_inc(x_loaded, 16)
                sp.wait_ge(out_made.sem, out_made.at(B, t))
                sp.dma_start(out_tiles[bass.ds(t, 1)].rearrange("a p b n -> p (a b) n"), slot(xb, t)).then_inc(stored, 16)
            sp.wait_ge(x_loaded, 16 * CT + 16)
            sp.wait_ge(stored, 16 * CT + 16)

        @block.gpsimd
        def _(pool):
            pool.sem_inc(*convolved.lead())
            with pool.Fori(0, CT) as t:
                for g in range(GROUPS_T):
                    pool.wait_ge(convolved.sem, convolved.at((g - 1) * PAIRS, t))
                    for q in range(4):
                        target = bands[q * S:(q + 1) * S, g % 2, :, :, q * S:(q + 1) * S].rearrange("p a b c -> p (a b) c")
                        row = padded_dram[bass.ds(t, 1), q * S + g * GROUP:q * S + (g + 1) * GROUP, :, 0:S]
                        row = row.rearrange("e c a b -> (e c a) b")
                        source = bass.AP(tensor=row.tensor, offset=row.offset, ap=[[1, S], *row.ap])
                        pool.dma_start(target, source).then_inc(band_loaded[g % 2], 16)
            for s in band_loaded:
                pool.wait_ge(s, CT * GROUPS_T // 2 * 4 * 16)

        @block.scalar
        def _(act):
            act.sem_inc(*kept.lead())

            def normalise(b, t):
                if b == 0:
                    act.wait_ge(x_loaded, 16 if t is None else t * 16 + 32)
                if b >= 2:
                    act.wait_ge(turned.sem, turned.at(b - 1, t))
                source = slot(xb, 0 if t is None else t + 1)
                nc.scalar.activation(xn[:, b % 2, :], source[:, b, :], ACT.Identity,
                                     scale=rstd[:, b:b + 1], bias=shift[:, b:b + 1]).then_inc(normed.next(), 1)

            for b in range(B):
                normalise(b, None)
            with act.Fori(0, CT) as t:
                for n in range(S // 2):
                    act.wait_ge(convolved.sem, convolved.at(n + 1, t))
                    nc.scalar.copy(slot(xt, t)[:, 2 * n:2 * n + 2, :, :].rearrange("p c b h -> p (c b h)"),
                                                  psum[:, n % 4, :, :].rearrange("p c n -> p (c n)")).then_inc(kept.next(), 1)
                    if n >= S // 2 - B:
                        normalise(n - (S // 2 - B), t)
            for s in (normed, kept):
                s.end_of_pass()

        @block.vector
        def _(dve):
            def turn(b, t):
                dve.wait_ge(normed.sem, normed.at(b + 1, t))
                target = slot(xt, 0 if t is None else t + 1)
                nc.vector.transpose(target[:, :, b, :].rearrange("p j h -> p h j"),
                                    xn[:, b % 2, :].rearrange("p (h j) -> p h j", j=S)).then_inc(turned.next(), 1)

            for b in range(B):
                turn(b, None)
            for t in range(CT):
                for s in (turned, back, out_made):
                    s.start_pass()
                for b in range(B):
                    turn(b, t)
                dve.wait_ge(kept.sem, kept.at(S // 2, t))
                for b in range(B):
                    nc.vector.transpose(yb[:, b % 2, :].rearrange("p (h j) -> p h j", j=S),
                                                       slot(xt, t)[:, :, b, :].rearrange("p j h -> p h j")).then_inc(back.next(), 1)
                    dve.wait_ge(back.sem, back.now(t))
                    at = slot(xb, t)[:, b, :].rearrange("p (h j) -> p h j", j=S)
                    nc.vector.scalar_tensor_tensor(
                        at, yb[:, b % 2, :].rearrange("p (h j) -> p h j", j=S)[:, :, ::-1], bias[:, t:t + 1], at,
                        ALU.add, ALU.add).then_inc(out_made.next(), 1)
            for s in (turned, back, out_made):
                s.end_of_pass()

        @block.tensor
        def _(pe):
            with pe.Fori(0, CT) as t:
                pe.wait_ge(turned.sem, turned.at(0, t))
                for n in range(S // 2):
                    g = 2 * n // GROUP
                    if n % PAIRS == 0:
                        pe.wait_ge(band_loaded[g % 2], t * (GROUPS_T // 2 * 64) + (g // 2 + 1) * 64)
                    pe.wait_ge(kept.sem, kept.at(n - 3, t))
                    for c in range(2):
                        channel = 2 * n + c
                        out = psum[:, n % 4, c, :].rearrange("p (b h) -> p b h", h=S)
                        for k, tap in enumerate((3, 0, 1, 2, 4, 5, 6)):
                            down = tap - TAPS // 2
                            rows = slice(max(0, -down), S - max(0, down))
                            ins = nc.tensor.matmul(out[:, :, rows], bands[:, g % 2, channel % GROUP, tap, :],
                                                   slot(xt, t)[:, channel, :, rows.start + down:rows.stop + down],
                                                   start=(k == 0), stop=(k == TAPS - 1))
                    ins.then_inc(convolved.next(), 1)
            convolved.end_of_pass()


def rwkv_layer(nc, const, x_in, x_out, w):
    S, CAP, LN_EPS, NEG = 32, 40.0, 1e-5, -1e38
    SLOTS = 3
    with ExitStack() as ctx:
        def sb(name, shape, dt=F32):
            return ctx.enter_context(nc.sbuf_tensor(name, shape, dt))

        def signal(name, per=None, head=0):
            return Signal(ctx.enter_context(nc.semaphore(name)), per, head)

        lin_w = {n: sb(n + "_t", [P, CT, C]) for n in ("Wk", "Wv", "Wr", "Wo")}
        conv_w = sb("conv_t", [P, CT, 3, 4, C])
        names = ("ln_g", "ln_b", "w_param", "u", "bn_g", "bn_b", "gamma_g", "gamma_s")
        cols = {n: sb(n + "_3", [P, CT]) for n in names}
        decay = sb("decay3", [P, CT])
        cap = sb("cap3", [P, CT])
        bn_scale = sb("bn_scale", [P, CT])
        bn_minus = sb("bn_minus", [P, CT])
        eps = sb("eps3", [P, 1])
        with nc.sbuf_tensor("conv_rows", [P, CT, C * 9], F32) as conv_rows, \
                nc.sbuf_tensor("lin_rows", [P, 4, CT, C], F32) as lin_rows:
            pieces, loads = [], [(conv_rows[:, :, :], w["conv_w"].rearrange("(p m) c a b -> p m (c a b)", m=CT))]
            for n, name in enumerate(lin_w):
                loads.append((lin_rows[:, n, :, :], w[name].rearrange("(p m) c -> p m c", m=CT)))
                for t in range(CT):
                    pieces.append(([lin_rows[:, n, m, t::CT] for m in range(CT)], lin_w[name][:, t, :]))
            for name in names:
                source = w[name] if len(w[name].shape) == 1 else w[name].rearrange("a c b d -> (a c b d)")
                loads.append((cols[name][:, :], source.rearrange("(p t) -> p t", t=CT)))
            for tap in range(9):
                for t in range(CT):
                    first = t * 9 + tap
                    pieces.append(([conv_rows[:, m, first:C * 9:CT * 9] for m in range(CT)], conv_w[:, t, tap // 3, (0, 1, 3)[tap % 3], :]))
            turn_weights(nc, "w3", const["ident"], pieces, loads)
        prepared = ctx.enter_context(nc.semaphore("prepared3"))
        with nc.Block() as block:
            @block.vector
            def _(dve):
                g0, g1, g2, minus = conv_w[:, :, :, 0, :], conv_w[:, :, :, 1, :], conv_w[:, :, :, 3, :], conv_w[:, :, :, 2, :]
                nc.vector.tensor_tensor(minus, g0, g2, ALU.add).then_inc(prepared, 1)
                dve.wait_ge(prepared, 1)
                nc.vector.tensor_tensor(minus, minus, g1, ALU.subtract).then_inc(prepared, 1)
                dve.wait_ge(prepared, 2)
                nc.vector.scalar_tensor_tensor(g1, minus, 0.5, g1, ALU.mult, ALU.add).then_inc(prepared, 1)
                dve.wait_ge(prepared, 3)
                nc.vector.tensor_scalar(minus, minus, 0.5, None, ALU.mult)
        with nc.Block() as block:
            @block.scalar
            def _(act):
                nc.scalar.activation(decay[:, :], cols["w_param"][:, :], ACT.Exp).then_inc(prepared, 1)

            @block.vector
            def _(dve):
                nc.vector.memset(eps[:, :], LN_EPS)
                nc.vector.tensor_scalar(cap[:, :], cols["u"][:, :], -1.0, CAP, ALU.mult, ALU.add)
                nc.vector.tensor_scalar(bn_scale[:, :], cols["bn_g"][:, :], 1.0 / np.sqrt(1.0 + 1e-5), None, ALU.mult)
                nc.vector.tensor_scalar(bn_minus[:, :], cols["bn_g"][:, :], -1.0 / np.sqrt(1.0 + 1e-5), None, ALU.mult)
                dve.wait_ge(prepared, 4)
                nc.vector.tensor_scalar(decay[:, :], decay[:, :], -1.0, None, ALU.mult)

        gn = GroupNorm(nc, sb, const["turn"], "gn3")
        xin = sb("xin3", [P, CT * T])
        xres = sb("xres3", [P, CT, T])
        xp = sb("xp", [P, CT, S + 2, S + 2])
        k = sb("k3", [P, CT, T])
        v = sb("v3", [P, CT, T])
        h = k
        mixes = sb("mixes", [P, 4, CT, S + 2, S // 2])
        p = sb("p3", [P, T + 2])
        to_a = sb("to_a", [P, 2, T])
        to_f = sb("to_f", [P, SLOTS, T])
        to_e = sb("to_e", [P, SLOTS, T])
        num = sb("num3", [P, T + 2])
        den = sb("den3", [P, T + 2])
        sides = (xin[:, 0:T], to_f[:, 0, :], to_f[:, 1, :])
        sigmoids = to_a[:, 0, :].rearrange("p (a b) -> p a b", a=2)
        psum = ctx.enter_context(nc.psum_tensor("psum3", [P, 4, HALF], F32))
        mean_psum = ctx.enter_context(nc.psum_tensor("mean3", [P, 2, HALF], F32))
        var_psum = ctx.enter_context(nc.psum_tensor("var3", [P, 2, HALF], F32))
        norm = ChannelNorm(nc, to_a[:, 1, :].rearrange("p (a b) -> p a b", a=2), mean_psum, var_psum, const["col_mean"], eps[:, :])

        ITEMS = 2 * CT
        RING = [("kv", n) for n in range(4 * CT)] + [("conv", n) for n in range(4)] + [("gate", n) for n in range(2 * CT)] + \
            [("conv", n) for n in range(4, 4 * CT)]
        FACTOR = (1, 2, 0, 3)
        SCALAR_READS = [item for item in RING if item[0] != "conv" or item[1] % 4 == 0]
        VECTOR_READS = [item for item in RING if item not in SCALAR_READS]
        MIX = len(RING)
        assert (MIX + 2 * CT) % 4 == 0
        x_loaded, res_loaded, stored = (ctx.enter_context(nc.semaphore(n)) for n in ("x_loaded3", "res_loaded3", "stored3"))
        xin_free = signal("xin_free3")
        framed = signal("framed")
        mixes_made = signal("mixes_made", 4)
        step = signal("step3", 10 + 2 + 2 * CT, 10)
        act_step = signal("act_step3", 1 + 2 + ITEMS, 1)
        gn_moments, gn_groups, gn_var, gn_rstd, xp_made = (signal(n + "3", 1, 1) for n in ("gn_moments", "gn_groups", "gn_var", "gn_rstd", "xp_made"))
        product = signal("product3", len(RING), len(RING))
        emptied = signal("emptied3", len(SCALAR_READS))
        conv_read = signal("conv_read", len(VECTOR_READS))
        max_made = signal("max_made", ITEMS)
        fall = signal("fall", ITEMS)
        rise = signal("rise", ITEMS)
        jump = signal("jump", ITEMS)
        jump_capped = signal("jump_capped", ITEMS)
        a_exped = signal("a_exped", ITEMS)
        f_exped = signal("f_exped", ITEMS)
        e_exped = signal("e_exped", ITEMS)
        kv_made = signal("kv_made", ITEMS)
        ev_made = signal("ev_made", ITEMS)
        num_made = signal("num_made", ITEMS)
        den_made = signal("den_made", ITEMS)
        num_out = signal("num_out", ITEMS)
        den_out = signal("den_out", ITEMS)
        den_inv = signal("den_inv", ITEMS)
        h_made = signal("h_made", ITEMS + 2 * CT)
        side_used = signal("side_used", CT)
        side_summed = signal("side_summed", 4 * CT)
        averaged, centred, squared, varied, inv_made = (signal(n + "3", 2) for n in ("averaged", "centred", "squared", "varied", "inv_made"))
        hn_made = signal("hn_made", 2 * CT)
        mixed = signal("mixed", 2 * CT)
        out_made = signal("out_made3", 2 * CT, 2 * CT)

        def half_of(ap, half):
            return ap[:, :, half * HALF:(half + 1) * HALF] if len(ap.shape) == 3 else ap[:, half * HALF:(half + 1) * HALF]

        def way(ap, backwards):
            return ap[:, ::-1] if backwards else ap

        def now(ap):
            return ap[:, 1:T + 1]

        def before(ap, backwards):
            return ap[:, 2:T + 2] if backwards else ap[:, 0:T]

        def rows_of(t, half):
            top = 1 + half * S // 2
            return xp[:, t, top:top + S // 2, 1:1 + S]

        def columns(n):
            return xp[:, :, :, n:n + S - 1:2]

        def filled_at(kind, n):
            return RING.index((kind, n)) + 1

        def scalar_read_at(kind, n):
            return SCALAR_READS.index((kind, n)) + 1

        def side_columns(m, odd):
            return sides[m].rearrange("p (a b) -> p a b", a=2)[:, :, odd::2]

        block = ctx.enter_context(nc.Block())

        @block.sync
        def _(sp):
            sp.sem_inc(stored, 16)
            sp.dma_start(xin[:, :], x_in[0:1].rearrange("a (p t) n -> p (a t n)", t=CT)).then_inc(x_loaded, 16)
            with sp.Fori(0, B) as i:
                sp.wait_ge(stored, i * 16 + 16)
                sp.dma_start(xres[:, :, :].rearrange("p t n -> p (t n)"), x_in[bass.ds(i, 1)].rearrange("a (p t) n -> p (a t n)", t=CT)).then_inc(res_loaded, 16)
                sp.wait_ge(xin_free.sem, i + 1)
                sp.wait_ge(side_used.sem, side_used.at(1, i))
                sp.dma_start(xin[:, :], x_in[bass.ds((i + 1) % B, 1)].rearrange("a (p t) n -> p (a t n)", t=CT)).then_inc(x_loaded, 16)
                sp.wait_ge(out_made.sem, out_made.at(2 * CT, i))
                sp.dma_start(x_out[bass.ds(i, 1)].rearrange("a (p t) n -> p (a t n)", t=CT), xres[:, :, :].rearrange("p t n -> p (t n)")).then_inc(stored, 16)
            sp.wait_ge(stored, 16 * B + 16)
            sp.wait_ge(x_loaded, 16 * B + 16)

        @block.gpsimd
        def _(pool):
            pool.memset(xp[:, :, :, :], 0.0).then_inc(framed.next(), 1)
            for tile, value in ((p, NEG), (num, 0.0), (den, 0.0)):
                pool.memset(tile[:, 0:1], value).then_inc(framed.next(), 1)
                pool.memset(tile[:, T + 1:T + 2], value).then_inc(framed.next(), 1)
            with pool.Fori(0, B) as i:
                for n in range(ITEMS + 1):
                    if n < ITEMS:
                        t, backwards = n // 2, n % 2
                        pool.wait_ge(max_made.sem, max_made.at(n + 1, i))
                        pool.tensor_tensor(to_a[:, n % 2, :], k[:, t, :], now(p), ALU.subtract).then_inc(rise.next(), 1)
                        pool.tensor_tensor(to_e[:, n % SLOTS, :], k[:, t, :], before(p, backwards), ALU.subtract).then_inc(jump.next(), 1)
                        pool.wait_ge(jump.sem, jump.now(i))
                        pool.sem_inc(gn.turn, 1)
                        pool.tensor_scalar(to_e[:, n % SLOTS, :], to_e[:, n % SLOTS, :], cap[:, t:t + 1], None, ALU.min).then_inc(jump_capped.next(), 1)
                    if n > 0:
                        last, backwards = n - 1, (n - 1) % 2
                        pool.wait_ge(ev_made.sem, ev_made.at(last + 1, i))
                        pool.wait_ge(den_made.sem, den_made.at(last + 1, i))
                        pool.tensor_tensor(to_e[:, last % SLOTS, :], to_e[:, last % SLOTS, :], before(den, backwards), ALU.add).then_inc(den_out.next(), 1)
            for s in (rise, jump, jump_capped, den_out):
                s.end_of_pass()

        @block.scalar
        def _(act):
            def group_rstd(i):
                act.wait_ge(gn_var.sem, gn_var.at(1, i))
                gn.scalar_rstd(act, act_step, i, gn_rstd)

            group_rstd(None)
            with act.Fori(0, B) as i:
                def keep_kv(first, count):
                    for n in range(first, first + count):
                        t = n // 4
                        act.wait_ge(product.sem, product.at(filled_at("kv", n), i))
                        target = half_of((k if n % 4 < 2 else v)[:, t, :], n % 2)
                        nc.scalar.copy(target, psum[:, n % 4, :]).then_inc(emptied.next(), 1)

                def keep_conv(m):
                    at = filled_at("conv", 4 * m)
                    if m == 0:
                        act.wait_ge(xp_made.sem, xp_made.at(0, i))
                    else:
                        act.wait_ge(h_made.sem, h_made.at(ITEMS, i))
                    act.wait_ge(product.sem, product.at(at, i))
                    nc.scalar.activation(side_columns(m, 0), psum[:, (at - 1) % 4, :].rearrange("p (a b) -> p a b", a=2), ACT.Identity,
                                         scale=bn_scale[:, m:m + 1], bias=cols["bn_b"][:, m:m + 1])
                    nc.scalar.activation(side_columns(m, 1), psum[:, (at - 1) % 4, :].rearrange("p (a b) -> p a b", a=2), ACT.Identity,
                                         scale=bn_scale[:, m:m + 1], bias=cols["bn_b"][:, m:m + 1]).then_inc(emptied.next(), 1)

                def exps(n):
                    t = n // 2
                    act.wait_ge(rise.sem, rise.at(n + 1, i))
                    nc.scalar.activation(to_a[:, n % 2, :], to_a[:, n % 2, :], ACT.Exp).then_inc(a_exped.next(), 1)
                    act.wait_ge(fall.sem, fall.at(n + 1, i))
                    nc.scalar.activation(to_f[:, n % SLOTS, :], to_f[:, n % SLOTS, :], ACT.Exp, bias=decay[:, t:t + 1]).then_inc(f_exped.next(), 1)
                    act.wait_ge(jump_capped.sem, jump_capped.at(n + 1, i))
                    nc.scalar.activation(to_e[:, n % SLOTS, :], to_e[:, n % SLOTS, :], ACT.Exp, bias=cols["u"][:, t:t + 1]).then_inc(e_exped.next(), 1)

                def sigmoid(n):
                    if n < 2:
                        act.wait_ge(num_made.sem, num_made.at(ITEMS - 1, i))
                    else:
                        act.wait_ge(h_made.sem, h_made.at(ITEMS + n - 1, i))
                    at = filled_at("gate", n)
                    act.wait_ge(product.sem, product.at(at, i))
                    nc.scalar.activation(sigmoids[:, n % 2, :], psum[:, (at - 1) % 4, :], ACT.Sigmoid).then_inc(emptied.next(), 1)

                def inverse(n):
                    at = to_e[:, n % SLOTS, :]
                    act.wait_ge(den_out.sem, den_out.at(n + 1, i))
                    nc.scalar.activation(at, at, ACT.Ln).then_inc(act_step.next(), 1)
                    act.wait_ge(act_step.sem, act_step.now(i))
                    nc.scalar.activation(at, at, ACT.Exp, scale=-1.0).then_inc(den_inv.next(), 1)

                keep_kv(0, 4)
                for n in range(ITEMS + 1):
                    if n < ITEMS:
                        exps(n)
                    if n < 2:
                        keep_kv(4 + 2 * n, 2)
                    if n == 2:
                        keep_kv(8, 4)
                    if n == ITEMS:
                        sigmoid(0)
                        sigmoid(1)
                    if n > 0:
                        inverse(n - 1)
                    if n == 3:
                        keep_conv(0)
                for n in range(2, 2 * CT):
                    sigmoid(n)
                keep_conv(1)
                for half in range(2):
                    act.wait_ge(centred.sem, centred.at(half + 1, i))
                    norm.scalar_square(v, h, half).then_inc(squared.next(), 1)
                group_rstd(i)
                for half in range(2):
                    act.wait_ge(varied.sem, varied.at(half + 1, i))
                    norm.scalar_log(half).then_inc(act_step.next(), 1)
                act.wait_ge(act_step.sem, act_step.now(i))
                for half in range(2):
                    norm.scalar_exp(half).then_inc(inv_made.next(), 1)
                keep_conv(2)
            for s in (act_step, gn_rstd, emptied, a_exped, f_exped, e_exped, den_inv, squared, inv_made):
                s.end_of_pass()

        @block.vector
        def _(dve):
            dve.wait_ge(framed.sem, framed.at(7))
            dve.sem_inc(*out_made.lead())

            def moments(i):
                dve.wait_ge(x_loaded, 16 if i is None else i * 16 + 32)
                gn.vector_moments(dve, xin[:, :], step, i, gn_moments)

            def variance(i):
                dve.wait_ge(gn_groups.sem, gn_groups.at(1, i))
                gn.vector_variance(dve, var_psum[:, 0, 0:2], step, i, gn_var)

            def normalise(i):
                dve.wait_ge(gn_rstd.sem, gn_rstd.at(1, i))
                gn.vector_shift(dve, step, i)
                if i is not None:
                    dve.wait_ge(product.sem, product.at(filled_at("gate", 2 * CT - 1), i))
                for t in range(CT):
                    ins = nc.vector.tensor_scalar(xp[:, t, 1:S + 1, 1:S + 1], xin[:, t * T:(t + 1) * T].rearrange("p (a b) -> p a b", b=S),
                                                  gn.rstd[:, :], gn.shift[:, :], ALU.mult, ALU.add)
                ins.then_inc(xp_made.next(), 1)
                dve.wait_ge(xp_made.sem, xp_made.at(1, i))
                dve.sem_inc(xin_free.sem, 1)

            moments(None)
            variance(None)
            normalise(None)
            with dve.Fori(0, B) as i:
                dve.wait_ge(xp_made.sem, xp_made.at(0, i))
                dve.wait_ge(product.sem, product.at(0, i))
                nc.vector.tensor_tensor(mixes[:, 1], columns(1), columns(2), ALU.add).then_inc(mixes_made.next(), 1)
                nc.vector.tensor_tensor(mixes[:, 2], columns(2), columns(1), ALU.subtract).then_inc(mixes_made.next(), 1)

                def maxima(n):
                    t, backwards = n // 2, n % 2
                    if backwards == 0:
                        dve.wait_ge(emptied.sem, emptied.at(scalar_read_at("kv", 4 * t + 1), i))
                    if n > 0:
                        dve.wait_ge(jump.sem, jump.at(n, i))
                        dve.wait_ge(fall.sem, fall.at(n, i))
                    if n > 1:
                        dve.wait_ge(kv_made.sem, kv_made.at(n - 1, i))
                    nc.vector.tensor_tensor_scan(
                        way(now(p), backwards), decay[:, t:t + 1].broadcast_to([P, T]), way(k[:, t, :], backwards),
                        NEG, ALU.add, ALU.max).then_inc(max_made.next(), 1)
                    dve.wait_ge(max_made.sem, max_made.now(i))
                    nc.vector.tensor_tensor(to_f[:, n % SLOTS, :], before(p, backwards), now(p), ALU.subtract).then_inc(fall.next(), 1)

                def scans(n):
                    t, backwards = n // 2, n % 2
                    a, f = to_a[:, n % 2, :], to_f[:, n % SLOTS, :]
                    dve.wait_ge(a_exped.sem, a_exped.at(n + 1, i))
                    dve.wait_ge(f_exped.sem, f_exped.at(n + 1, i))
                    if n > 0:
                        dve.wait_ge(num_out.sem, num_out.at(n, i))
                        dve.wait_ge(den_out.sem, den_out.at(n, i))
                    nc.vector.tensor_tensor_scan(
                        way(now(den), backwards), way(f, backwards), way(a, backwards), 0.0, ALU.mult, ALU.add).then_inc(den_made.next(), 1)
                    if backwards == 0:
                        dve.wait_ge(emptied.sem, emptied.at(scalar_read_at("kv", 4 * t + 3), i))
                    dve.wait_ge(den_made.sem, den_made.now(i))
                    nc.vector.tensor_tensor(a, a, v[:, t, :], ALU.mult).then_inc(kv_made.next(), 1)
                    dve.wait_ge(kv_made.sem, kv_made.now(i))
                    nc.vector.tensor_tensor_scan(
                        way(now(num), backwards), way(f, backwards), way(a, backwards), 0.0, ALU.mult, ALU.add).then_inc(num_made.next(), 1)
                    dve.wait_ge(e_exped.sem, e_exped.at(n + 1, i))
                    dve.wait_ge(num_made.sem, num_made.now(i))
                    nc.vector.tensor_tensor(f, to_e[:, n % SLOTS, :], v[:, t, :], ALU.mult).then_inc(ev_made.next(), 1)
                    dve.wait_ge(ev_made.sem, ev_made.now(i))
                    nc.vector.tensor_tensor(f, f, before(num, backwards), ALU.add).then_inc(num_out.next(), 1)

                def quotient(n):
                    t, backwards = n // 2, n % 2
                    ev = to_f[:, n % SLOTS, :]
                    dve.wait_ge(den_inv.sem, den_inv.at(n + 1, i))
                    dve.wait_ge(num_out.sem, num_out.at(n + 1, i))
                    at = h[:, t, :]
                    if backwards == 0:
                        dve.wait_ge(jump.sem, jump.at(n + 2, i))
                        nc.vector.tensor_tensor(at, ev, to_e[:, n % SLOTS, :], ALU.mult).then_inc(h_made.next(), 1)
                    else:
                        nc.vector.tensor_tensor(ev, ev, to_e[:, n % SLOTS, :], ALU.mult).then_inc(step.next(), 1)
                        dve.wait_ge(step.sem, step.now(i))
                        dve.wait_ge(h_made.sem, h_made.at(n, i))
                        nc.vector.tensor_tensor(at, at, ev, ALU.add).then_inc(h_made.next(), 1)

                def sum_side(m, n):
                    at = filled_at("conv", 4 * m + n)
                    source = psum[:, (at - 1) % 4, :].rearrange("p (a b) -> p a b", a=2)
                    if n == 1:
                        dve.wait_ge(emptied.sem, emptied.at(scalar_read_at("conv", 4 * m), i))
                    dve.wait_ge(product.sem, product.at(at, i))
                    if n != 3:
                        if n == 2:
                            dve.wait_ge(side_summed.sem, side_summed.at(4 * m + 2, i))
                        ins = nc.vector.scalar_tensor_tensor(side_columns(m, 0), source, bn_scale[:, m:m + 1], side_columns(m, 0), ALU.mult, ALU.add)
                        ins.then_inc(side_summed.next(), 1)
                    if n != 2:
                        if n == 3:
                            dve.wait_ge(side_summed.sem, side_summed.at(4 * m + 3, i))
                        scale = bn_minus if n == 1 else bn_scale
                        ins = nc.vector.scalar_tensor_tensor(side_columns(m, 1), source, scale[:, m:m + 1], side_columns(m, 1), ALU.mult, ALU.add)
                        ins.then_inc(side_summed.next(), 1)
                    dve.wait_ge(side_summed.sem, side_summed.now(i))
                    dve.sem_inc(conv_read.next(), 1)

                def add_side(m):
                    if m == 0:
                        dve.wait_ge(res_loaded, i * 16 + 16)
                    dve.wait_ge(side_summed.sem, side_summed.at(4 * m + 4, i))
                    at, y = xres[:, m, :], sides[m]
                    nc.vector.scalar_tensor_tensor(y, y, 0.01, y, ALU.mult, ALU.max).then_inc(step.next(), 1)
                    dve.wait_ge(step.sem, step.now(i))
                    nc.vector.scalar_tensor_tensor(at, y, cols["gamma_s"][:, m:m + 1], at, ALU.mult, ALU.add).then_inc(side_used.next(), 1)

                maxima(0)
                nc.vector.tensor_tensor(mixes[:, 0], columns(0), columns(2), ALU.subtract).then_inc(mixes_made.next(), 1)
                nc.vector.tensor_tensor(mixes[:, 3], columns(3), columns(1), ALU.subtract).then_inc(mixes_made.next(), 1)
                for n in range(ITEMS):
                    if n + 1 < ITEMS:
                        maxima(n + 1)
                    if n == ITEMS - 2:
                        sum_side(0, 1)
                    if n == ITEMS - 1:
                        sum_side(0, 2)
                        sum_side(0, 3)
                    scans(n)
                    if n > 0:
                        quotient(n - 1)
                quotient(ITEMS - 1)
                dve.wait_ge(h_made.sem, h_made.at(ITEMS, i))
                for n in range(2 * CT):
                    at = half_of(h[:, n // 2, :], n % 2)
                    dve.wait_ge(emptied.sem, emptied.at(scalar_read_at("gate", n), i))
                    nc.vector.scalar_tensor_tensor(at, sigmoids[:, n % 2, :], 0.5, at, ALU.mult, ALU.mult).then_inc(h_made.next(), 1)
                add_side(0)
                for half in range(2):
                    dve.wait_ge(averaged.sem, averaged.at(half + 1, i))
                    norm.vector_centre(h, half).then_inc(centred.next(), 1)
                moments(i)
                variance(i)
                sum_side(1, 1)
                normalise(i)
                for n in range(2, 4):
                    sum_side(1, n)
                add_side(1)
                for half in range(2):
                    dve.wait_ge(inv_made.sem, inv_made.at(half + 1, i))
                    norm.vector_scale(h, half).then_inc(step.next(), 1)
                    dve.wait_ge(step.sem, step.now(i))
                    for t in range(CT):
                        at = half_of(h[:, t, :], half)
                        nc.vector.tensor_scalar(at, at, cols["ln_g"][:, t:t + 1], cols["ln_b"][:, t:t + 1],
                                                                  ALU.mult, ALU.add).then_inc(hn_made.next(), 1)
                for n in range(1, 4):
                    sum_side(2, n)
                add_side(2)
                for n in range(2 * CT):
                    m, half = n // 2, n % 2
                    dve.wait_ge(mixed.sem, mixed.at(n + 1, i))
                    at = half_of(xres[:, m, :], half)
                    if half == 0:
                        dve.wait_ge(side_used.sem, side_used.at(m + 1, i))
                    nc.vector.scalar_tensor_tensor(at, psum[:, (MIX + n) % 4, :], cols["gamma_g"][:, m:m + 1],
                                                                      at, ALU.mult, ALU.add).then_inc(out_made.next(), 1)
            for s in (step, gn_moments, gn_var, xp_made, max_made, fall, kv_made, num_made, den_made, ev_made, num_out,
                      h_made, side_used, side_summed, conv_read, mixes_made, centred, hn_made, out_made):
                s.end_of_pass()

        @block.tensor
        def _(pe):
            pe.sem_inc(*product.lead())

            def groups(i):
                pe.wait_ge(gn_moments.sem, gn_moments.at(1, i))
                gn.tensor_groups(pe, var_psum[:, 0, 0:2], const["group_mean"]).then_inc(gn_groups.next(), 1)

            groups(None)
            with pe.Fori(0, B) as i:
                def fill(at):
                    kind, n = RING[at]
                    if at < 4:
                        pe.wait_ge(out_made.sem, out_made.at(at - 3, i))
                    elif RING[at - 4] in SCALAR_READS:
                        pe.wait_ge(emptied.sem, emptied.at(SCALAR_READS.index(RING[at - 4]) + 1, i))
                    else:
                        pe.wait_ge(conv_read.sem, conv_read.at(VECTOR_READS.index(RING[at - 4]) + 1, i))
                    bank = psum[:, at % 4, :]
                    if kind == "conv":
                        m, factor = n // 4, FACTOR[n % 4]
                        if m == 0:
                            pe.wait_ge(mixes_made.sem, mixes_made.at(n + 1, i))
                        for down in range(3):
                            for t in range(CT):
                                ins = nc.tensor.matmul(bank, conv_w[:, t, down, factor, m * P:(m + 1) * P],
                                                       mixes[:, factor, t, down:down + S, :].rearrange("p a b -> p (a b)"),
                                                       start=(down == 0 and t == 0), stop=(down == 2 and t == CT - 1))
                    else:
                        m, half = (n // 4 if kind == "kv" else n // 2), n % 2
                        weights = lin_w["Wr" if kind == "gate" else "Wk" if n % 4 < 2 else "Wv"]
                        for t in range(CT):
                            ins = nc.tensor.matmul(bank.rearrange("p (a b) -> p a b", b=S), weights[:, t, m * P:(m + 1) * P],
                                                   rows_of(t, half), start=(t == 0), stop=(t == CT - 1))
                    ins.then_inc(product.next(), 1)

                pe.wait_ge(xp_made.sem, xp_made.at(0, i))
                first_of_tile = [filled_at("conv", 4 * m) - 1 for m in range(CT)]
                for at in range(len(RING)):
                    if at == first_of_tile[1] + 2:
                        groups(i)
                    if at == first_of_tile[1] + 1:
                        for half in range(2):
                            pe.wait_ge(h_made.sem, h_made.at(ITEMS + 2 * CT - 1 + half, i))
                            norm.tensor_sum(mean_psum, h, half).then_inc(averaged.next(), 1)
                    if at == first_of_tile[2]:
                        pe.wait_ge(gn_var.sem, gn_var.at(1, i))
                        for half in range(2):
                            pe.wait_ge(squared.sem, squared.at(half + 1, i))
                            norm.tensor_sum(var_psum, v, half).then_inc(varied.next(), 1)
                    fill(at)
                for n in range(2 * CT):
                    m, half = n // 2, n % 2
                    if n == 0:
                        pe.wait_ge(hn_made.sem, hn_made.at(CT, i))
                    if n == 1:
                        pe.wait_ge(hn_made.sem, hn_made.at(2 * CT, i))
                    if n == 0:
                        pe.wait_ge(emptied.sem, emptied.at(scalar_read_at("conv", 4 * CT - 4), i))
                    elif n < 4:
                        pe.wait_ge(conv_read.sem, conv_read.at(len(VECTOR_READS) - 3 + n, i))
                    else:
                        pe.wait_ge(out_made.sem, out_made.at(n - 3, i))
                    for t in range(CT):
                        ins = nc.tensor.matmul(psum[:, (MIX + n) % 4, :], lin_w["Wo"][:, t, m * P:(m + 1) * P],
                                               half_of(h[:, t, :], half), start=(t == 0), stop=(t == CT - 1))
                    ins.then_inc(mixed.next(), 1)
            for s in (gn_groups, product, averaged, varied, mixed):
                s.end_of_pass()


def build(nc, args, x_out):
    with ExitStack() as ctx:
        tiles = {name: ctx.enter_context(nc.sbuf_tensor(name, shape, F32)) for name, shape in
                 (("ident", [P, P]), ("group_mean", [P, P]), ("col_mean", [P, P]))}
        const = {name: tile[:, :] for name, tile in tiles.items()}
        const["turn"] = ctx.enter_context(nc.semaphore("turn"))
        make_constants(nc, const["ident"], const["group_mean"], const["col_mean"])
        x = args["x"].rearrange("b c h w -> b c (h w)")
        y = x_out.rearrange("b c h w -> b c (h w)")
        x1 = nc.dram_tensor("x1", [B, C, T], F32).ap()
        x2 = nc.dram_tensor("x2", [B, C, T], F32).ap()
        x3 = nc.dram_tensor("x3", [B, C, T], F32).ap()
        attention_layer(nc, const, x, x1, args["L0_conv_w_qkv"], args["L0_conv_w_proj"], args["L0_conv_b_proj"])
        moments = ctx.enter_context(nc.sbuf_tensor("x2_moments", [P, B, 2], F32))
        s5_layer(nc, const, x1, x2, moments, {k[8:]: v for k, v in args.items() if k.startswith("L1_conv_")})
        depthwise_layer(nc, const, x2, x3, moments, {k[8:]: v for k, v in args.items() if k.startswith("L2_conv_")})
        rwkv_layer(nc, const, x3, y, {k[8:]: v for k, v in args.items() if k.startswith("L3_conv_")})


def kernel(**inputs):
    import numpy as _np
    import concourse.bacc as _bacc
    from concourse.bass_utils import run_bass_kernel_spmd as _run

    nc = _bacc.Bacc("TRN2", target_bir_lowering=False, num_devices=1)
    arrays, args = {}, {}
    for name, value in inputs.items():
        a = _np.ascontiguousarray(value)
        arrays[f"in_{name}"] = a
        args[name] = nc.dram_tensor(f"in_{name}", a.shape, mybir.dt.from_np(a.dtype), kind="ExternalInput").ap()
    out = nc.dram_tensor("out", inputs["x"].shape, F32, kind="ExternalOutput").ap()
    build(nc, args, out)
    r = _run(nc, [arrays], core_ids=[0])
    return r.results[0]["out"]
```
